# Optimizing a Trainium2 kernel written in Bass

```python
import numpy as np
import jax
import jax.numpy as jnp

def _softmax(x, axis=-1):
    return jax.nn.softmax(x, axis=axis)

def _gelu(x):
    return jax.nn.gelu(x, approximate=True)

def _silu(x):
    return jax.nn.silu(x)

def _sigmoid(x):
    return jax.nn.sigmoid(x)

def _layernorm(x, axis=-1, eps=1e-05):
    m = jnp.mean(x, axis=axis, keepdims=True)
    v = jnp.var(x, axis=axis, keepdims=True)
    return (x - m) / jnp.sqrt(v + eps)

def _scatter_add(tgt, idx, src, axis=0):
    return tgt.at[idx].add(src)

def _segment_sum(src, seg, n):
    return jax.ops.segment_sum(src, seg, n)
kernel_name = 'mk_decoder_postln_d1_seqx_r2_25f5ed'

def setup_inputs(seed: int=0):
    np.random.seed(seed)
    _w = jnp.asarray

    def _rec_inputs():
        import jax
        import jax.numpy as jnp
        _rk = jax.random.key(seed)
        x = -0.000125 + 0.9999 * jax.random.normal(jax.random.fold_in(_rk, 1), (8, 224, 512), jnp.float32)
        _lenS = 224 - jax.random.randint(jax.random.fold_in(_rk, 7), (8,), 0, max(1, 224 // 4) + 1, jnp.int32)
        _lenS2 = 750 - jax.random.randint(jax.random.fold_in(_rk, 8), (8,), 0, max(1, 750 // 4) + 1, jnp.int32)
        _ctx_2048P = jax.random.normal(jax.random.fold_in(_rk, 11), (8, 16, 1024), jnp.float32)
        _ctx_2048c = jax.random.dirichlet(jax.random.fold_in(_rk, 511), 0.3 * jnp.ones((16,), jnp.float32), (8, 750))
        _ctx_2048t = jnp.einsum('bsk,bkd->bsd', _ctx_2048c, _ctx_2048P)
        _ctx_2048t = _ctx_2048t * jax.lax.rsqrt(jnp.mean(jnp.square(_ctx_2048t)) + 1e-12) * 0.953939
        ctx_2048 = -1.39393e-06 + 0.999914 * (_ctx_2048t + 0.3 * jax.random.normal(jax.random.fold_in(_rk, 611), (8, 750, 1024), jnp.float32))
        return (x, ctx_2048)
    x, ctx_2048 = _rec_inputs()

    def _L0_attn_setup():
        import jax, jax.numpy as jnp
        import numpy as np
        key = jax.random.key(seed)
        k1, k2, k3, k4 = jax.random.split(key, 4)
        B, N, D = (4, 1024, 512)
        D1, D2 = (512, 512)
        X = jax.random.normal(k1, (B, N, D), dtype=jnp.float32)
        s_q = (2.0 / (D + D1)) ** 0.5
        s_v = (2.0 / (D + D2)) ** 0.5
        W_Q = jax.random.normal(k2, (D, D1), dtype=jnp.float32) * s_q
        W_K = jax.random.normal(k3, (D, D1), dtype=jnp.float32) * s_q
        W_V = jax.random.normal(k4, (D, D2), dtype=jnp.float32) * s_v
        return {'X': X, 'W_Q': W_Q, 'W_K': W_K, 'W_V': W_V}
    _L0_attn_all = _L0_attn_setup()
    _L0_attn_in = {k: v for k, v in _L0_attn_all.items() if k in ('W_Q', 'W_K', 'W_V')}
    del _L0_attn_all

    def _L0_xattn_setup():
        import jax, jax.numpy as jnp
        import numpy as np
        B, N, DIM = (8, 2048, 512)
        M, CTX = (128, 1024)
        HEADS, DH = (16, 64)
        INNER = HEADS * DH
        EPS = 1e-06

        def _split_heads(t):
            b, n, _ = t.shape
            return t.reshape(b, n, HEADS, DH).transpose(0, 2, 1, 3)
        key = jax.random.key(seed)
        ks = jax.random.split(key, 6)
        x = jax.random.normal(ks[0], (B, N, DIM), dtype=jnp.float32)
        context = jax.random.normal(ks[1], (B, M, CTX), dtype=jnp.float32)
        Wq = jax.random.normal(ks[2], (DIM, INNER), dtype=jnp.float32) / np.sqrt(DIM)
        Wkv = jax.random.normal(ks[3], (CTX, 2 * INNER), dtype=jnp.float32) / np.sqrt(CTX)
        null_kv = jax.random.normal(ks[4], (2, DH), dtype=jnp.float32) / np.sqrt(2.0)
        Wout = jax.random.normal(ks[5], (INNER, DIM), dtype=jnp.float32) / np.sqrt(INNER)
        ln_scale = jnp.ones((DIM,), dtype=jnp.float32)
        ln_bias = jnp.zeros((DIM,), dtype=jnp.float32)
        return {'x': x, 'context': context, 'Wq': Wq, 'Wkv': Wkv, 'null_kv': null_kv, 'Wout': Wout, 'ln_scale': ln_scale, 'ln_bias': ln_bias}
    _L0_xattn_all = _L0_xattn_setup()
    _L0_xattn_in = {k: v for k, v in _L0_xattn_all.items() if k in ('Wq', 'Wkv', 'null_kv', 'Wout', 'ln_scale', 'ln_bias')}
    del _L0_xattn_all

    def _L0_ffn_setup():
        import jax, jax.numpy as jnp
        import numpy as np
        IN_DIM = 512
        HIDDEN = 512
        OUT_DIM = 512
        NUM_EXPERTS = 16
        TOP_K = 2
        ROUTER_TEMP = 1.0
        LN_EPS = 1e-05

        def _layernorm(h, g, b):
            mu = jnp.mean(h, axis=-1, keepdims=True)
            var = jnp.mean(jnp.square(h - mu), axis=-1, keepdims=True)
            return (h - mu) * jax.lax.rsqrt(var + LN_EPS) * g + b
        key = jax.random.key(seed)
        ks = jax.random.split(key, 8)
        s_in = 1.0 / np.sqrt(IN_DIM)
        s_h = 1.0 / np.sqrt(HIDDEN)
        x = jax.random.normal(ks[0], (4, 1024, IN_DIM), dtype=jnp.float32)
        Wr = jax.random.uniform(ks[1], (IN_DIM, NUM_EXPERTS), jnp.float32, -s_in, s_in)
        br = jax.random.uniform(ks[2], (NUM_EXPERTS,), jnp.float32, -s_in, s_in)
        W1 = jax.random.uniform(ks[3], (NUM_EXPERTS, IN_DIM, HIDDEN), jnp.float32, -s_in, s_in)
        b1 = jax.random.uniform(ks[4], (NUM_EXPERTS, HIDDEN), jnp.float32, -s_in, s_in)
        g1 = jnp.ones((NUM_EXPERTS, HIDDEN), jnp.float32)
        be1 = jnp.zeros((NUM_EXPERTS, HIDDEN), jnp.float32)
        W2 = jax.random.uniform(ks[5], (NUM_EXPERTS, HIDDEN, OUT_DIM), jnp.float32, -s_h, s_h)
        b2 = jax.random.uniform(ks[6], (NUM_EXPERTS, OUT_DIM), jnp.float32, -s_h, s_h)
        return {'x': x, 'Wr': Wr, 'br': br, 'W1': W1, 'b1': b1, 'g1': g1, 'be1': be1, 'W2': W2, 'b2': b2}
    _L0_ffn_all = _L0_ffn_setup()
    _L0_ffn_in = {k: v for k, v in _L0_ffn_all.items() if k in ('Wr', 'br', 'W1', 'b1', 'g1', 'be1', 'W2', 'b2')}
    del _L0_ffn_all
    return {'x': x, 'ctx_2048': ctx_2048, 'L0_attn_W_Q': _L0_attn_in['W_Q'], 'L0_attn_W_K': _L0_attn_in['W_K'], 'L0_attn_W_V': _L0_attn_in['W_V'], 'L0_xattn_Wq': _L0_xattn_in['Wq'], 'L0_xattn_Wkv': _L0_xattn_in['Wkv'], 'L0_xattn_null_kv': _L0_xattn_in['null_kv'], 'L0_xattn_Wout': _L0_xattn_in['Wout'], 'L0_xattn_ln_scale': _L0_xattn_in['ln_scale'], 'L0_xattn_ln_bias': _L0_xattn_in['ln_bias'], 'L0_ffn_Wr': _L0_ffn_in['Wr'], 'L0_ffn_br': _L0_ffn_in['br'], 'L0_ffn_W1': _L0_ffn_in['W1'], 'L0_ffn_b1': _L0_ffn_in['b1'], 'L0_ffn_g1': _L0_ffn_in['g1'], 'L0_ffn_be1': _L0_ffn_in['be1'], 'L0_ffn_W2': _L0_ffn_in['W2'], 'L0_ffn_b2': _L0_ffn_in['b2']}

def reference(x, ctx_2048, L0_attn_W_Q, L0_attn_W_K, L0_attn_W_V, L0_xattn_Wq, L0_xattn_Wkv, L0_xattn_null_kv, L0_xattn_Wout, L0_xattn_ln_scale, L0_xattn_ln_bias, L0_ffn_Wr, L0_ffn_br, L0_ffn_W1, L0_ffn_b1, L0_ffn_g1, L0_ffn_be1, L0_ffn_W2, L0_ffn_b2):
    import jax
    import jax.numpy as jnp

    def _L0_attn_ref(X, W_Q, W_K, W_V):
        import jax, jax.numpy as jnp
        import numpy as np
        D1 = W_Q.shape[1]
        Q = jnp.einsum('bnd,de->bne', X, W_Q)
        K = jnp.einsum('bnd,de->bne', X, W_K)
        V = jnp.einsum('bnd,de->bne', X, W_V)
        scale = 1.0 / jnp.sqrt(jnp.asarray(D1, dtype=X.dtype))
        A = jnp.einsum('bne,bme->bnm', Q, K) * scale
        A = jax.nn.softmax(A, axis=-1)
        return jnp.einsum('bnm,bme->bne', A, V)

    def _L0_xattn_ref(x, context, Wq, Wkv, null_kv, Wout, ln_scale, ln_bias):
        import jax, jax.numpy as jnp
        import numpy as np
        B, N, DIM = (8, 2048, 512)
        M, CTX = (128, 1024)
        HEADS, DH = (16, 64)
        INNER = HEADS * DH
        EPS = 1e-06

        def _split_heads(t):
            b, n, _ = t.shape
            return t.reshape(b, n, HEADS, DH).transpose(0, 2, 1, 3)
        scale = DH ** (-0.5)
        b = x.shape[0]
        q = _split_heads(jnp.einsum('bnd,df->bnf', x, Wq))
        kv = jnp.einsum('bmc,cf->bmf', context, Wkv)
        k, v = jnp.split(kv, 2, axis=-1)
        k, v = (_split_heads(k), _split_heads(v))
        nk = jnp.broadcast_to(null_kv[0], (b, HEADS, 1, DH))
        nv = jnp.broadcast_to(null_kv[1], (b, HEADS, 1, DH))
        k = jnp.concatenate((nk, k), axis=-2)
        v = jnp.concatenate((nv, v), axis=-2)
        q = q * scale
        sim = jnp.einsum('bhid,bhjd->bhij', q, k)
        attn = jax.nn.softmax(sim, axis=-1)
        out = jnp.einsum('bhij,bhjd->bhid', attn, v)
        out = out.transpose(0, 2, 1, 3).reshape(b, -1, INNER)
        out = jnp.einsum('bnf,fd->bnd', out, Wout)
        mu = jnp.mean(out, axis=-1, keepdims=True)
        var = jnp.var(out, axis=-1, keepdims=True)
        out = (out - mu) * jax.lax.rsqrt(var + EPS) * ln_scale + ln_bias
        return out

    def _L0_ffn_ref(x, Wr, br, W1, b1, g1, be1, W2, b2):
        import jax, jax.numpy as jnp
        import numpy as np
        IN_DIM = 512
        HIDDEN = 512
        OUT_DIM = 512
        NUM_EXPERTS = 16
        TOP_K = 2
        ROUTER_TEMP = 1.0
        LN_EPS = 1e-05

        def _layernorm(h, g, b):
            mu = jnp.mean(h, axis=-1, keepdims=True)
            var = jnp.mean(jnp.square(h - mu), axis=-1, keepdims=True)
            return (h - mu) * jax.lax.rsqrt(var + LN_EPS) * g + b
        orig_shape = x.shape[:-1]
        x_flat = x.reshape(-1, x.shape[-1])
        logits = (x_flat @ Wr + br) / max(ROUTER_TEMP, 1e-06)
        probs = jax.nn.softmax(logits, axis=-1)
        topk_w, topk_idx = jax.lax.top_k(probs, TOP_K)
        topk_w = topk_w / jnp.clip(jnp.sum(topk_w, axis=-1, keepdims=True), 1e-09)
        h = jnp.einsum('nc,ech->neh', x_flat, W1) + b1
        h = _layernorm(h, g1, be1)
        h = jax.nn.gelu(h, approximate=False)
        expert_out = jnp.einsum('neh,eho->neo', h, W2) + b2
        sel = jnp.take_along_axis(expert_out, topk_idx[:, :, None], axis=1)
        y_flat = jnp.sum(sel * topk_w[:, :, None], axis=1)
        return y_flat.reshape(*orig_shape, y_flat.shape[-1])
    x = _layernorm(x + _L0_attn_ref(x, L0_attn_W_Q, L0_attn_W_K, L0_attn_W_V), axis=-1)
    x = _layernorm(x + _L0_xattn_ref(x, ctx_2048, L0_xattn_Wq, L0_xattn_Wkv, L0_xattn_null_kv, L0_xattn_Wout, L0_xattn_ln_scale, L0_xattn_ln_bias), axis=-1)
    x = _layernorm(x + _L0_ffn_ref(x, L0_ffn_Wr, L0_ffn_br, L0_ffn_W1, L0_ffn_b1, L0_ffn_g1, L0_ffn_be1, L0_ffn_W2, L0_ffn_b2), axis=-1)
    return x

_drawn_inputs = setup_inputs


def setup_inputs(seed=0):
    import zlib

    import numpy as np

    out = dict(_drawn_inputs(seed))
    spreads = {'L0_xattn_ln_scale': (1.0, 0.2),
     'L0_xattn_ln_bias': (0.0, 0.1),
     'L0_ffn_g1': (1.0, 0.2),
     'L0_ffn_be1': (0.0, 0.298)}
    factors = {'L0_xattn_null_kv': 4.14, 'L0_ffn_b1': 4.461, 'L0_ffn_b2': 3.222}
    for name, (base, spread) in spreads.items():
        noise = np.random.default_rng([zlib.crc32(name.encode()), seed]).standard_normal(out[name].shape)
        drawn = base * np.exp(spread * noise) if base else spread * noise
        out[name] = jnp.asarray(drawn.astype(out[name].dtype))
    for name, factor in factors.items():
        out[name] = (out[name] * factor).astype(out[name].dtype)
    return out
```

```python
from contextlib import ExitStack

import concourse.bass as bass
from concourse import mybir

F32 = mybir.dt.float32
F32R = mybir.dt.float32r
BF16 = mybir.dt.bfloat16
I32 = mybir.dt.int32
U32 = mybir.dt.uint32
ALU = mybir.AluOpType
ACT = mybir.ActivationFunctionType
AX = mybir.AxisListType.X

B, S, D = 8, 224, 512
CTX_LEN, CTX_D = 750, 1024
HEADS, DH = 16, 64
INNER = HEADS * DH
E, TOP_K, HID = 16, 2, 512
QT = S // 2
KD = D // 128
TOKENS = B * S
TILES = TOKENS // QT
SLOT = 128
SLOT_TILES = (TOKENS * TOP_K + E * (SLOT - 1)) // SLOT
SLOTS = SLOT_TILES * SLOT
LN_EPS, OUT_EPS = 1e-5, 1e-6
RSQRT_MAGIC = 1597463007.0
RING = 4


class Steps:

    def __init__(self, eng, sem, base=0):
        self.eng, self.sem, self.base, self.n = eng, sem, base, 0

    def step(self, instruction):
        self.n += 1
        instruction.then_inc(self.sem, 1)
        self.eng.wait_ge(self.sem, self.base + self.n)


def rsqrt_steps(st, y, v, t, eps):
    eng = st.eng
    st.step(eng.tensor_scalar(v, v, eps, None, ALU.add))
    st.step(eng.tensor_scalar(y.bitcast(I32), v.bitcast(I32), -0.5, RSQRT_MAGIC, ALU.mult, ALU.add))
    for _ in range(3):
        st.step(eng.tensor_tensor(t, y, y, ALU.mult))
        st.step(eng.tensor_tensor(t, t, v, ALU.mult))
        st.step(eng.tensor_scalar(t, t, -0.5, 1.5, ALU.mult, ALU.add))
        st.step(eng.tensor_tensor(y, y, t, ALU.mult))


RSQRT_STEPS = 14


def pool_round(pool, out, in_):
    return pool.tensor_scalar(out, in_, 1.0, 1.0, ALU.mult, ALU.mult)


def pool_inverse_root(pool, y, v, minus_half, eps, done, count, alone):
    own_instruction(pool, alone)
    pool.tensor_scalar(v, v, eps, 1.0, ALU.add, ALU.mult).then_inc(done, 1)
    pool.wait_ge(done, count + 1)
    pool.tensor_tensor(y, v, minus_half, ALU.pow).then_inc(done, 1)


def matmul3(pe, out, stat_hi, stat_lo, mov_hi, mov_lo, first, last):
    pe.matmul(out, stat_hi, mov_hi, start=first, stop=False)
    pe.matmul(out, stat_hi, mov_lo, start=False, stop=False)
    return pe.matmul(out, stat_lo, mov_hi, start=False, stop=last)


def own_instruction(eng, counter):
    eng.sem_inc(counter, 1)


def make_identity(pool, ident, done):
    pool.memset(ident, 0.0).then_inc(done, 1)
    pool.wait_ge(done, 1)
    pool.affine_select(out=ident, in_=ident, compare_op=ALU.not_equal, fill=1.0, base=0,
                       pattern=[[-1, ident.shape[1]]], channel_multiplier=1).then_inc(done, 1)


def as_f32(ap):
    return ap.bitcast(F32)


class Scope:

    kept = None
    made = {}

    def __init__(self, nc, stack, tag, phase=None):
        self.nc, self.stack, self.tag, self.phase = nc, stack, tag, phase or tag

    def sb(self, name, shape, dt=F32):
        return self.stack.enter_context(self.nc.sbuf_tensor(f"{self.tag}_{name}", shape, dt))

    def bank(self, name, shape=(128, 512), dt=F32):
        return self.stack.enter_context(self.nc.psum_tensor(f"{self.tag}_{name}", list(shape), dt))

    def sem(self, name):
        if Scope.kept is None:
            return self.stack.enter_context(self.nc.semaphore(f"{self.tag}_{name}"))
        if (self.phase, name) not in Scope.made:
            Scope.made[self.phase, name] = Scope.kept.enter_context(self.nc.semaphore(f"{self.phase}_{name}"))
        return Scope.made[self.phase, name]

    def clear(self):
        with self.nc.Block() as block:
            @block.sync
            def _(sp):
                for (phase, _), sem in Scope.made.items():
                    if phase == self.phase:
                        sp.sem_clear(sem)



def self_attention(nc, xT, x, wq, wk, wv, wxq, x1_dram, qT_dram, slot_x_dram):
    SCALE = float(D) ** -0.5
    NW = 5
    with ExitStack() as stack:
        m = Scope(nc, stack, "sa")
        ident = m.sb("ident", [128, 128])
        w_raw = m.sb("w_raw", [128, 2, KD, 512])
        w_hi = m.sb("w_hi", [128, NW, KD, 512], F32R)
        w_lo = m.sb("w_lo", [128, NW, KD, 512], F32R)
        xT_raw = m.sb("xT_raw", [128, KD, S])
        xT_hi = m.sb("xT_hi", [128, KD, S], F32R)
        xT_lo = m.sb("xT_lo", [128, KD, S], F32R)
        x_tok = m.sb("x_tok", [QT, 2, D])
        qk_hi = m.sb("qk_hi", [128, 2, KD, S], F32R)
        qk_lo = m.sb("qk_lo", [128, 2, KD, S], F32R)
        v_hi = m.sb("v_hi", [QT, 2, D], F32R)
        v_lo = m.sb("v_lo", [QT, 2, D], F32R)
        probs = m.sb("probs", [QT, 2, S])
        pT_hi = m.sb("pT_hi", [QT, 2, S], F32R)
        pT_lo = m.sb("pT_lo", [QT, 2, S], F32R)
        stat = m.sb("stat", [QT, 2, 4])
        mv = m.sb("mv", [QT, 2, 2])
        bn = m.sb("bn", [QT, 2, 6])
        rs = m.sb("rs", [QT, 2, 1])
        minus_half = m.sb("minus_half", [QT, 2, 1])
        res = m.sb("res", [QT, 2, D])
        x1 = m.sb("x1", [QT, 2, D])
        x1T_hi = m.sb("x1T_hi", [128, KD, S], F32R)
        x1T_lo = m.sb("x1T_lo", [128, KD, S], F32R)
        xq = m.sb("xq", [128, INNER // 128, S])
        zeros = m.sb("zeros", [128, SLOTS * D // (B * 128)])
        ring = [m.bank(f"ring{n}") for n in range(RING)]
        s_bank, pT_bank = m.bank("scores"), m.bank("pT")
        o_bank = [m.bank(f"o{n}") for n in range(2)]

        ident_done = m.sem("ident_done")
        w_loaded = [m.sem(f"w_loaded{n}") for n in range(2)]
        w_hi_done, w_lo_done = m.sem("w_hi_done"), m.sem("w_lo_done")
        xT_loaded, xT_hi_done, xT_lo_done = m.sem("xT_loaded"), m.sem("xT_hi_done"), m.sem("xT_lo_done")
        x_loaded = m.sem("x_loaded")
        ring_full, ring_hi, ring_out = m.sem("ring_full"), m.sem("ring_hi"), m.sem("ring_out")
        scores_ready, max_ready, exp_done = m.sem("scores_ready"), m.sem("max_ready"), m.sem("exp_done")
        pT_full, pT_hi_done, pT_done = m.sem("pT_full"), m.sem("pT_hi_done"), m.sem("pT_done")
        o_full, o_read = m.sem("o_full"), m.sem("o_read")
        zeros_ready, slots_zeroed = m.sem("zeros_ready"), m.sem("slots_zeroed")
        x1_ready, x1_stored, xq_stored = m.sem("x1_ready"), m.sem("x1_stored"), m.sem("xq_stored")
        mv_ready, root_done = m.sem("mv_ready"), m.sem("root_done")
        dve_steps = m.sem("dve_steps")
        waits_alone, dve_waits_alone = m.sem("waits_alone"), m.sem("dve_waits_alone")

        def qkv_job(b):
            return 0 if isinstance(b, int) and b == 0 else b * 12 - 6

        def next_job(b):
            return 12 * B - 6 if isinstance(b, int) and b == B - 1 else (b + 1) * 12

        QKV_BANK0, NEXT_BANK0 = 2, 0

        def bank_of(first, b, n):
            if first is qkv_job:
                return ring[((0 if isinstance(b, int) and b == 0 else QKV_BANK0) + n) % RING]
            return ring[((next_job(b) if isinstance(b, int) else NEXT_BANK0) + n) % RING]

        w_dram = [wq, wk, wv, wxq[:, 0:512], wxq[:, 512:1024]]
        STEPS = 1 + 1 + 3

        block = stack.enter_context(nc.Block())

        def batches(eng, body):
            body(0)
            with eng.Fori(1, B - 2) as b:
                body(b)
            body(B - 2)
            body(B - 1)

        def is_int(b, *values):
            return isinstance(b, int) and b in values

        @block.sync
        def _(sp):
            sp.dma_start(xT_raw[:], xT[0]).then_inc(xT_loaded, 16)
            for n in range(NW):
                if n >= 2:
                    sp.wait_ge(w_lo_done, n - 1)
                sp.dma_start(w_raw[:, n % 2], w_dram[n].rearrange("(t p) n -> p t n", p=128))\
                    .then_inc(w_loaded[n % 2], 16)
            sp.dma_start(x_tok[:], x[0].rearrange("(j p) d -> p j d", p=QT)).then_inc(x_loaded, 16)
            sp.wait_ge(xT_lo_done, 1)
            sp.dma_start(xT_raw[:], xT[1]).then_inc(xT_loaded, 16)

            def store_queries(b):
                sp.wait_ge(ring_out, next_job(b) + 6 + RING)
                sp.dma_start(qT_dram[bass.ds(b, 1)].rearrange("o (t p) s -> p (o t) s", p=128), xq[:])\
                    .then_inc(xq_stored, 16)

            def body(b):
                if not is_int(b, B - 2, B - 1):
                    sp.wait_ge(xT_lo_done, b + 2)
                    sp.dma_start(xT_raw[:], xT[bass.ds(b + 2, 1)].rearrange("o p t s -> p (o t) s"))\
                        .then_inc(xT_loaded, 16)
                if not is_int(b, 0):
                    store_queries(b - 1)
                sp.wait_ge(x1_ready, b * 2 + 2)
                sp.dma_start(x1_dram[bass.ds(b, 1)].rearrange("o (j p) d -> p (o j) d", p=QT), x1[:])\
                    .then_inc(x1_stored, 16)
                if not is_int(b, B - 1):
                    sp.dma_start(x_tok[:], x[bass.ds(b + 1, 1)].rearrange("o (j p) d -> p (o j) d", p=QT))\
                        .then_inc(x_loaded, 16)

            batches(sp, body)
            store_queries(B - 1)
            sp.wait_ge(x1_stored, 16 * B)
            sp.wait_ge(xq_stored, 16 * B)

        @block.gpsimd
        def _(pool):
            def split_x(b):
                if not is_int(b, 0):
                    pool.wait_ge(ring_full, qkv_job(b - 1) + 6)
                pool.wait_ge(xT_loaded, (b + 1) * 16)
                own_instruction(pool, waits_alone)
                pool_round(pool, xT_hi[:], xT_raw[:]).then_inc(xT_hi_done, 1)

            split_x(0)
            pool.memset(zeros[:], 0.0).then_inc(zeros_ready, 1)
            make_identity(pool, ident[:], ident_done)
            pool.memset(minus_half[:], -0.5).then_inc(ident_done, 1)
            pool.wait_ge(ident_done, 3)

            def root(b):
                pool.wait_ge(mv_ready, b + 1)
                pool_inverse_root(pool, rs[:], mv[:, :, 1:2], minus_half[:], LN_EPS, root_done, b * 2, waits_alone)

            split_x(1)
            root(0)
            split_x(2)
            with pool.Fori(1, B - 2) as b:
                root(b)
                split_x(b + 2)
            root(B - 2)
            root(B - 1)

        @block.scalar
        def _(act):
            slots = slot_x_dram.rearrange("r d -> (r d)").rearrange("(b p k) -> b p k", b=B, p=128)

            def zero_slots(b):
                act.dma_start(slots[bass.ds(b, 1)].rearrange("o p k -> p (o k)"), zeros[:]).then_inc(slots_zeroed, 16)

            for n in range(NW):
                act.wait_ge(w_loaded[n % 2], 16 * (n // 2 + 1))
                act.copy(w_hi[:, n], w_raw[:, n % 2]).then_inc(w_hi_done, 1)

            def hi(job, bank, out):
                act.wait_ge(ring_full, job + 1)
                act.copy(out, bank).then_inc(ring_hi, 1)

            def qkv_hi(b):
                job = qkv_job(b)
                for n in range(4):
                    bank = bank_of(qkv_job, b, n)[:, 0:2 * S].rearrange("p (f s) -> p f s", f=2)
                    hi(job + n, bank, qk_hi[:, n // 2, 2 * (n % 2):2 * (n % 2) + 2, :])
                for j in range(2):
                    hi(job + 4 + j, bank_of(qkv_job, b, 4 + j)[0:QT, :], v_hi[:, j, :])

            def x1T_split(b):
                for n in range(2):
                    bank = bank_of(next_job, b, n)[:, 0:2 * S].rearrange("p (t s) -> p t s", t=2)
                    hi(next_job(b) + n, bank, x1T_hi[:, 2 * n:2 * n + 2, :])

            def body(b):
                act.wait_ge(max_ready, b + 1)
                for j in range(2):
                    act.activation(probs[:, j, :], s_bank[0:QT, j * S:(j + 1) * S], ACT.Exp,
                                   bias=stat[:, j, 1:2], scale=SCALE, accum_out=stat[:, j, 2:3])\
                        .then_inc(exp_done, 1)
                if not is_int(b, 0):
                    x1T_split(b - 1)
                act.wait_ge(pT_full, b + 1)
                act.copy(pT_hi[:].rearrange("p t s -> p (t s)"), pT_bank[0:QT, 0:2 * S]).then_inc(pT_hi_done, 1)
                zero_slots(b)
                if not is_int(b, B - 1):
                    qkv_hi(b + 1)

            qkv_hi(0)
            act.wait_ge(zeros_ready, 1)
            batches(act, body)
            x1T_split(B - 1)
            act.wait_ge(slots_zeroed, 16 * B)

        @block.vector
        def _(dve):
            dve.sem_inc(ring_out, RING)
            for n in range(NW):
                if n == 1:
                    dve.wait_ge(xT_hi_done, 1)
                    dve.tensor_tensor(xT_lo[:], xT_raw[:], as_f32(xT_hi[:]), ALU.subtract).then_inc(xT_lo_done, 1)
                dve.wait_ge(w_hi_done, n + 1)
                dve.tensor_tensor(w_lo[:, n], w_raw[:, n % 2], as_f32(w_hi[:, n]), ALU.subtract)\
                    .then_inc(w_lo_done, 1)

            def lo(hi_count, bank, hi, out):
                dve.wait_ge(ring_hi, hi_count + 1)
                dve.tensor_tensor(out, bank, as_f32(hi), ALU.subtract).then_inc(ring_out, 1)

            def qkv_count(b):
                return 0 if is_int(b, 0) else b * 8 - 2

            def x1T_count(b):
                return B * 8 - 2 if is_int(b, B - 1) else b * 8 + 12

            def qkv_lo(b):
                for n in range(4):
                    bank = bank_of(qkv_job, b, n)[:, 0:2 * S].rearrange("p (f s) -> p f s", f=2)
                    part = (slice(None), n // 2, slice(2 * (n % 2), 2 * (n % 2) + 2), slice(None))
                    lo(qkv_count(b) + n, bank, qk_hi[part], qk_lo[part])
                for j in range(2):
                    lo(qkv_count(b) + 4 + j, bank_of(qkv_job, b, 4 + j)[0:QT, :], v_hi[:, j, :], v_lo[:, j, :])

            def next_batch(b):
                for n in range(2):
                    bank = bank_of(next_job, b, n)[:, 0:2 * S].rearrange("p (t s) -> p t s", t=2)
                    lo(x1T_count(b) + n, bank, x1T_hi[:, 2 * n:2 * n + 2, :], x1T_lo[:, 2 * n:2 * n + 2, :])
                if not is_int(b, 0):
                    dve.wait_ge(xq_stored, b * 16)
                for n in range(4):
                    dve.wait_ge(ring_full, next_job(b) + 2 + n + 1)
                    dve.tensor_copy(xq[:, 2 * n:2 * n + 2, :].rearrange("p t s -> p (t s)"),
                                    bank_of(next_job, b, 2 + n)[:, 0:2 * S]).then_inc(ring_out, 1)

            def split_x(b):
                dve.wait_ge(xT_hi_done, b + 1)
                dve.tensor_tensor(xT_lo[:], xT_raw[:], as_f32(xT_hi[:]), ALU.subtract).then_inc(xT_lo_done, 1)

            def body(b):
                st = Steps(dve, dve_steps, b * STEPS)
                dve.wait_ge(scores_ready, b + 1)
                st.step(dve.tensor_reduce(stat[:, :, 0], s_bank[0:QT, 0:2 * S].rearrange("p (j s) -> p j s", j=2),
                                          AX, ALU.max))
                dve.tensor_scalar(stat[:, :, 1], stat[:, :, 0], -SCALE, None, ALU.mult).then_inc(max_ready, 1)
                if not is_int(b, 0):
                    next_batch(b - 1)
                dve.wait_ge(exp_done, b * 2 + 2)
                st.step(dve.reciprocal(stat[:, :, 3:4], stat[:, :, 2:3]))
                dve.wait_ge(pT_hi_done, b + 1)
                dve.tensor_tensor(pT_lo[:].rearrange("p t s -> p (t s)"), pT_bank[0:QT, 0:2 * S],
                                  as_f32(pT_hi[:]).rearrange("p t s -> p (t s)"), ALU.subtract).then_inc(pT_done, 1)
                dve.wait_ge(x_loaded, b * 16 + 16)
                for j in range(2):
                    dve.wait_ge(o_full, b * 2 + j + 1)
                    dve.scalar_tensor_tensor(out=res[:, j, :], in0=o_bank[j][0:QT, :], scalar=stat[:, j, 3:4],
                                             in1=x_tok[:, j, :], op0=ALU.mult, op1=ALU.add).then_inc(o_read, 1)
                    dve.wait_ge(o_read, b * 2 + j + 1)
                    st.step(dve.bn_stats(bn[:, j, :], res[:, j, :]))
                    own_instruction(dve, dve_waits_alone)
                    ins = dve.bn_aggr(mv[:, j, :], bn[:, j, :])
                    if j == 0:
                        st.step(ins)
                ins.then_inc(mv_ready, 1)
                dve.wait_ge(root_done, b * 2 + 2)
                if not is_int(b, 0):
                    dve.wait_ge(x1_stored, b * 16)
                for j in range(2):
                    dve.tensor_scalar(x1[:, j, :], res[:, j, :], mv[:, j, 0:1], rs[:, j, 0:1],
                                      ALU.subtract, ALU.mult).then_inc(x1_ready, 1)
                if not is_int(b, B - 1):
                    qkv_lo(b + 1)
                if not is_int(b, B - 2, B - 1):
                    split_x(b + 2)
                assert st.n == STEPS

            qkv_lo(0)
            split_x(1)
            batches(dve, body)
            next_batch(B - 1)

        @block.tensor
        def _(pe):
            def open_bank(job):
                pe.wait_ge(ring_out, job + 1)

            def ring_done(job):
                return job + RING + 1

            def qkv(b):
                pe.wait_ge(xT_lo_done, b + 1)
                for n in range(4):
                    open_bank(qkv_job(b) + n)
                    if is_int(b, 0):
                        pe.wait_ge(w_lo_done, n // 2 + 1)
                    bank = bank_of(qkv_job, b, n)
                    for f in range(2):
                        cols = slice((2 * (n % 2) + f) * 128, (2 * (n % 2) + f + 1) * 128)
                        for t in range(KD):
                            last = matmul3(pe, bank[:, f * S:(f + 1) * S], w_hi[:, n // 2, t, cols],
                                           w_lo[:, n // 2, t, cols], xT_hi[:, t, :], xT_lo[:, t, :],
                                           t == 0, t == KD - 1)
                    last.then_inc(ring_full, 1)
                for j in range(2):
                    open_bank(qkv_job(b) + 4 + j)
                    if is_int(b, 0):
                        pe.wait_ge(w_lo_done, 3)
                    for t in range(KD):
                        last = matmul3(pe, bank_of(qkv_job, b, 4 + j)[0:QT, :],
                                       xT_hi[:, t, j * QT:(j + 1) * QT], xT_lo[:, t, j * QT:(j + 1) * QT],
                                       w_hi[:, 2, t, :], w_lo[:, 2, t, :], t == 0, t == KD - 1)
                    last.then_inc(ring_full, 1)

            def transposed_and_queries(b):
                pe.wait_ge(x1_ready, b * 2 + 2)
                for n in range(2):
                    open_bank(next_job(b) + n)
                    for t in range(2):
                        for j in range(2):
                            c = (2 * n + t) * 128
                            last = pe.transpose(bank_of(next_job, b, n)[:, t * S + j * QT:t * S + (j + 1) * QT],
                                                x1[:, j, c:c + 128], ident[0:QT, 0:QT])
                    last.then_inc(ring_full, 1)
                for n in range(4):
                    open_bank(next_job(b) + 2 + n)
                    if n == 0:
                        pe.wait_ge(ring_out, ring_done(next_job(b) + 1))
                    if is_int(b, 0):
                        pe.wait_ge(w_lo_done, NW)
                    for f in range(2):
                        c = (2 * n + f) * 128
                        piece, c = 3 + c // 512, c % 512
                        for t in range(KD):
                            last = matmul3(pe, bank_of(next_job, b, 2 + n)[:, f * S:(f + 1) * S],
                                           w_hi[:, piece, t, c:c + 128], w_lo[:, piece, t, c:c + 128],
                                           x1T_hi[:, t, :], x1T_lo[:, t, :], t == 0, t == KD - 1)
                    last.then_inc(ring_full, 1)

            def body(b):
                pe.wait_ge(ring_out, ring_done(qkv_job(b) + 3))
                if not is_int(b, 0):
                    pe.wait_ge(exp_done, b * 2)
                for j in range(2):
                    for t in range(KD):
                        last = matmul3(pe, s_bank[0:QT, j * S:(j + 1) * S],
                                       qk_hi[:, 0, t, j * QT:(j + 1) * QT], qk_lo[:, 0, t, j * QT:(j + 1) * QT],
                                       qk_hi[:, 1, t, :], qk_lo[:, 1, t, :], t == 0, t == KD - 1)
                last.then_inc(scores_ready, 1)
                if not is_int(b, 0):
                    transposed_and_queries(b - 1)
                pe.wait_ge(exp_done, b * 2 + 2)
                if is_int(b, 0):
                    pe.wait_ge(ident_done, 2)
                else:
                    pe.wait_ge(pT_done, b)
                for t in range(2):
                    for j in range(2):
                        last = pe.transpose(pT_bank[0:QT, t * S + j * QT:t * S + (j + 1) * QT],
                                            probs[:, j, t * QT:(t + 1) * QT], ident[0:QT, 0:QT])
                last.then_inc(pT_full, 1)
                pe.wait_ge(ring_out, ring_done(qkv_job(b) + 5))
                pe.wait_ge(pT_done, b + 1)
                for j in range(2):
                    if not is_int(b, 0):
                        pe.wait_ge(o_read, b * 2 - 1 + j)
                    for t in range(2):
                        last = matmul3(pe, o_bank[j][0:QT, :], pT_hi[:, t, j * QT:(j + 1) * QT],
                                       pT_lo[:, t, j * QT:(j + 1) * QT], v_hi[:, t, :], v_lo[:, t, :],
                                       t == 0, t == 1)
                    last.then_inc(o_full, 1)
                if not is_int(b, B - 1):
                    qkv(b + 1)

            qkv(0)
            batches(pe, body)
            transposed_and_queries(B - 1)


def cross_attention(nc, half, ctxT, wkv, null_kv, qT_dram, oT_dram):
    SCALE = float(DH) ** -0.5
    NH = HEADS // 2
    FEAT = NH * DH
    KT = CTX_D // 128
    KEYS = CTX_LEN + 1
    KW = KEYS + 1
    HALF = KW // 2
    MT = -(-KEYS // 128)
    LAST = CTX_LEN - (MT - 1) * 128
    CHUNK = 2
    NC = KT // CHUNK
    JOBS = MT + 8 + 3 * NH + NH
    with ExitStack() as stack:
        m = Scope(nc, stack, f"xa{half}", "xa")
        if half:
            m.clear()
        ident = m.sb("ident", [128, 128])
        wk_hi, wk_lo = (m.sb(f"wk_{x}", [128, KT, FEAT], F32R) for x in ("hi", "lo"))
        wv_hi, wv_lo = (m.sb(f"wv_{x}", [128, KT, FEAT], F32R) for x in ("hi", "lo"))
        raw = m.sb("raw", [128, 2, CHUNK, CTX_LEN])
        ctx_hi, ctx_lo = (m.sb(f"ctx_{x}", [128, KT, KW], F32R) for x in ("hi", "lo"))
        v = m.sb("v", [128, MT, NH, 2, DH], F32R)
        k = m.sb("k", [128, 4, KW], F32R)
        probs = m.sb("probs", [QT, 2, 2, MT * 128])
        pT_hi, pT_lo = (m.sb(f"pT_{x}", [128, MT, S], F32R) for x in ("hi", "lo"))
        q_raw = m.sb("q_raw", [128, NH, S])
        q_hi, q_lo = (m.sb(f"q_{x}", [128, NH, S], F32R) for x in ("hi", "lo"))
        o_part = m.sb("o_part", [DH, S])
        oT = m.sb("oT", [128, NH // 2, S])
        stat = m.sb("stat", [QT, NH, 2, 4])
        null_k = m.sb("null_k", [128, 4])
        null_v = o_part[0:1, 0:DH]
        null_row = pT_lo[0:1].rearrange("p t s -> p (t s)")[:, 0:NH * 2 * DH].rearrange("p (h i d) -> p h i d", h=NH, i=2)
        ring = [m.bank(f"ring{n}") for n in range(RING)]
        s_bank = [m.bank(f"scores{j}", (128, 2, 512)) for j in range(2)]

        ident_done = m.sem("ident_done")
        raw_loaded = [m.sem(f"raw_loaded{n}") for n in range(2)]
        weights_hi, raw_hi, raw_lo = m.sem("weights_hi"), m.sem("raw_hi"), m.sem("raw_lo")
        key_first = m.sem("key_first")
        null_value_placed = m.sem("null_value_placed")
        null_loaded, null_placed, null_steps = m.sem("null_loaded"), m.sem("null_placed"), m.sem("null_steps")
        q_loaded, q_hi_done, q_lo_done = m.sem("q_loaded"), m.sem("q_hi_done"), m.sem("q_lo_done")
        ring_full, ring_first, ring_out = m.sem("ring_full"), m.sem("ring_first"), m.sem("ring_out")
        scores_ready = [m.sem(f"scores_ready{j}") for j in range(2)]
        max_done = m.sem("max_done")
        max_ready, exp_done = m.sem("max_ready"), m.sem("exp_done")
        inverse_ready, probs_ready = m.sem("inverse_ready"), m.sem("probs_ready")
        sum_steps = m.sem("sum_steps")
        oT_stored = m.sem("oT_stored")
        waits_alone = m.sem("waits_alone")

        f0 = half * FEAT
        w_pieces = [(cols, t) for cols in (INNER + f0, f0) for t in range(0, KT, CHUNK)]
        NP = len(w_pieces)

        def key_job(b, pair, n):
            return b * JOBS + (MT + n if pair == 0 else slot_job(0, 2 * pair - 2 + n, "keys"))

        def slot_job(b, h, what):
            j = MT + 2
            for s in range(h):
                j += (s < NH - 2) + (s >= 2) + 3 * (s >= 1)
            if what != "keys":
                j += h < NH - 2
            if what == "transposes":
                j += h >= 2
            return b * JOBS + j

        END = slot_job(0, NH, "keys")

        def product_job(b, h):
            return b * JOBS + END + 4 * (h - (NH - 2)) if h >= NH - 2 else slot_job(b, h + 2, "product")

        def transposes_job(b, h):
            return b * JOBS + END + 1 if h == NH - 1 else slot_job(b, h + 1, "transposes")

        assert END + 5 == JOBS

        def bank(local):
            return ring[local % RING]

        def before(b, local):
            return b * JOBS + (local - RING if local >= RING else
                               max(j for j in range(JOBS) if j % RING == local % RING) - JOBS) + 1

        block = stack.enter_context(nc.Block())

        @block.sync
        def _(sp):
            for i in range(2):
                sp.dma_start(null_k[i * DH:(i + 1) * DH, 0:1], null_kv[0, :].rearrange("(d o) -> d o", o=1))\
                    .then_inc(null_loaded, 16)
            sp.dma_start(null_v, null_kv[1:2, :]).then_inc(null_loaded, 16)
            for n, (cols, t) in enumerate(w_pieces):
                if n >= 2:
                    sp.wait_ge(raw_lo, n - 1)
                sp.dma_start(raw[:, n % 2, :, 0:FEAT],
                             wkv[t * 128:(t + CHUNK) * 128, cols:cols + FEAT].rearrange("(t p) n -> p t n", p=128))\
                    .then_inc(raw_loaded[n % 2], 16)

            def load_context(b):
                for n in range(NC):
                    sp.wait_ge(raw_lo, b * NC + NP + n - 1)
                    sp.dma_start(raw[:, n % 2], ctxT[bass.ds(b, 1), :, n * CHUNK:(n + 1) * CHUNK, :]
                                 .rearrange("o p t s -> p (o t) s")).then_inc(raw_loaded[n % 2], 16)

            def load_queries(b):
                src = qT_dram[bass.ds(b, 1), f0:f0 + FEAT, :].rearrange("o (h d) s -> d (o h) s", d=DH)
                for i in range(2):
                    sp.dma_start(q_raw[i * DH:(i + 1) * DH], src).then_inc(q_loaded, 16)

            def store(b):
                sp.wait_ge(ring_out, b * JOBS + JOBS + RING)
                sp.dma_start(oT_dram[bass.ds(b, 1), f0:f0 + FEAT, :].rearrange("o (t p) s -> p (o t) s", p=128),
                             oT[:]).then_inc(oT_stored, 16)

            sp.wait_ge(null_placed, 1)
            sp.dma_start(as_f32(v[LAST:LAST + 1, MT - 1].rearrange("p h i d -> p (h i d)")),
                           as_f32(null_row.rearrange("p h i d -> p (h i d)"))).then_inc(null_value_placed, 16)

            load_queries(0)
            load_context(0)
            with sp.Fori(1, B) as b:
                sp.wait_ge(q_lo_done, b)
                load_queries(b)
                load_context(b)
                store(b - 1)
            store(B - 1)
            sp.wait_ge(oT_stored, 16 * B)

        @block.gpsimd
        def _(pool):
            make_identity(pool, ident[:], ident_done)
            pool.memset(probs[:], 0.0).then_inc(ident_done, 1)
            def context_hi(b, n):
                pool.wait_ge(raw_loaded[n % 2], b * 16 * (NC // 2) + 16 * (NP // 2 + n // 2 + 1))
                own_instruction(pool, waits_alone)
                pool_round(pool, ctx_hi[:, n * CHUNK:(n + 1) * CHUNK, 0:CTX_LEN], raw[:, n % 2]).then_inc(raw_hi, 1)

            def queries_hi(b):
                pool.wait_ge(q_loaded, b * 32 + 32)
                own_instruction(pool, waits_alone)
                pool_round(pool, q_hi[:], q_raw[:]).then_inc(q_hi_done, 1)

            def normalise(b, h):
                for j in range(2):
                    pool.wait_ge(inverse_ready, b * 2 * NH + 2 * h + j + 1)
                    own_instruction(pool, waits_alone)
                    pool.tensor_scalar(probs[:, h % 2, j, 0:KW], probs[:, h % 2, j, 0:KW], stat[:, h, j, 3:4], 1.0,
                                       ALU.mult, ALU.mult).then_inc(probs_ready, 1)

            def body(b, more):
                for h in range(NH):
                    if more and h >= NH - 2:
                        if h == NH - 2:
                            pool.wait_ge(ring_full, key_job(b, 3, 1) + 1)
                        context_hi(b + 1, 2 * (h - NH + 2))
                    normalise(b, h)
                    if more and h >= NH - 2:
                        context_hi(b + 1, 2 * (h - NH + 2) + 1)
                if more:
                    pool.wait_ge(scores_ready[1], b * NH + NH)
                    queries_hi(b + 1)

            queries_hi(0)
            for n in range(NC):
                context_hi(0, n)
            with pool.Fori(0, B - 1) as b:
                body(b, True)
            body(B - 1, False)

        @block.scalar
        def _(act):
            act.sem_inc(exp_done, 2)
            for n, (cols, t) in enumerate(w_pieces):
                act.wait_ge(raw_loaded[n % 2], 16 * (n // 2 + 1))
                w = wv_hi if n < NP // 2 else wk_hi
                act.copy(w[:, t:t + CHUNK, :], raw[:, n % 2, :, 0:FEAT]).then_inc(weights_hi, 1)

            def values(b):
                for t in range(MT):
                    rows = 128 if t < MT - 1 else LAST
                    act.wait_ge(ring_full, b * JOBS + t + 1)
                    act.copy(v[0:rows, t, :, 0, :], bank(t)[0:rows, :].rearrange("p (h d) -> p h d", h=NH))\
                        .then_inc(ring_first, 1)

            def keys(b, pair, n):
                local = key_job(0, pair, n)
                act.wait_ge(ring_full, b * JOBS + local + 1)
                width = HALF if n == 0 else CTX_LEN - HALF
                for i in range(2):
                    ins = act.copy(k[0:DH, (2 * pair + i) % 4, n * HALF:n * HALF + width],
                                   bank(local)[i * DH:(i + 1) * DH, 0:width])
                    ins.then_inc(key_first, 1)

            def transposes(b, h):
                for n in range(MT // 2):
                    local = transposes_job(0, h) + n
                    act.wait_ge(ring_full, b * JOBS + local + 1)
                    act.copy(pT_hi[:, 2 * n:2 * n + 2, :].rearrange("p t s -> p (t s)"), bank(local)[:, 0:2 * S])\
                        .then_inc(ring_first, 1)

            def product(b, h):
                local = product_job(0, h)
                act.wait_ge(ring_full, b * JOBS + local + 1)
                act.wait_ge(ring_out, b * JOBS + RING + 1 + (product_job(0, h - 1) if h else
                                                           product_job(0, NH - 1) - JOBS))
                act.copy(o_part[:], bank(local)[0:DH, 0:S]).then_inc(ring_first, 1)

            def exponents(b, h):
                for j in range(2):
                    act.wait_ge(max_ready, b * 2 * NH + 2 * h + j + 1)
                    act.activation(probs[:, h % 2, j, 0:KW].rearrange("p (i s) -> p i s", i=2),
                                   s_bank[j][0:QT, :, 0:HALF], ACT.Exp, bias=stat[:, h, j, 1:2], scale=SCALE,
                                   accum_out=stat[:, h, j, 2:3]).then_inc(exp_done, 1)

            def body(b):
                values(b)
                for n in range(2):
                    keys(b, 0, n)
                for h in range(NH):
                    exponents(b, h)
                    if h < NH - 2:
                        keys(b, h // 2 + 1, h % 2)
                    if h >= 2:
                        product(b, h - 2)
                    if h >= 1:
                        transposes(b, h - 1)
                product(b, NH - 2)
                transposes(b, NH - 1)
                product(b, NH - 1)

            act.wait_ge(ident_done, 3)
            with act.Fori(0, B) as b:
                body(b)

        FIRSTS = JOBS - 8

        @block.vector
        def _(dve):
            dve.sem_inc(ring_out, RING)
            st = Steps(dve, null_steps)
            dve.wait_ge(null_loaded, 48)
            st.step(dve.tensor_copy(k[0:DH, 0, KW - 1:KW], null_k[0:DH, 0:1]))
            st.step(dve.tensor_copy(k[DH:128, 1, KW - 1:KW], null_k[DH:128, 0:1]))
            st.step(dve.tensor_tensor(null_k[DH:128, 1:2], null_k[DH:128, 0:1],
                                      as_f32(k[DH:128, 1, KW - 1:KW]), ALU.subtract))
            st.step(dve.tensor_copy(null_k[0:DH, 1:2], as_f32(k[0:DH, 0, KW - 1:KW])))
            for i in range(4):
                for c in range(2):
                    st.step(dve.tensor_copy(k[:, i, CTX_LEN + c:CTX_LEN + c + 1], null_k[:, 1:2]))
            st.step(dve.tensor_copy(null_row[:, :, 0, :],
                                    null_v.rearrange("p (o d) -> p o d", o=1).broadcast_to([1, NH, DH])))
            dve.tensor_tensor(null_row[:, :, 1, :],
                              null_v.rearrange("p (o d) -> p o d", o=1).broadcast_to([1, NH, DH]),
                              as_f32(null_row[:, :, 0, :]), ALU.subtract).then_inc(null_placed, 1)
            dve.memset(as_f32(ctx_hi[:, :, CTX_LEN:KW]), 0.0).then_inc(null_placed, 1)
            dve.memset(as_f32(ctx_lo[:, :, CTX_LEN:KW]), 0.0).then_inc(null_placed, 1)
            for n, (cols, t) in enumerate(w_pieces):
                hi, lo = (wv_hi, wv_lo) if n < NP // 2 else (wk_hi, wk_lo)
                dve.wait_ge(weights_hi, n + 1)
                dve.tensor_tensor(lo[:, t:t + CHUNK, :], raw[:, n % 2, :, 0:FEAT], as_f32(hi[:, t:t + CHUNK, :]),
                                  ALU.subtract).then_inc(raw_lo, 1)

            def context_lo(b, n):
                part = (slice(None), slice(n * CHUNK, (n + 1) * CHUNK), slice(0, CTX_LEN))
                dve.wait_ge(raw_hi, b * NC + n + 1)
                dve.tensor_tensor(ctx_lo[part], raw[:, n % 2], as_f32(ctx_hi[part]), ALU.subtract).then_inc(raw_lo, 1)

            def queries_lo(b):
                dve.wait_ge(q_hi_done, b + 1)
                dve.tensor_tensor(q_lo[:], q_raw[:], as_f32(q_hi[:]), ALU.subtract).then_inc(q_lo_done, 1)

            def firsts(local):
                keys_before = sum(key_job(0, p, n) < local for p in range(4) for n in range(2))
                return local - keys_before + 1

            def values(b):
                for t in range(MT):
                    rows = 128 if t < MT - 1 else LAST
                    dve.wait_ge(ring_first, b * FIRSTS + firsts(t))
                    dve.tensor_tensor(v[0:rows, t, :, 1, :], bank(t)[0:rows, :].rearrange("p (h d) -> p h d", h=NH),
                                      as_f32(v[0:rows, t, :, 0, :]), ALU.subtract).then_inc(ring_out, 1)

            def keys(b, pair, n):
                local = key_job(0, pair, n)
                width = HALF if n == 0 else CTX_LEN - HALF
                for i in range(2):
                    dve.wait_ge(key_first, b * 16 + 4 * pair + 2 * n + i + 1)
                    part = (2 * pair + i) % 4, slice(n * HALF, n * HALF + width)
                    ins = dve.tensor_tensor(k[(slice(DH, 128), *part)], bank(local)[i * DH:(i + 1) * DH, 0:width],
                                            as_f32(k[(slice(0, DH), *part)]), ALU.subtract)
                ins.then_inc(ring_out, 1)

            def transposes(b, h):
                for n in range(MT // 2):
                    local = transposes_job(0, h) + n
                    dve.wait_ge(ring_first, b * FIRSTS + firsts(local))
                    part = (slice(None), slice(2 * n, 2 * n + 2), slice(None))
                    dve.tensor_tensor(pT_lo[part].rearrange("p t s -> p (t s)"), bank(local)[:, 0:2 * S],
                                      as_f32(pT_hi[part]).rearrange("p t s -> p (t s)"), ALU.subtract)\
                       .then_inc(ring_out, 1)

            def product(b, h):
                local = product_job(0, h)
                dve.wait_ge(ring_first, b * FIRSTS + firsts(local))
                dve.tensor_tensor(oT[(h % 2) * DH:(h % 2 + 1) * DH, h // 2, :], bank(local)[DH:128, 0:S], o_part[:],
                                  ALU.add).then_inc(ring_out, 1)

            def maxima(b, h):
                for j in range(2):
                    dve.wait_ge(scores_ready[j], b * NH + h + 1)
                    dve.tensor_reduce(stat[:, h, j, 0:1], s_bank[j][0:QT, :, 0:HALF], mybir.AxisListType.XY, ALU.max)\
                       .then_inc(max_done, 1)
                    dve.wait_ge(max_done, b * 2 * NH + 2 * h + j + 1)
                    dve.tensor_scalar(stat[:, h, j, 1:2], stat[:, h, j, 0:1], -SCALE, None, ALU.mult)\
                       .then_inc(max_ready, 1)

            def inverses(b, h):
                for j in range(2):
                    dve.wait_ge(exp_done, b * 2 * NH + 2 * h + j + 3)
                    dve.tensor_tensor(stat[:, h, j, 2:3], stat[:, h, j, 2:3], probs[:, h % 2, j, KW - 1:KW],
                                      ALU.subtract).then_inc(sum_steps, 1)
                    dve.wait_ge(sum_steps, b * 2 * NH + 2 * h + j + 1)
                    dve.reciprocal(stat[:, h, j, 3:4], stat[:, h, j, 2:3]).then_inc(inverse_ready, 1)

            def body(b, more, first=False):
                values(b)
                for n in range(2):
                    keys(b, 0, n)
                for h in range(NH):
                    maxima(b, h)
                    if h < NH - 2:
                        keys(b, h // 2 + 1, h % 2)
                    if more and h >= NH - 2:
                        context_lo(b + 1, 2 * (h - NH + 2))
                    if h == 2 and not first:
                        dve.wait_ge(oT_stored, b * 16)
                    if h >= 2:
                        product(b, h - 2)
                    inverses(b, h)
                    if h >= 1:
                        transposes(b, h - 1)
                    if more and h >= NH - 2:
                        context_lo(b + 1, 2 * (h - NH + 2) + 1)
                product(b, NH - 2)
                transposes(b, NH - 1)
                product(b, NH - 1)
                if more:
                    queries_lo(b + 1)

            queries_lo(0)
            for n in range(NC):
                context_lo(0, n)
            body(0, True, first=True)
            with dve.Fori(1, B - 1) as b:
                body(b, True)
            body(B - 1, False)

        @block.tensor
        def _(pe):
            def open_bank(b, local):
                pe.wait_ge(ring_out, before(b, local) + RING)

            def values(b):
                for t in range(MT):
                    rows = 128 if t < MT - 1 else LAST
                    open_bank(b, t)
                    for c in range(KT):
                        if t == 0 and c % CHUNK == 0:
                            pe.wait_ge(raw_lo, b * NC + NP + c // CHUNK + 1)
                        last = matmul3(pe, bank(t)[0:rows, :], ctx_hi[:, c, t * 128:t * 128 + rows],
                                       ctx_lo[:, c, t * 128:t * 128 + rows], wv_hi[:, c, :], wv_lo[:, c, :],
                                       c == 0, c == KT - 1)
                    last.then_inc(ring_full, 1)

            def keys(b, pair, n):
                local = key_job(0, pair, n)
                open_bank(b, local)
                for c in range(KT):
                    last = matmul3(pe, bank(local)[:, 0:HALF], wk_hi[:, c, pair * 128:(pair + 1) * 128],
                                   wk_lo[:, c, pair * 128:(pair + 1) * 128],
                                   ctx_hi[:, c, n * HALF:(n + 1) * HALF], ctx_lo[:, c, n * HALF:(n + 1) * HALF],
                                   c == 0, c == KT - 1)
                last.then_inc(ring_full, 1)

            def scores(b, h):
                pe.wait_ge(ring_out, key_job(b, h // 2, 1) + RING + 1)
                for j in range(2):
                    pe.wait_ge(exp_done, b * 2 * NH + 2 * h + j + 1)
                    for i in range(2):
                        for n, q in enumerate((q_hi, q_lo)):
                            last = pe.matmul(s_bank[j][0:QT, i, 0:HALF], q[:, h, j * QT:(j + 1) * QT],
                                             k[:, h % 4, i * HALF:(i + 1) * HALF], start=(n == 0), stop=(n == 1))
                    last.then_inc(scores_ready[j], 1)

            def transposes(b, h):
                pe.wait_ge(probs_ready, b * 2 * NH + 2 * h + 2)
                for n in range(MT // 2):
                    local = transposes_job(0, h) + n
                    open_bank(b, local)
                    for t in range(2):
                        for j in range(2):
                            c = (2 * n + t) * 128
                            last = pe.transpose(bank(local)[:, t * S + j * QT:t * S + (j + 1) * QT],
                                                probs[:, h % 2, j, c:c + 128], ident[0:QT, 0:QT])
                    last.then_inc(ring_full, 1)

            def product(b, h):
                local = product_job(0, h)
                open_bank(b, local)
                pe.wait_ge(ring_out, transposes_job(b, h) + 2 + RING + 1)
                for t in range(MT):
                    rows = 128 if t < MT - 1 else LAST + 1
                    for n, p in enumerate((pT_hi, pT_lo)):
                        last = pe.matmul(bank(local)[:, 0:S], v[0:rows, t, h].rearrange("p i d -> p (i d)"),
                                         p[0:rows, t, :], start=(t == 0 and n == 0), stop=(t == MT - 1 and n == 1))
                last.then_inc(ring_full, 1)

            def body(b):
                values(b)
                for n in range(2):
                    keys(b, 0, n)
                pe.wait_ge(q_lo_done, b + 1)
                for h in range(NH):
                    scores(b, h)
                    if h < NH - 2:
                        keys(b, h // 2 + 1, h % 2)
                    if h >= 2:
                        product(b, h - 2)
                    if h >= 1:
                        transposes(b, h - 1)
                product(b, NH - 2)
                transposes(b, NH - 1)
                product(b, NH - 1)

            pe.wait_ge(ident_done, 3)
            pe.wait_ge(null_value_placed, 16)
            pe.wait_ge(null_placed, 3)
            with pe.Fori(0, B) as b:
                body(b)


def output_router(nc, oT_dram, wout, ln_scale, ln_bias, x1_dram, wr, br, x2_dram, logits_dram):
    FT = INNER // 128
    with ExitStack() as stack:
        m = Scope(nc, stack, "out")
        ident = m.sb("ident", [128, 128])
        w_raw = m.sb("w_raw", [128, 2, 2, D])
        w_hi, w_lo = (m.sb(f"w_{x}", [128, FT, D], F32R) for x in ("hi", "lo"))
        o_raw = m.sb("o_raw", [128, FT, S])
        o_hi, o_lo = (m.sb(f"o_{x}", [128, FT, S], F32R) for x in ("hi", "lo"))
        scale_b, bias_b = m.sb("scale_b", [QT, D]), m.sb("bias_b", [QT, D])
        wr_sb = m.sb("wr", [128, KD, E])
        br_b = m.sb("br_b", [QT, E])
        x1 = m.sb("x1", [QT, 2, D])
        normed = m.sb("normed", [QT, 2, D])
        res = m.sb("res", [QT, 2, D])
        x2 = m.sb("x2", [QT, 2, D])
        x2T = m.sb("x2T", [128, KD, S])
        logits = m.sb("logits", [QT, 2, E])
        bn, mv, rs = m.sb("bn", [QT, 2, 6]), m.sb("mv", [QT, 2, 2]), m.sb("rs", [QT, 2, 1])
        minus_half = m.sb("minus_half", [QT, 2, 1])
        y_bank = [m.bank(f"y{j}") for j in range(2)]
        t_bank = [m.bank(f"t{j}") for j in range(2)]
        l_bank = m.bank("l")

        ident_done, consts_loaded = m.sem("ident_done"), m.sem("consts_loaded")
        w_loaded = [m.sem(f"w_loaded{n}") for n in range(2)]
        w_hi_done, w_lo_done = m.sem("w_hi_done"), m.sem("w_lo_done")
        o_loaded, o_hi_done, o_lo_done = m.sem("o_loaded"), m.sem("o_hi_done"), m.sem("o_lo_done")
        x1_loaded, y_full, y_read = m.sem("x1_loaded"), m.sem("y_full"), m.sem("y_read")
        x2_ready, x2_stored = m.sem("x2_ready"), m.sem("x2_stored")
        t_full, t_read = m.sem("t_full"), m.sem("t_read")
        l_full, l_read, l_stored = m.sem("l_full"), m.sem("l_read"), m.sem("l_stored")
        biased, summed = m.sem("biased"), m.sem("summed")
        mv_ready, root_done = m.sem("mv_ready"), m.sem("root_done")
        dve_steps = m.sem("dve_steps")
        waits_alone, dve_waits_alone = m.sem("waits_alone"), m.sem("dve_waits_alone")
        STEPS = 6
        NW = FT // 2
        block = stack.enter_context(nc.Block())

        @block.sync
        def _(sp):
            for n in range(NW):
                if n >= 2:
                    sp.wait_ge(w_lo_done, n - 1)
                sp.dma_start(w_raw[:, n % 2], wout[n * 256:(n + 1) * 256, :].rearrange("(t p) n -> p t n", p=128))\
                    .then_inc(w_loaded[n % 2], 16)
                if n == 0:
                    sp.dma_start(o_raw[:], oT_dram[0].rearrange("(t p) s -> p t s", p=128)).then_inc(o_loaded, 16)
            sp.dma_start(scale_b[:], ln_scale.rearrange("(o n) -> o n", o=1).broadcast_to([QT, D])).then_inc(consts_loaded, 16)
            sp.dma_start(bias_b[:], ln_bias.rearrange("(o n) -> o n", o=1).broadcast_to([QT, D])).then_inc(consts_loaded, 16)
            sp.dma_start(wr_sb[:], wr.rearrange("(t p) e -> p t e", p=128)).then_inc(consts_loaded, 16)
            sp.dma_start(br_b[:], br.rearrange("(o n) -> o n", o=1).broadcast_to([QT, E])).then_inc(consts_loaded, 16)

            def load_x1(b):
                sp.dma_start(x1[:], x1_dram[bass.ds(b, 1)].rearrange("o (j p) d -> p (o j) d", p=QT))\
                    .then_inc(x1_loaded, 16)

            def store(b):
                sp.wait_ge(x2_ready, b * 2 + 2)
                sp.dma_start(x2_dram[bass.ds(b, 1)].rearrange("o (j p) d -> p (o j) d", p=QT), x2[:])\
                    .then_inc(x2_stored, 16)

            def store_logits(b):
                sp.wait_ge(l_read, b + 1)
                sp.dma_start(logits_dram[:, bass.ds(b * 2, 2), :], logits[:]).then_inc(l_stored, 16)

            load_x1(0)
            sp.wait_ge(o_lo_done, 1)
            sp.dma_start(o_raw[:], oT_dram[1].rearrange("(t p) s -> p t s", p=128)).then_inc(o_loaded, 16)
            with sp.Fori(1, B - 1) as b:
                sp.wait_ge(o_lo_done, b + 1)
                sp.dma_start(o_raw[:], oT_dram[bass.ds(b + 1, 1)].rearrange("o (t p) s -> p (o t) s", p=128))\
                    .then_inc(o_loaded, 16)
                store(b - 1)
                load_x1(b)
                store_logits(b - 1)
            store(B - 2)
            load_x1(B - 1)
            store_logits(B - 2)
            store(B - 1)
            store_logits(B - 1)
            sp.wait_ge(x2_stored, 16 * B)
            sp.wait_ge(l_stored, 16 * B)

        @block.gpsimd
        def _(pool):
            make_identity(pool, ident[:], ident_done)
            pool.wait_ge(consts_loaded, 64)

            pool.memset(minus_half[:], -0.5).then_inc(ident_done, 1)
            pool.wait_ge(ident_done, 3)

            def body(b):
                pool.wait_ge(x1_loaded, b * 16 + 16)
                pool.tensor_tensor(x1[:], x1[:], bias_b[:].rearrange("p (o d) -> p o d", o=1).broadcast_to([QT, 2, D]),
                                   ALU.add).then_inc(biased, 1)
                for n, eps in enumerate((OUT_EPS, LN_EPS)):
                    pool.wait_ge(mv_ready, b * 2 + n + 1)
                    pool_inverse_root(pool, rs[:], mv[:, :, 1:2], minus_half[:], eps, root_done, b * 4 + 2 * n, waits_alone)

            with pool.Fori(0, B) as b:
                body(b)

        @block.scalar
        def _(act):
            for n in range(NW):
                act.wait_ge(w_loaded[n % 2], 16 * (n // 2 + 1))
                act.copy(w_hi[:, 2 * n:2 * n + 2, :], w_raw[:, n % 2]).then_inc(w_hi_done, 1)

            def split(b, first=False):
                act.wait_ge(o_loaded, b * 16 + 16)
                if not first:
                    act.wait_ge(y_full, b * 2)
                act.copy(o_hi[:], o_raw[:]).then_inc(o_hi_done, 1)

            def transposed(b):
                for n in range(2):
                    act.wait_ge(t_full, b * 2 + n + 1)
                    act.copy(x2T[:, 2 * n:2 * n + 2, :].rearrange("p t s -> p (t s)"), t_bank[n][:, 0:2 * S])\
                        .then_inc(t_read, 1)

            split(0, first=True)
            with act.Fori(1, B) as b:
                split(b)
                transposed(b - 1)
            transposed(B - 1)

        @block.vector
        def _(dve):
            for n in range(NW):
                dve.wait_ge(w_hi_done, n + 1)
                dve.tensor_tensor(w_lo[:, 2 * n:2 * n + 2, :], w_raw[:, n % 2], as_f32(w_hi[:, 2 * n:2 * n + 2, :]),
                                  ALU.subtract).then_inc(w_lo_done, 1)

            def split(b):
                dve.wait_ge(o_hi_done, b + 1)
                dve.tensor_tensor(o_lo[:], o_raw[:], as_f32(o_hi[:]), ALU.subtract).then_inc(o_lo_done, 1)

            def moments(st, of, done, count):
                for j in range(2):
                    dve.wait_ge(done, count + j + 1)
                    st.step(dve.bn_stats(bn[:, j, :], of(j)))
                    own_instruction(dve, dve_waits_alone)
                    ins = dve.bn_aggr(mv[:, j, :], bn[:, j, :])
                    if j == 0:
                        st.step(ins)
                ins.then_inc(mv_ready, 1)

            def norms(b, first=False, split_next=True):
                st = Steps(dve, dve_steps, b * STEPS)
                moments(st, lambda j: y_bank[j][0:QT, :], y_full, b * 2)
                if split_next:
                    split(b + 1)
                dve.wait_ge(mv_ready, b * 2 + 1)
                for j in range(2):
                    dve.scalar_tensor_tensor(out=normed[:, j, :], in0=y_bank[j][0:QT, :], scalar=mv[:, j, 0:1],
                                             in1=scale_b[:], op0=ALU.subtract, op1=ALU.mult).then_inc(y_read, 1)
                dve.wait_ge(root_done, b * 4 + 2)
                dve.wait_ge(biased, b + 1)
                for j in range(2):
                    dve.wait_ge(y_read, b * 2 + j + 1)
                    dve.scalar_tensor_tensor(out=res[:, j, :], in0=normed[:, j, :], scalar=rs[:, j, 0:1],
                                             in1=x1[:, j, :], op0=ALU.mult, op1=ALU.add).then_inc(summed, 1)
                moments(st, lambda j: res[:, j, :], summed, b * 2)
                dve.wait_ge(root_done, b * 4 + 4)
                if not first:
                    dve.wait_ge(x2_stored, b * 16)
                    dve.wait_ge(t_full, b * 2)
                for j in range(2):
                    dve.tensor_scalar(x2[:, j, :], res[:, j, :], mv[:, j, 0:1], rs[:, j, 0:1],
                                      ALU.subtract, ALU.mult).then_inc(x2_ready, 1)
                assert st.n == STEPS

            def add_router_bias(b, first=False):
                dve.wait_ge(l_full, b + 1)
                if not first:
                    dve.wait_ge(l_stored, b * 16)
                dve.tensor_tensor(logits[:], l_bank[0:QT, 0:2 * E].rearrange("p (j e) -> p j e", j=2),
                                  br_b[:].rearrange("p (o e) -> p o e", o=1).broadcast_to([QT, 2, E]), ALU.add)\
                   .then_inc(l_read, 1)

            split(0)
            dve.wait_ge(consts_loaded, 64)
            norms(0, first=True)
            norms(1)
            add_router_bias(0, first=True)
            with dve.Fori(2, B - 1) as b:
                norms(b)
                add_router_bias(b - 1)
            norms(B - 1, split_next=False)
            add_router_bias(B - 2)
            add_router_bias(B - 1)

        @block.tensor
        def _(pe):
            def projection(b, first=False):
                pe.wait_ge(o_lo_done, b + 1)
                for j in range(2):
                    if not first:
                        pe.wait_ge(y_read, b * 2 - 1 + j)
                    for t in range(FT):
                        if first and j == 0 and t % 2 == 0:
                            pe.wait_ge(w_lo_done, t // 2 + 1)
                        last = matmul3(pe, y_bank[j][0:QT, :], o_hi[:, t, j * QT:(j + 1) * QT],
                                       o_lo[:, t, j * QT:(j + 1) * QT], w_hi[:, t, :], w_lo[:, t, :],
                                       t == 0, t == FT - 1)
                    last.then_inc(y_full, 1)

            def router(b, first=False):
                pe.wait_ge(x2_ready, b * 2 + 2)
                if not first:
                    pe.wait_ge(t_read, b * 2)
                for n in range(2):
                    for t in range(2):
                        for j in range(2):
                            c = (2 * n + t) * 128
                            last = pe.transpose(t_bank[n][:, t * S + j * QT:t * S + (j + 1) * QT],
                                                x2[:, j, c:c + 128], ident[0:QT, 0:QT])
                    last.then_inc(t_full, 1)
                pe.wait_ge(t_read, b * 2 + 2)
                if not first:
                    pe.wait_ge(l_read, b)
                for j in range(2):
                    for t in range(KD):
                        last = pe.matmul(l_bank[0:QT, j * E:(j + 1) * E], x2T[:, t, j * QT:(j + 1) * QT],
                                         wr_sb[:, t, :], start=(t == 0), stop=(t == KD - 1))
                last.then_inc(l_full, 1)

            pe.wait_ge(ident_done, 2)
            pe.wait_ge(consts_loaded, 64)
            projection(0, first=True)
            projection(1)
            router(0, first=True)
            with pe.Fori(2, B) as b:
                projection(b)
                router(b - 1)
            router(B - 1)


def routing(nc, logits_dram, x2_dram, slot_x_dram, slot_of_dram, weight_dram, expert_dram):
    N = TILES * E
    with ExitStack() as stack:
        m = Scope(nc, stack, "rt")
        lg = m.sb("lg", [QT, TILES, E])
        pr = m.sb("pr", [QT, TILES, E])
        cand = m.sb("cand", [QT, TILES, E])
        picked = [m.sb(f"picked{c}", [QT, TILES, E]) for c in range(TOP_K)]
        chosen = m.sb("chosen", [QT, TILES, E], BF16)
        red = m.sb("red", [QT, TILES, 8])
        iota_e = m.sb("iota_e", [128, E])
        iota_t = m.sb("iota_t", [128, SLOT_TILES])
        lower = m.sb("lower", [QT, 128], BF16)
        ones = m.sb("ones", [QT, 128], BF16)
        count = m.sb("count", [128, E])
        ntile, ntile_i = m.sb("ntile", [128, E]), m.sb("ntile_i", [128, E], I32)
        cum = [m.sb(f"cum{n}", [128, E]) for n in range(2)]
        first_slot = m.sb("first_slot", [128, E])
        at = m.sb("at", [QT, TILES, E])
        tmp = m.sb("tmp", [QT, TILES, E])
        slot_f = m.sb("slot_f", [QT, TOP_K, TILES])
        slot_i = m.sb("slot_i", [QT, TOP_K, TILES], I32)
        weight = m.sb("weight", [QT, TOP_K, TILES])
        cmp = m.sb("cmp", [128, SLOT_TILES, E])
        expert = m.sb("expert", [128, SLOT_TILES])
        expert_i = m.sb("expert_i", [128, SLOT_TILES], I32)
        x2 = m.sb("x2", [QT, TILES, D])
        rank_bank = m.bank("rank")

        loaded, x2_loaded, consts_done = m.sem("loaded"), m.sem("x2_loaded"), m.sem("consts_done")
        shifted, exp_done = m.sem("shifted"), m.sem("exp_done")
        chosen_ready, rank_ready = m.sem("chosen_ready"), m.sem("rank_ready")
        slots_ready, weights_ready, experts_ready = m.sem("slots_ready"), m.sem("weights_ready"), m.sem("experts_ready")
        stored, scattered = m.sem("stored"), m.sem("scattered")
        steps = m.sem("steps")
        block = stack.enter_context(nc.Block())

        @block.sync
        def _(sp):
            sp.dma_start(lg[:], logits_dram).then_inc(loaded, 16)
            sp.dma_start(x2[:], x2_dram.rearrange("b (j p) d -> p (b j) d", p=QT)).then_inc(x2_loaded, 16)
            sp.wait_ge(slots_ready, 1)
            sp.dma_start(slot_of_dram, slot_i[:]).then_inc(stored, 16)
            sp.wait_ge(weights_ready, 1)
            sp.dma_start(weight_dram, weight[:]).then_inc(stored, 16)
            sp.wait_ge(experts_ready, 1)
            sp.dma_start(expert_dram, expert_i[:]).then_inc(stored, 16)
            sp.wait_ge(stored, 48)

        @block.gpsimd
        def _(pool):
            pool.iota(iota_e[:], pattern=[[1, E]], base=0, channel_multiplier=0,
                      allow_small_or_imprecise_dtypes=True).then_inc(consts_done, 1)
            pool.iota(iota_t[:], pattern=[[1, SLOT_TILES]], base=0, channel_multiplier=0,
                      allow_small_or_imprecise_dtypes=True).then_inc(consts_done, 1)
            pool.memset(ones[:], 1.0).then_inc(consts_done, 1)
            pool.memset(lower[:], 1.0).then_inc(consts_done, 1)
            pool.wait_ge(consts_done, 4)
            pool.affine_select(out=lower[:], in_=lower[:], compare_op=ALU.is_gt, fill=0.0, base=0,
                               pattern=[[1, 128]], channel_multiplier=-1).then_inc(consts_done, 1)
            pool.wait_ge(slots_ready, 1)
            pool.wait_ge(x2_loaded, 16)
            for c in range(TOP_K):
                for t in range(TILES):
                    pool.indirect_dma_start(slot_x_dram, bass.IndirectOffsetOnAxis(ap=slot_i[:, c, t:t + 1].bitcast(U32), axis=0),
                                            x2[:, t, :], None).then_inc(scattered, 16)
            pool.wait_ge(scattered, 16 * TOP_K * TILES)

        @block.scalar
        def _(act):
            act.wait_ge(shifted, 1)
            act.activation(pr[:], lg[:], ACT.Exp).then_inc(exp_done, 1)

        @block.tensor
        def _(pe):
            pe.wait_ge(consts_done, 5)
            pe.wait_ge(chosen_ready, 1)
            rank = rank_bank[:, 0:(TILES + 1) * E].rearrange("p (t e) -> p t e", e=E)
            pe.matmul(rank_bank[:, 0:N], lower[:], chosen[:].rearrange("p t e -> p (t e)"), start=True, stop=False,
                      skip_group_check=True)
            for t in range(TILES):
                later = TILES - t
                last = pe.matmul(rank[:, t + 1:TILES + 1, :], ones[:],
                                 chosen[:, t:t + 1, :].broadcast_to([QT, later, E]), start=False,
                                 stop=(t == TILES - 1), skip_group_check=True)
            last.then_inc(rank_ready, 1)

        @block.vector
        def _(dve):
            st = Steps(dve, steps)
            per_e = lambda ap: ap.rearrange("p (o e) -> p o e", o=1).broadcast_to([QT, TILES, E])
            per_t = lambda ap: ap.broadcast_to([QT, TILES, E])
            dve.wait_ge(loaded, 16)
            dve.wait_ge(consts_done, 5)
            st.step(dve.tensor_reduce(red[:, :, 0], lg[:], AX, ALU.max))
            dve.tensor_tensor(lg[:], lg[:], per_t(red[:, :, 0:1]), ALU.subtract).then_inc(shifted, 1)
            dve.wait_ge(exp_done, 1)
            st.step(dve.tensor_reduce(red[:, :, 1], pr[:], AX, ALU.add))
            st.step(dve.reciprocal(red[:, :, 2], red[:, :, 1]))
            st.step(dve.tensor_tensor(pr[:], pr[:], per_t(red[:, :, 2:3]), ALU.mult))
            for c in range(TOP_K):
                st.step(dve.tensor_reduce(red[:, :, 3 + c], pr[:], AX, ALU.max))
                st.step(dve.tensor_tensor(cand[:], pr[:], per_t(red[:, :, 3 + c:4 + c]), ALU.is_equal))
                st.step(dve.scalar_tensor_tensor(out=cand[:], in0=cand[:], scalar=-float(E), in1=per_e(iota_e[0:QT]),
                                                 op0=ALU.mult, op1=ALU.add))
                st.step(dve.tensor_reduce(red[:, :, 5], cand[:], AX, ALU.min))
                st.step(dve.tensor_tensor(picked[c][:], cand[:], per_t(red[:, :, 5:6]), ALU.is_equal))
                if c == 0:
                    st.step(dve.scalar_tensor_tensor(out=pr[:], in0=picked[0][:], scalar=-2.0, in1=pr[:],
                                                     op0=ALU.mult, op1=ALU.add))
            dve.tensor_tensor(chosen[:], picked[0][:], picked[1][:], ALU.add).then_inc(chosen_ready, 1)
            st.step(dve.tensor_tensor(red[:, :, 6], red[:, :, 3], red[:, :, 4], ALU.add))
            st.step(dve.tensor_scalar(red[:, :, 6], red[:, :, 6], 1e-9, None, ALU.max))
            st.step(dve.reciprocal(red[:, :, 7], red[:, :, 6]))
            for c in range(TOP_K):
                ins = dve.tensor_tensor(weight[:, c, :], red[:, :, 3 + c], red[:, :, 7], ALU.mult)
                if c == 0:
                    st.step(ins)
            ins.then_inc(weights_ready, 1)
            dve.wait_ge(rank_ready, 1)
            st.step(dve.tensor_copy(count[:], rank_bank[:, N:N + E]))
            st.step(dve.tensor_scalar(count[:], count[:], 1.0 / SLOT, (SLOT - 1) / SLOT - (SLOT - 1) / (2 * SLOT),
                                      ALU.mult, ALU.add))
            st.step(dve.tensor_copy(ntile_i[:], count[:]))
            st.step(dve.tensor_copy(ntile[:], ntile_i[:]))
            st.step(dve.tensor_copy(cum[0][:], ntile[:]))
            for n, d in enumerate((1, 2, 4, 8)):
                a, z = cum[n % 2], cum[(n + 1) % 2]
                st.step(dve.tensor_copy(z[:, 0:d], a[:, 0:d]))
                st.step(dve.tensor_tensor(z[:, d:E], a[:, d:E], a[:, 0:E - d], ALU.add))
            total = cum[0]
            st.step(dve.tensor_tensor(first_slot[:], total[:], ntile[:], ALU.subtract))
            st.step(dve.tensor_scalar(first_slot[:], first_slot[:], float(SLOT), None, ALU.mult))
            st.step(dve.tensor_tensor(at[:], rank_bank[0:QT, 0:N].rearrange("p (t e) -> p t e", e=E),
                                      per_e(first_slot[0:QT]), ALU.add))
            for c in range(TOP_K):
                st.step(dve.tensor_tensor(tmp[:], at[:], picked[c][:], ALU.mult))
                st.step(dve.tensor_reduce(slot_f[:, c, :], tmp[:], AX, ALU.add))
            dve.tensor_copy(slot_i[:], slot_f[:]).then_inc(slots_ready, 1)
            st.step(dve.tensor_tensor(cmp[:], iota_t[:].rearrange("p (t o) -> p t o", o=1).broadcast_to([128, SLOT_TILES, E]),
                                      total[:].rearrange("p (o e) -> p o e", o=1).broadcast_to([128, SLOT_TILES, E]),
                                      ALU.is_ge))
            st.step(dve.tensor_reduce(expert[:], cmp[:], AX, ALU.add))
            st.step(dve.tensor_scalar(expert[:], expert[:], float(E - 1), None, ALU.min))
            dve.tensor_copy(expert_i[:], expert[:]).then_inc(experts_ready, 1)


def experts(nc, slot_x_dram, expert_dram, w1, b1, ffn_gb, w2, b2, slot_y_dram):
    N = SLOT_TILES
    W2_POOL = 2
    with ExitStack() as stack:
        m = Scope(nc, stack, "ex")
        ident = m.sb("ident", [128, 128])
        two = lambda name, shape, dt=F32: [m.sb(f"{name}{n}", shape, dt) for n in range(2)]
        w1_raw, w1_hi, w1_lo = two("w1_raw", [128, KD, HID]), two("w1_hi", [128, KD, HID], F32R), two("w1_lo", [128, KD, HID], F32R)
        w2_raw, w2_hi, w2_lo = two("w2_raw", [128, KD, D]), two("w2_hi", [128, KD, D], F32R), two("w2_lo", [128, KD, D], F32R)
        gb = two("gb", [128, 2, KD])
        x = two("x", [128, D])
        xT_hi, xT_lo = two("xT_hi", [128, KD, SLOT], F32R), two("xT_lo", [128, KD, SLOT], F32R)
        normed = two("normed", [128, HID])
        g = two("g", [128, KD, SLOT])
        g_hi, g_lo = two("g_hi", [128, KD, SLOT], F32R), two("g_lo", [128, KD, SLOT], F32R)
        y = two("y", [128, D])
        bias_raw = m.sb("bias_raw", [64, 2, D])
        bias = m.sb("bias", [128, 2, D], F32R)
        row_expert = m.sb("row_expert", [128, SLOT])
        pick1, pick2 = two("pick1", [128, SLOT], F32R), two("pick2", [128, SLOT], F32R)
        expert_i = m.sb("expert_i", [128, N], I32)
        expert_f = m.sb("expert_f", [128, N])
        changed = m.sb("changed", [128, N], I32)
        minus_half = m.sb("minus_half", [128, 1])
        bn, mv, rs = m.sb("bn", [128, 6]), m.sb("mv", [128, 2]), two("rs", [128, 2])
        x_bank, g_bank = m.bank("xT"), m.bank("gT")
        h_bank = [m.bank(f"h{n}") for n in range(2)]
        y_bank = [m.bank(f"y_bank{n}") for n in range(2)]

        def sems(name):
            return [m.sem(f"{name}{n}") for n in range(2)]

        ident_done, setup_loaded, setup = m.sem("ident_done"), m.sem("setup_loaded"), m.sem("setup")
        setup_pool, zeroed = m.sem("setup_pool"), m.sem("zeroed")
        w1_loaded, w2_loaded, gb_loaded, x_loaded = sems("w1_loaded"), sems("w2_loaded"), sems("gb_loaded"), sems("x_loaded")
        w1_hi_done, w1_done = m.sem("w1_hi_done"), m.sem("w1_done")
        w2_hi_done, w2_done, w2_pool_done = m.sem("w2_hi_done"), m.sem("w2_done"), m.sem("w2_pool_done")
        xT_full, xT_hi_done, xT_done = m.sem("xT_full"), m.sem("xT_hi_done"), m.sem("xT_done")
        h_full, norm_ready, normed_ready = m.sem("h_full"), m.sem("norm_ready"), m.sem("normed_ready")
        g_full, gelu_done, g_hi_done, g_done = m.sem("g_full"), m.sem("gelu_done"), m.sem("g_hi_done"), m.sem("g_done")
        pick1_done, pick2_done = m.sem("pick1_done"), m.sem("pick2_done")
        y_full, y_ready, y_stored = m.sem("y_full"), m.sem("y_ready"), sems("y_stored")
        dve_steps, dve_waits_alone, waits_alone = m.sem("dve_steps"), m.sem("dve_waits_alone"), m.sem("waits_alone")
        mv_ready, root_done = m.sem("mv_ready"), m.sem("root_done")
        block = stack.enter_context(nc.Block())

        def steps(eng, body, ahead=0, behind=0):
            low, high = 4, (N - ahead) // 2 * 2
            for i in range(-ahead, low):
                body(i // 2, i % 2)
            with eng.Fori(low // 2, high // 2) as u:
                body(u, 0)
                body(u, 1)
            for i in range(high, N + behind):
                body(i // 2, i % 2)

        def tile(u, p, d=0):
            return u + (p + d) // 2 + (N + 1) // 2 * ((p + d) % 2)

        def loads(u, p, d=0):
            return (u + (p + d) // 2 + 1) * 16

        def real(i):
            return not isinstance(i, int) or 0 <= i < N

        def known_below(i, n):
            return isinstance(i, int) and i < n

        SETUP = 7

        @block.sync
        def _(sp):
            sp.dma_start(expert_i[:], expert_dram).then_inc(setup_loaded, 16)
            sp.wait_ge(zeroed, 1)
            for n, b in enumerate((b1, b2)):
                for r in range(2):
                    sp.dma_start(bias_raw[32 * r:32 * r + E, n, :], b).then_inc(setup_loaded, 16)
            sp.wait_ge(setup, SETUP)

            def load_x(u, p, d):
                i, q = 2 * u + p + d, (p + d) % 2
                if not known_below(i, 2):
                    sp.wait_ge(xT_full, i - 1)
                sp.dma_start(x[q][:], slot_x_dram[bass.ds(tile(u, p, d) * SLOT, SLOT), :]).then_inc(x_loaded[q], 16)

            def load_weight(u, p, d, w, raw, split, loaded):
                i, q, at = 2 * u + p + d, (p + d) % 2, tile(u, p, d)
                e = sp.value_load(expert_i[0:1, bass.ds(at, 1)], min_val=0, max_val=E - 1)
                new = dict()
                if not known_below(i, 2):
                    new = dict(cond=sp.value_load(changed[0:1, bass.ds(at, 1)], min_val=0, max_val=1))
                    for sem in split:
                        sp.wait_ge(sem, i - 1)
                sp.dma_start(raw[q][:], w[bass.ds(e, 1)].rearrange("o (t p) n -> p (o t) n", p=128), **new)\
                    .then_inc(loaded[q], 16)
                return e

            def body(u, p):
                i, q = 2 * u + p, 1 - p
                if real(i + 1):
                    load_x(u, p, 1)
                if real(i):
                    load_weight(u, p, 0, w1, w1_raw, [w1_done], w1_loaded)
                if real(i - 1):
                    e = load_weight(u, p, -1, w2, w2_raw, [w2_done, w2_pool_done], w2_loaded)
                    if not known_below(i, 3):
                        sp.wait_ge(gelu_done, i - 2)
                    sp.dma_start(gb[q][:], ffn_gb[bass.ds(e, 1)].rearrange("o p i t -> p (o i) t")).then_inc(gb_loaded[q], 16)

            steps(sp, body, 1, 1)
            for p in range(2):
                sp.wait_ge(y_stored[p], 16 * ((N + 1 - p) // 2))

        @block.gpsimd
        def _(pool):
            pool.memset(bias_raw[:], 0.0).then_inc(zeroed, 1)
            make_identity(pool, ident[:], ident_done)
            pool.iota(row_expert[:], pattern=[[0, SLOT]], base=0, channel_multiplier=1,
                      allow_small_or_imprecise_dtypes=True).then_inc(setup_pool, 1)

            pool.memset(minus_half[:], -0.5).then_inc(ident_done, 1)
            pool.wait_ge(ident_done, 3)

            def body(u, p):
                i, q = 2 * u + p, 1 - p
                j = i - 1
                if real(j):
                    pool.wait_ge(w2_loaded[q], loads(u, p, -1))
                    if not known_below(j, 2):
                        pool.wait_ge(y_full, j - 1)
                    own_instruction(pool, waits_alone)
                    pool_round(pool, w2_hi[q][:], w2_raw[q][:]).then_inc(w2_hi_done, 1)
                    pool.wait_ge(w2_hi_done, j + 1)
                    own_instruction(pool, waits_alone)
                    pool.tensor_tensor(w2_lo[q][:, 0:W2_POOL], w2_raw[q][:, 0:W2_POOL], as_f32(w2_hi[q][:, 0:W2_POOL]),
                                       ALU.subtract).then_inc(w2_pool_done, 1)
                if real(i):
                    pool.wait_ge(mv_ready, i + 1)
                    pool_inverse_root(pool, rs[p][:, 0:1], mv[:, 1:2], minus_half[:], LN_EPS, root_done, i * 2, waits_alone)
                    pool.wait_ge(root_done, i * 2 + 2)
                    own_instruction(pool, waits_alone)
                    pool.tensor_scalar(rs[p][:, 1:2], mv[:, 0:1], rs[p][:, 0:1], -1.0, ALU.mult, ALU.mult)\
                        .then_inc(norm_ready, 1)
                if real(j):
                    pool.wait_ge(gelu_done, j + 1)
                    own_instruction(pool, waits_alone)
                    pool_round(pool, g_hi[q][:], g[q][:]).then_inc(g_hi_done, 1)

            steps(pool, body, 0, 1)

        @block.scalar
        def _(act):
            def body(u, p):
                i, q = 2 * u + p, 1 - p
                j = i - 1
                if real(j):
                    act.wait_ge(norm_ready, j + 1)
                    act.activation(normed[q][:], h_bank[q][:, :], ACT.Identity, bias=rs[q][:, 1:2], scale=rs[q][:, 0:1])\
                        .then_inc(normed_ready, 1)
                if real(i + 1):
                    act.wait_ge(xT_full, i + 2)
                    act.copy(xT_hi[q][:].rearrange("p t s -> p (t s)"), x_bank[:, :]).then_inc(xT_hi_done, 1)
                    act.wait_ge(w1_loaded[q], loads(u, p, 1))
                    if not known_below(i, 1):
                        act.wait_ge(h_full, i)
                    act.copy(w1_hi[q][:], w1_raw[q][:]).then_inc(w1_hi_done, 1)
                if real(j):
                    act.wait_ge(g_full, j + 1)
                    act.wait_ge(gb_loaded[q], loads(u, p, -1))
                    for t in range(KD):
                        last = act.activation(g[q][:, t, :], g_bank[:, t * SLOT:(t + 1) * SLOT], ACT.Gelu,
                                              bias=gb[q][:, 1, t:t + 1], scale=gb[q][:, 0, t:t + 1])
                    last.then_inc(gelu_done, 1)
                if real(i - 2):
                    act.wait_ge(y_full, i - 1)
                    if not known_below(i, 4):
                        act.wait_ge(y_stored[p], loads(u, p, -4))
                    act.copy(y[p][:], y_bank[p][:, :]).then_inc(y_ready, 1)
                    act.wait_ge(y_ready, i - 1)
                    act.dma_start(slot_y_dram[bass.ds(tile(u, p, -2) * SLOT, SLOT), :], y[p][:]).then_inc(y_stored[p], 16)

            steps(act, body, 1, 2)

        @block.vector
        def _(dve):
            st = Steps(dve, setup)
            dve.wait_ge(setup_pool, 1)
            st.step(dve.tensor_scalar(row_expert[32:64], row_expert[32:64], -32.0, None, ALU.add))
            st.step(dve.memset(row_expert[64:128], -1.0))
            dve.wait_ge(setup_loaded, 80)
            st.step(dve.tensor_copy(expert_f[:], expert_i[:]))
            st.step(dve.tensor_tensor(changed[:, 1:], expert_f[:, 1:], expert_f[:, 0:N - 1], ALU.not_equal))
            st.step(dve.memset(as_f32(bias[64:128]), 0.0))
            st.step(dve.tensor_copy(bias[0:64], bias_raw[:]))
            st.step(dve.tensor_tensor(bias[32:64], bias_raw[32:64], as_f32(bias[32:64]), ALU.subtract))
            assert st.n == SETUP

            def pick(at, out, done):
                dve.tensor_scalar(out, row_expert[:], expert_f[:, bass.ds(at, 1)], None, ALU.is_equal).then_inc(done, 1)

            def body(u, p):
                i, q = 2 * u + p, 1 - p
                j = i - 1
                if real(i + 1):
                    if not known_below(i, 1):
                        dve.wait_ge(h_full, i)
                    pick(tile(u, p, 1), pick1[q][:], pick1_done)
                    dve.wait_ge(xT_hi_done, i + 2)
                    dve.tensor_tensor(xT_lo[q][:].rearrange("p t s -> p (t s)"), x_bank[:, :],
                                      as_f32(xT_hi[q][:]).rearrange("p t s -> p (t s)"), ALU.subtract).then_inc(xT_done, 1)
                    dve.wait_ge(w1_hi_done, i + 2)
                    dve.tensor_tensor(w1_lo[q][:], w1_raw[q][:], as_f32(w1_hi[q][:]), ALU.subtract).then_inc(w1_done, 1)
                if real(i):
                    dve.wait_ge(h_full, i + 1)
                    dve.bn_stats(bn[:], h_bank[p][:, :]).then_inc(dve_steps, 1)
                    dve.wait_ge(dve_steps, i + 1)
                    if not known_below(i, 1):
                        dve.wait_ge(norm_ready, i)
                    own_instruction(dve, dve_waits_alone)
                    dve.bn_aggr(mv[:], bn[:]).then_inc(mv_ready, 1)
                if real(j):
                    dve.wait_ge(w2_hi_done, j + 1)
                    dve.tensor_tensor(w2_lo[q][:, W2_POOL:], w2_raw[q][:, W2_POOL:], as_f32(w2_hi[q][:, W2_POOL:]),
                                      ALU.subtract).then_inc(w2_done, 1)
                    pick(tile(u, p, -1), pick2[q][:], pick2_done)
                if real(j):
                    dve.wait_ge(g_hi_done, j + 1)
                    dve.tensor_tensor(g_lo[q][:], g[q][:], as_f32(g_hi[q][:]), ALU.subtract).then_inc(g_done, 1)

            steps(dve, body, 1, 1)

        @block.tensor
        def _(pe):
            pe.wait_ge(ident_done, 2)
            pe.wait_ge(setup, SETUP)

            def layer(bank, pick, n, a_hi, a_lo, w_hi, w_lo):
                pe.matmul(bank[:, :], pick[:], bias[:, n, :], start=True, stop=False)
                for t in range(KD):
                    last = matmul3(pe, bank[:, :], a_hi[:, t, :], a_lo[:, t, :], w_hi[:, t, :], w_lo[:, t, :],
                                   False, t == KD - 1)
                return last

            def body(u, p):
                i, q = 2 * u + p, 1 - p
                j = i - 1
                if real(i + 1):
                    pe.wait_ge(x_loaded[q], loads(u, p, 1))
                    if not known_below(i, 0):
                        pe.wait_ge(xT_done, i + 1)
                    for t in range(KD):
                        last = pe.transpose(x_bank[:, t * SLOT:(t + 1) * SLOT], x[q][:, t * 128:(t + 1) * 128], ident[:])
                    last.then_inc(xT_full, 1)
                if real(i):
                    pe.wait_ge(xT_done, i + 1)
                    pe.wait_ge(w1_done, i + 1)
                    pe.wait_ge(pick1_done, i + 1)
                    if not known_below(i, 2):
                        pe.wait_ge(normed_ready, i - 1)
                    layer(h_bank[p], pick1[p], 0, xT_hi[p], xT_lo[p], w1_hi[p], w1_lo[p]).then_inc(h_full, 1)
                if real(j):
                    pe.wait_ge(normed_ready, j + 1)
                    if not known_below(j, 1):
                        pe.wait_ge(gelu_done, j)
                    for t in range(KD):
                        last = pe.transpose(g_bank[:, t * SLOT:(t + 1) * SLOT], normed[q][:, t * 128:(t + 1) * 128], ident[:])
                    last.then_inc(g_full, 1)
                if real(i - 2):
                    pe.wait_ge(g_done, i - 1)
                    pe.wait_ge(w2_done, i - 1)
                    pe.wait_ge(w2_pool_done, i - 1)
                    pe.wait_ge(pick2_done, i - 1)
                    if not known_below(i, 4):
                        pe.wait_ge(y_ready, i - 3)
                    layer(y_bank[p], pick2[p], 1, g_hi[p], g_lo[p], w2_hi[p], w2_lo[p]).then_inc(y_full, 1)

            steps(pe, body, 1, 2)


def combine(nc, slot_y_dram, slot_of_dram, weight_dram, x2_dram, out):
    G = 2
    NG = TILES // G
    with ExitStack() as stack:
        m = Scope(nc, stack, "cb")
        slot_i = m.sb("slot_i", [QT, TOP_K, TILES], I32)
        weight = m.sb("weight", [QT, TOP_K, TILES])
        x2 = m.sb("x2", [QT, TILES, D])
        y = m.sb("y", [QT, TOP_K, TILES, D])
        res = m.sb("res", [QT, TILES, D])
        bn, mv, rs = m.sb("bn", [QT, G, 6]), m.sb("mv", [QT, G, 2]), m.sb("rs", [QT, G, 2])
        x2_loaded, weight_loaded, slot_loaded = m.sem("x2_loaded"), m.sem("weight_loaded"), m.sem("slot_loaded")
        gathered = [m.sem(f"gathered{g}") for g in range(NG)]
        steps, ready, stored = m.sem("steps"), m.sem("ready"), m.sem("stored")
        block = stack.enter_context(nc.Block())

        @block.gpsimd
        def _(pool):
            pool.dma_start(slot_i[:], slot_of_dram).then_inc(slot_loaded, 16)
            pool.wait_ge(slot_loaded, 16)
            for t in range(TILES):
                for c in range(TOP_K):
                    pool.indirect_dma_start(y[:, c, t, :], None, slot_y_dram,
                                            bass.IndirectOffsetOnAxis(ap=slot_i[:, c, t:t + 1].bitcast(U32), axis=0))\
                        .then_inc(gathered[t // G], 16)

        @block.sync
        def _(sp):
            sp.dma_start(x2[:], x2_dram.rearrange("b (j p) d -> p (b j) d", p=QT)).then_inc(x2_loaded, 16)
            sp.dma_start(weight[:], weight_dram).then_inc(weight_loaded, 16)
            for g in range(NG):
                sp.wait_ge(ready, g + 1)
                sp.dma_start(out[g * G // 2:(g + 1) * G // 2].rearrange("b (j p) d -> p (b j) d", p=QT),
                             res[:, g * G:(g + 1) * G, :]).then_inc(stored, 16)
            sp.wait_ge(stored, 16 * NG)

        @block.vector
        def _(dve):
            dve.wait_ge(x2_loaded, 16)
            dve.wait_ge(weight_loaded, 16)
            st = Steps(dve, steps)
            for g in range(NG):
                dve.wait_ge(gathered[g], 16 * TOP_K * G)
                for c in range(TOP_K):
                    for j in range(G):
                        t = g * G + j
                        ins = dve.scalar_tensor_tensor(out=res[:, t, :], in0=y[:, c, t, :], scalar=weight[:, c, t:t + 1],
                                                       in1=x2[:, t, :] if c == 0 else res[:, t, :],
                                                       op0=ALU.mult, op1=ALU.add)
                        if j < G - 1:
                            ins.then_inc(steps, 1)
                            st.n += 1
                    st.step(ins)
                for j in range(G):
                    st.step(dve.bn_stats(bn[:, j, :], res[:, g * G + j, :]))
                    st.step(dve.bn_aggr(mv[:, j, :], bn[:, j, :]))
                rsqrt_steps(st, rs[:, :, 0:1], mv[:, :, 1:2], rs[:, :, 1:2], LN_EPS)
                for j in range(G):
                    t = g * G + j
                    ins = dve.tensor_scalar(res[:, t, :], res[:, t, :], mv[:, j, 0:1], rs[:, j, 0:1],
                                            ALU.subtract, ALU.mult)
                    if j < G - 1:
                        st.step(ins)
                ins.then_inc(ready, 1)


def decoder_layer(nc, a, out):
    def scratch(name, shape, dt=F32):
        return nc.dram_tensor(name, shape, dt).ap()

    x1 = scratch("x1_scratch", (B, S, D))
    qT = scratch("qT_scratch", (B, INNER, S))
    oT = scratch("oT_scratch", (B, INNER, S))
    x2 = scratch("x2_scratch", (B, S, D))
    logits = scratch("logits_scratch", (QT, TILES, E))
    slot_of = scratch("slot_of_scratch", (QT, TOP_K, TILES), I32)
    weight = scratch("weight_scratch", (QT, TOP_K, TILES))
    expert = scratch("expert_scratch", (128, SLOT_TILES), I32)
    slot_x = scratch("slot_x_scratch", (SLOTS, D))
    slot_y = scratch("slot_y_scratch", (SLOTS, D))
    Scope.made = {}
    with ExitStack() as Scope.kept:
        blocks(nc, a, out, x1, qT, oT, x2, logits, slot_of, weight, expert, slot_x, slot_y)


def blocks(nc, a, out, x1, qT, oT, x2, logits, slot_of, weight, expert, slot_x, slot_y):
    self_attention(nc, a["xT"], a["x"], a["L0_attn_W_Q"], a["L0_attn_W_K"], a["L0_attn_W_V"], a["L0_xattn_Wq"],
                   x1, qT, slot_x)
    for half in range(2):
        cross_attention(nc, half, a["ctxT"], a["L0_xattn_Wkv"], a["L0_xattn_null_kv"], qT, oT)
    output_router(nc, oT, a["L0_xattn_Wout"], a["L0_xattn_ln_scale"], a["L0_xattn_ln_bias"], x1,
                  a["L0_ffn_Wr"], a["L0_ffn_br"], x2, logits)
    routing(nc, logits, x2, slot_x, slot_of, weight, expert)
    experts(nc, slot_x, expert, a["L0_ffn_W1"], a["L0_ffn_b1"], a["ffn_gb"], a["L0_ffn_W2"], a["L0_ffn_b2"], slot_y)
    combine(nc, slot_y, slot_of, weight, x2, out)


def kernel(**inputs):
    import numpy as _np
    import concourse.bacc as _bacc
    from concourse import mybir as _mybir
    from concourse.bass_utils import run_bass_kernel_spmd as _run

    a = {k: _np.ascontiguousarray(v) for k, v in inputs.items()}

    def features_first(t):
        b, s, d = t.shape
        return _np.ascontiguousarray(t.reshape(b, s, d // 128, 128).transpose(0, 3, 2, 1))

    a["xT"] = features_first(a["x"])
    a["ctxT"] = features_first(a.pop("ctx_2048"))
    gb = _np.stack([a.pop("L0_ffn_g1"), a.pop("L0_ffn_be1")], axis=1)
    a["ffn_gb"] = _np.ascontiguousarray(gb.reshape(E, 2, HID // 128, 128).transpose(0, 3, 1, 2))

    nc = _bacc.Bacc("TRN2", target_bir_lowering=False, num_devices=1)
    arrays = {f"in_{k}_dram": v for k, v in a.items()}
    aps = {k: nc.dram_tensor(f"in_{k}_dram", v.shape, _mybir.dt.from_np(v.dtype), kind="ExternalInput").ap()
           for k, v in a.items()}
    out = nc.dram_tensor("out_0_dram", (B, S, D), F32, kind="ExternalOutput").ap()
    decoder_layer(nc, aps, out)
    r = _run(nc, [arrays], core_ids=[0])
    return r.results[0]["out_0_dram"]
```

```python
from contextlib import ExitStack

import concourse.bass as bass
from concourse import mybir

F32 = mybir.dt.float32
F32R = mybir.dt.float32r
BF16 = mybir.dt.bfloat16
I32 = mybir.dt.int32
U32 = mybir.dt.uint32
ALU = mybir.AluOpType
ACT = mybir.ActivationFunctionType
AX = mybir.AxisListType.X

B, S, D = 8, 224, 512
CTX_LEN, CTX_D = 750, 1024
HEADS, DH = 16, 64
INNER = HEADS * DH
E, TOP_K, HID = 16, 2, 512
QT = S // 2
KD = D // 128
TOKENS = B * S
TILES = TOKENS // QT
SLOT = 128
SLOT_TILES = (TOKENS * TOP_K + E * (SLOT - 1)) // SLOT
SLOTS = SLOT_TILES * SLOT
LN_EPS, OUT_EPS = 1e-5, 1e-6
RSQRT_MAGIC = 1597463007.0
RING = 4


class Steps:

    def __init__(self, eng, sem, base=0):
        self.eng, self.sem, self.base, self.n = eng, sem, base, 0

    def step(self, instruction):
        self.n += 1
        instruction.then_inc(self.sem, 1)
        self.eng.wait_ge(self.sem, self.base + self.n)


def rsqrt_steps(st, y, v, t, eps):
    eng = st.eng
    st.step(eng.tensor_scalar(v, v, eps, None, ALU.add))
    st.step(eng.tensor_scalar(y.bitcast(I32), v.bitcast(I32), -0.5, RSQRT_MAGIC, ALU.mult, ALU.add))
    for _ in range(3):
        st.step(eng.tensor_tensor(t, y, y, ALU.mult))
        st.step(eng.tensor_tensor(t, t, v, ALU.mult))
        st.step(eng.tensor_scalar(t, t, -0.5, 1.5, ALU.mult, ALU.add))
        st.step(eng.tensor_tensor(y, y, t, ALU.mult))


RSQRT_STEPS = 14


def pool_round(pool, out, in_):
    return pool.tensor_scalar(out, in_, 1.0, 1.0, ALU.mult, ALU.mult)


def pool_inverse_root(pool, y, v, minus_half, eps, done, count, alone):
    own_instruction(pool, alone)
    pool.tensor_scalar(v, v, eps, 1.0, ALU.add, ALU.mult).then_inc(done, 1)
    pool.wait_ge(done, count + 1)
    pool.tensor_tensor(y, v, minus_half, ALU.pow).then_inc(done, 1)


def matmul3(pe, out, stat_hi, stat_lo, mov_hi, mov_lo, first, last):
    pe.matmul(out, stat_hi, mov_hi, start=first, stop=False)
    pe.matmul(out, stat_hi, mov_lo, start=False, stop=False)
    return pe.matmul(out, stat_lo, mov_hi, start=False, stop=last)


def own_instruction(eng, counter):
    eng.sem_inc(counter, 1)


def make_identity(pool, ident, done):
    pool.memset(ident, 0.0).then_inc(done, 1)
    pool.wait_ge(done, 1)
    pool.affine_select(out=ident, in_=ident, compare_op=ALU.not_equal, fill=1.0, base=0,
                       pattern=[[-1, ident.shape[1]]], channel_multiplier=1).then_inc(done, 1)


def as_f32(ap):
    return ap.bitcast(F32)


class Scope:

    kept = None
    made = {}
    free = []

    def __init__(self, nc, stack, tag, phase=None):
        self.nc, self.stack, self.tag, self.phase = nc, stack, tag, phase or tag

    def sb(self, name, shape, dt=F32):
        return self.stack.enter_context(self.nc.sbuf_tensor(f"{self.tag}_{name}", shape, dt))

    def sb_under(self, name, shape, dt=F32):
        with self.nc.sbuf_tensor(f"{self.tag}_{name}", shape, dt) as memory:
            return memory

    def bank(self, name, shape=(128, 512), dt=F32):
        return self.stack.enter_context(self.nc.psum_tensor(f"{self.tag}_{name}", list(shape), dt))

    def sem(self, name):
        if Scope.kept is None:
            return self.stack.enter_context(self.nc.semaphore(f"{self.tag}_{name}"))
        if (self.phase, name) not in Scope.made:
            Scope.made[self.phase, name] = Scope.free.pop() if Scope.free else \
                Scope.kept.enter_context(self.nc.semaphore(f"{self.phase}_{name}"))
        return Scope.made[self.phase, name]

    def clear(self, over):
        with self.nc.Block() as block:
            @block.sync
            def _(sp):
                for (phase, _), sem in Scope.made.items():
                    if phase in (self.phase, over):
                        sp.sem_clear(sem)
        for key in [key for key in Scope.made if key[0] == over]:
            Scope.free.append(Scope.made.pop(key))


def self_attention(nc, xT, x, wq, wk, wv, wxq, x1_dram, qT_dram, slot_x_dram):
    SCALE = float(D) ** -0.5
    NW = 5
    with ExitStack() as stack:
        m = Scope(nc, stack, "sa")
        ident = m.sb("ident", [128, 128])
        w_raw = m.sb("w_raw", [128, 2, KD, 512])
        w_hi = m.sb("w_hi", [128, NW, KD, 512], F32R)
        w_lo = m.sb("w_lo", [128, NW, KD, 512], F32R)
        xT_raw = m.sb("xT_raw", [128, KD, S])
        xT_hi = m.sb("xT_hi", [128, KD, S], F32R)
        xT_lo = m.sb("xT_lo", [128, KD, S], F32R)
        x_tok = m.sb("x_tok", [QT, 2, D])
        qk_hi = m.sb("qk_hi", [128, 2, KD, S], F32R)
        qk_lo = m.sb("qk_lo", [128, 2, KD, S], F32R)
        v_hi = m.sb("v_hi", [QT, 2, D], F32R)
        v_lo = m.sb("v_lo", [QT, 2, D], F32R)
        probs = m.sb("probs", [QT, 2, S])
        pT_hi = m.sb("pT_hi", [QT, 2, S], F32R)
        pT_lo = m.sb("pT_lo", [QT, 2, S], F32R)
        stat = m.sb("stat", [QT, 2, 4])
        mv = m.sb("mv", [QT, 2, 2])
        bn = m.sb("bn", [QT, 2, 6])
        rs = m.sb("rs", [QT, 2, 1])
        minus_half = m.sb("minus_half", [QT, 2, 1])
        res = m.sb("res", [QT, 2, D])
        x1 = m.sb("x1", [QT, 2, D])
        x1T_hi = m.sb("x1T_hi", [128, KD, S], F32R)
        x1T_lo = m.sb("x1T_lo", [128, KD, S], F32R)
        xq = m.sb("xq", [128, INNER // 128, S])
        zeros = m.sb("zeros", [128, SLOTS * D // (B * 128)])
        ring = [m.bank(f"ring{n}") for n in range(RING)]
        s_bank, pT_bank = m.bank("scores"), m.bank("pT")
        o_bank = [m.bank(f"o{n}") for n in range(2)]

        ident_done = m.sem("ident_done")
        w_loaded = [m.sem(f"w_loaded{n}") for n in range(2)]
        w_hi_done, w_lo_done = m.sem("w_hi_done"), m.sem("w_lo_done")
        xT_loaded, xT_hi_done, xT_lo_done = m.sem("xT_loaded"), m.sem("xT_hi_done"), m.sem("xT_lo_done")
        x_loaded = m.sem("x_loaded")
        ring_full, ring_hi, ring_out = m.sem("ring_full"), m.sem("ring_hi"), m.sem("ring_out")
        scores_ready, max_ready, exp_done = m.sem("scores_ready"), m.sem("max_ready"), m.sem("exp_done")
        pT_full, pT_hi_done, pT_done = m.sem("pT_full"), m.sem("pT_hi_done"), m.sem("pT_done")
        o_full, o_read = m.sem("o_full"), m.sem("o_read")
        zeros_ready, slots_zeroed = m.sem("zeros_ready"), m.sem("slots_zeroed")
        x1_ready, x1_stored, xq_stored = m.sem("x1_ready"), m.sem("x1_stored"), m.sem("xq_stored")
        mv_ready, root_done = m.sem("mv_ready"), m.sem("root_done")
        dve_steps = m.sem("dve_steps")
        waits_alone, dve_waits_alone = m.sem("waits_alone"), m.sem("dve_waits_alone")

        def qkv_job(b):
            return 0 if isinstance(b, int) and b == 0 else b * 12 - 6

        def next_job(b):
            return 12 * B - 6 if isinstance(b, int) and b == B - 1 else (b + 1) * 12

        QKV_BANK0, NEXT_BANK0 = 2, 0

        def bank_of(first, b, n):
            if first is qkv_job:
                return ring[((0 if isinstance(b, int) and b == 0 else QKV_BANK0) + n) % RING]
            return ring[((next_job(b) if isinstance(b, int) else NEXT_BANK0) + n) % RING]

        w_dram = [wq, wk, wv, wxq[:, 0:512], wxq[:, 512:1024]]
        STEPS = 1 + 1 + 3

        block = stack.enter_context(nc.Block())

        def batches(eng, body):
            body(0)
            with eng.Fori(1, B - 2) as b:
                body(b)
            body(B - 2)
            body(B - 1)

        def is_int(b, *values):
            return isinstance(b, int) and b in values

        @block.sync
        def _(sp):
            sp.dma_start(xT_raw[:], xT[0]).then_inc(xT_loaded, 16)
            for n in range(NW):
                if n >= 2:
                    sp.wait_ge(w_lo_done, n - 1)
                sp.dma_start(w_raw[:, n % 2], w_dram[n].rearrange("(t p) n -> p t n", p=128))\
                    .then_inc(w_loaded[n % 2], 16)
            sp.dma_start(x_tok[:], x[0].rearrange("(j p) d -> p j d", p=QT)).then_inc(x_loaded, 16)
            sp.wait_ge(xT_lo_done, 1)
            sp.dma_start(xT_raw[:], xT[1]).then_inc(xT_loaded, 16)

            def store_queries(b):
                sp.wait_ge(ring_out, next_job(b) + 6 + RING)
                sp.dma_start(qT_dram[bass.ds(b, 1)].rearrange("o (t p) s -> p (o t) s", p=128), xq[:])\
                    .then_inc(xq_stored, 16)

            def body(b):
                if not is_int(b, B - 2, B - 1):
                    sp.wait_ge(xT_lo_done, b + 2)
                    sp.dma_start(xT_raw[:], xT[bass.ds(b + 2, 1)].rearrange("o p t s -> p (o t) s"))\
                        .then_inc(xT_loaded, 16)
                if not is_int(b, 0):
                    store_queries(b - 1)
                sp.wait_ge(x1_ready, b * 2 + 2)
                sp.dma_start(x1_dram[bass.ds(b, 1)].rearrange("o (j p) d -> p (o j) d", p=QT), x1[:])\
                    .then_inc(x1_stored, 16)
                if not is_int(b, B - 1):
                    sp.dma_start(x_tok[:], x[bass.ds(b + 1, 1)].rearrange("o (j p) d -> p (o j) d", p=QT))\
                        .then_inc(x_loaded, 16)

            batches(sp, body)
            store_queries(B - 1)
            sp.wait_ge(x1_stored, 16 * B)
            sp.wait_ge(xq_stored, 16 * B)

        @block.gpsimd
        def _(pool):
            def split_x(b):
                if not is_int(b, 0):
                    pool.wait_ge(ring_full, qkv_job(b - 1) + 6)
                pool.wait_ge(xT_loaded, (b + 1) * 16)
                own_instruction(pool, waits_alone)
                pool_round(pool, xT_hi[:], xT_raw[:]).then_inc(xT_hi_done, 1)

            split_x(0)
            pool.memset(zeros[:], 0.0).then_inc(zeros_ready, 1)
            make_identity(pool, ident[:], ident_done)
            pool.memset(minus_half[:], -0.5).then_inc(ident_done, 1)
            pool.wait_ge(ident_done, 3)

            def root(b):
                pool.wait_ge(mv_ready, b + 1)
                pool_inverse_root(pool, rs[:], mv[:, :, 1:2], minus_half[:], LN_EPS, root_done, b * 2, waits_alone)

            split_x(1)
            root(0)
            split_x(2)
            with pool.Fori(1, B - 2) as b:
                root(b)
                split_x(b + 2)
            root(B - 2)
            root(B - 1)

        @block.scalar
        def _(act):
            slots = slot_x_dram.rearrange("r d -> (r d)").rearrange("(b p k) -> b p k", b=B, p=128)

            def zero_slots(b):
                act.dma_start(slots[bass.ds(b, 1)].rearrange("o p k -> p (o k)"), zeros[:]).then_inc(slots_zeroed, 16)

            for n in range(NW):
                act.wait_ge(w_loaded[n % 2], 16 * (n // 2 + 1))
                act.copy(w_hi[:, n], w_raw[:, n % 2]).then_inc(w_hi_done, 1)

            def hi(job, bank, out):
                act.wait_ge(ring_full, job + 1)
                act.copy(out, bank).then_inc(ring_hi, 1)

            def qkv_hi(b):
                job = qkv_job(b)
                for n in range(4):
                    bank = bank_of(qkv_job, b, n)[:, 0:2 * S].rearrange("p (f s) -> p f s", f=2)
                    hi(job + n, bank, qk_hi[:, n // 2, 2 * (n % 2):2 * (n % 2) + 2, :])
                for j in range(2):
                    hi(job + 4 + j, bank_of(qkv_job, b, 4 + j)[0:QT, :], v_hi[:, j, :])

            def x1T_split(b):
                for n in range(2):
                    bank = bank_of(next_job, b, n)[:, 0:2 * S].rearrange("p (t s) -> p t s", t=2)
                    hi(next_job(b) + n, bank, x1T_hi[:, 2 * n:2 * n + 2, :])

            def body(b):
                act.wait_ge(max_ready, b + 1)
                for j in range(2):
                    act.activation(probs[:, j, :], s_bank[0:QT, j * S:(j + 1) * S], ACT.Exp,
                                   bias=stat[:, j, 1:2], scale=SCALE, accum_out=stat[:, j, 2:3])\
                        .then_inc(exp_done, 1)
                if not is_int(b, 0):
                    x1T_split(b - 1)
                act.wait_ge(pT_full, b + 1)
                act.copy(pT_hi[:].rearrange("p t s -> p (t s)"), pT_bank[0:QT, 0:2 * S]).then_inc(pT_hi_done, 1)
                zero_slots(b)
                if not is_int(b, B - 1):
                    qkv_hi(b + 1)

            qkv_hi(0)
            act.wait_ge(zeros_ready, 1)
            batches(act, body)
            x1T_split(B - 1)
            act.wait_ge(slots_zeroed, 16 * B)

        @block.vector
        def _(dve):
            dve.sem_inc(ring_out, RING)
            for n in range(NW):
                if n == 1:
                    dve.wait_ge(xT_hi_done, 1)
                    dve.tensor_tensor(xT_lo[:], xT_raw[:], as_f32(xT_hi[:]), ALU.subtract).then_inc(xT_lo_done, 1)
                dve.wait_ge(w_hi_done, n + 1)
                dve.tensor_tensor(w_lo[:, n], w_raw[:, n % 2], as_f32(w_hi[:, n]), ALU.subtract)\
                    .then_inc(w_lo_done, 1)

            def lo(hi_count, bank, hi, out):
                dve.wait_ge(ring_hi, hi_count + 1)
                dve.tensor_tensor(out, bank, as_f32(hi), ALU.subtract).then_inc(ring_out, 1)

            def qkv_count(b):
                return 0 if is_int(b, 0) else b * 8 - 2

            def x1T_count(b):
                return B * 8 - 2 if is_int(b, B - 1) else b * 8 + 12

            def qkv_lo(b):
                for n in range(4):
                    bank = bank_of(qkv_job, b, n)[:, 0:2 * S].rearrange("p (f s) -> p f s", f=2)
                    part = (slice(None), n // 2, slice(2 * (n % 2), 2 * (n % 2) + 2), slice(None))
                    lo(qkv_count(b) + n, bank, qk_hi[part], qk_lo[part])
                for j in range(2):
                    lo(qkv_count(b) + 4 + j, bank_of(qkv_job, b, 4 + j)[0:QT, :], v_hi[:, j, :], v_lo[:, j, :])

            def next_batch(b):
                for n in range(2):
                    bank = bank_of(next_job, b, n)[:, 0:2 * S].rearrange("p (t s) -> p t s", t=2)
                    lo(x1T_count(b) + n, bank, x1T_hi[:, 2 * n:2 * n + 2, :], x1T_lo[:, 2 * n:2 * n + 2, :])
                if not is_int(b, 0):
                    dve.wait_ge(xq_stored, b * 16)
                for n in range(4):
                    dve.wait_ge(ring_full, next_job(b) + 2 + n + 1)
                    dve.tensor_copy(xq[:, 2 * n:2 * n + 2, :].rearrange("p t s -> p (t s)"),
                                    bank_of(next_job, b, 2 + n)[:, 0:2 * S]).then_inc(ring_out, 1)

            def split_x(b):
                dve.wait_ge(xT_hi_done, b + 1)
                dve.tensor_tensor(xT_lo[:], xT_raw[:], as_f32(xT_hi[:]), ALU.subtract).then_inc(xT_lo_done, 1)

            def body(b):
                st = Steps(dve, dve_steps, b * STEPS)
                dve.wait_ge(scores_ready, b + 1)
                st.step(dve.tensor_reduce(stat[:, :, 0], s_bank[0:QT, 0:2 * S].rearrange("p (j s) -> p j s", j=2),
                                          AX, ALU.max))
                dve.tensor_scalar(stat[:, :, 1], stat[:, :, 0], -SCALE, None, ALU.mult).then_inc(max_ready, 1)
                if not is_int(b, 0):
                    next_batch(b - 1)
                dve.wait_ge(exp_done, b * 2 + 2)
                st.step(dve.reciprocal(stat[:, :, 3:4], stat[:, :, 2:3]))
                dve.wait_ge(pT_hi_done, b + 1)
                dve.tensor_tensor(pT_lo[:].rearrange("p t s -> p (t s)"), pT_bank[0:QT, 0:2 * S],
                                  as_f32(pT_hi[:]).rearrange("p t s -> p (t s)"), ALU.subtract).then_inc(pT_done, 1)
                dve.wait_ge(x_loaded, b * 16 + 16)
                for j in range(2):
                    dve.wait_ge(o_full, b * 2 + j + 1)
                    dve.scalar_tensor_tensor(out=res[:, j, :], in0=o_bank[j][0:QT, :], scalar=stat[:, j, 3:4],
                                             in1=x_tok[:, j, :], op0=ALU.mult, op1=ALU.add).then_inc(o_read, 1)
                    dve.wait_ge(o_read, b * 2 + j + 1)
                    st.step(dve.bn_stats(bn[:, j, :], res[:, j, :]))
                    own_instruction(dve, dve_waits_alone)
                    ins = dve.bn_aggr(mv[:, j, :], bn[:, j, :])
                    if j == 0:
                        st.step(ins)
                ins.then_inc(mv_ready, 1)
                dve.wait_ge(root_done, b * 2 + 2)
                if not is_int(b, 0):
                    dve.wait_ge(x1_stored, b * 16)
                for j in range(2):
                    dve.tensor_scalar(x1[:, j, :], res[:, j, :], mv[:, j, 0:1], rs[:, j, 0:1],
                                      ALU.subtract, ALU.mult).then_inc(x1_ready, 1)
                if not is_int(b, B - 1):
                    qkv_lo(b + 1)
                if not is_int(b, B - 2, B - 1):
                    split_x(b + 2)
                assert st.n == STEPS

            qkv_lo(0)
            split_x(1)
            batches(dve, body)
            next_batch(B - 1)

        @block.tensor
        def _(pe):
            def open_bank(job):
                pe.wait_ge(ring_out, job + 1)

            def ring_done(job):
                return job + RING + 1

            def qkv(b):
                pe.wait_ge(xT_lo_done, b + 1)
                for n in range(4):
                    open_bank(qkv_job(b) + n)
                    if is_int(b, 0):
                        pe.wait_ge(w_lo_done, n // 2 + 1)
                    bank = bank_of(qkv_job, b, n)
                    for f in range(2):
                        cols = slice((2 * (n % 2) + f) * 128, (2 * (n % 2) + f + 1) * 128)
                        for t in range(KD):
                            last = matmul3(pe, bank[:, f * S:(f + 1) * S], w_hi[:, n // 2, t, cols],
                                           w_lo[:, n // 2, t, cols], xT_hi[:, t, :], xT_lo[:, t, :],
                                           t == 0, t == KD - 1)
                    last.then_inc(ring_full, 1)
                for j in range(2):
                    open_bank(qkv_job(b) + 4 + j)
                    if is_int(b, 0):
                        pe.wait_ge(w_lo_done, 3)
                    for t in range(KD):
                        last = matmul3(pe, bank_of(qkv_job, b, 4 + j)[0:QT, :],
                                       xT_hi[:, t, j * QT:(j + 1) * QT], xT_lo[:, t, j * QT:(j + 1) * QT],
                                       w_hi[:, 2, t, :], w_lo[:, 2, t, :], t == 0, t == KD - 1)
                    last.then_inc(ring_full, 1)

            def transposed_and_queries(b):
                pe.wait_ge(x1_ready, b * 2 + 2)
                for n in range(2):
                    open_bank(next_job(b) + n)
                    for t in range(2):
                        for j in range(2):
                            c = (2 * n + t) * 128
                            last = pe.transpose(bank_of(next_job, b, n)[:, t * S + j * QT:t * S + (j + 1) * QT],
                                                x1[:, j, c:c + 128], ident[0:QT, 0:QT])
                    last.then_inc(ring_full, 1)
                for n in range(4):
                    open_bank(next_job(b) + 2 + n)
                    if n == 0:
                        pe.wait_ge(ring_out, ring_done(next_job(b) + 1))
                    if is_int(b, 0):
                        pe.wait_ge(w_lo_done, NW)
                    for f in range(2):
                        c = (2 * n + f) * 128
                        piece, c = 3 + c // 512, c % 512
                        for t in range(KD):
                            last = matmul3(pe, bank_of(next_job, b, 2 + n)[:, f * S:(f + 1) * S],
                                           w_hi[:, piece, t, c:c + 128], w_lo[:, piece, t, c:c + 128],
                                           x1T_hi[:, t, :], x1T_lo[:, t, :], t == 0, t == KD - 1)
                    last.then_inc(ring_full, 1)

            def body(b):
                pe.wait_ge(ring_out, ring_done(qkv_job(b) + 3))
                if not is_int(b, 0):
                    pe.wait_ge(exp_done, b * 2)
                for j in range(2):
                    for t in range(KD):
                        last = matmul3(pe, s_bank[0:QT, j * S:(j + 1) * S],
                                       qk_hi[:, 0, t, j * QT:(j + 1) * QT], qk_lo[:, 0, t, j * QT:(j + 1) * QT],
                                       qk_hi[:, 1, t, :], qk_lo[:, 1, t, :], t == 0, t == KD - 1)
                last.then_inc(scores_ready, 1)
                if not is_int(b, 0):
                    transposed_and_queries(b - 1)
                pe.wait_ge(exp_done, b * 2 + 2)
                if is_int(b, 0):
                    pe.wait_ge(ident_done, 2)
                else:
                    pe.wait_ge(pT_done, b)
                for t in range(2):
                    for j in range(2):
                        last = pe.transpose(pT_bank[0:QT, t * S + j * QT:t * S + (j + 1) * QT],
                                            probs[:, j, t * QT:(t + 1) * QT], ident[0:QT, 0:QT])
                last.then_inc(pT_full, 1)
                pe.wait_ge(ring_out, ring_done(qkv_job(b) + 5))
                pe.wait_ge(pT_done, b + 1)
                for j in range(2):
                    if not is_int(b, 0):
                        pe.wait_ge(o_read, b * 2 - 1 + j)
                    for t in range(2):
                        last = matmul3(pe, o_bank[j][0:QT, :], pT_hi[:, t, j * QT:(j + 1) * QT],
                                       pT_lo[:, t, j * QT:(j + 1) * QT], v_hi[:, t, :], v_lo[:, t, :],
                                       t == 0, t == 1)
                    last.then_inc(o_full, 1)
                if not is_int(b, B - 1):
                    qkv(b + 1)

            qkv(0)
            batches(pe, body)
            transposed_and_queries(B - 1)


def cross_attention(nc, half, ctxT, wkv, null_kv, qT_dram, oT_dram):
    SCALE = float(DH) ** -0.5
    NH = HEADS // 2
    FEAT = NH * DH
    KT = CTX_D // 128
    KEYS = CTX_LEN + 1
    KW = KEYS + 1
    HALF = KW // 2
    MT = -(-KEYS // 128)
    LAST = CTX_LEN - (MT - 1) * 128
    CHUNK = 2
    NC = KT // CHUNK
    EARLY = [("keys", 0, 0), ("keys", 0, 1), ("values", 0)]
    order = [("values", t) for t in range(1, MT)]
    for h in range(NH):
        order += [("keys", h // 2 + 1, h % 2)] if h < NH - 2 else []
        order += [("product", h - 2)] if h >= 2 else []
        order += [("keys", 0, 0)] if h == NH - 1 else []
        order += [("transposes", h - 1, n) for n in range(MT // 2)] if h >= 1 else []
    order += [("keys", 0, 1), ("product", NH - 2)] + [("transposes", NH - 1, n) for n in range(MT // 2)]
    order += [("values", 0), ("product", NH - 1)]
    JOBS = len(order)
    PLACE = {job: n for n, job in enumerate(order)}
    BEFORE = JOBS - PLACE["keys", 0, 0]
    FIRSTS = sum(job[0] != "keys" for job in order)
    FIRSTS_BEFORE = sum(job[0] != "keys" for job in order[-BEFORE:])
    with ExitStack() as stack:
        m = Scope(nc, stack, f"xa{half}", "xa")
        if half:
            m.clear(over="sa")
        ident = m.sb("ident", [128, 128])
        wk_hi, wk_lo = (m.sb(f"wk_{x}", [128, KT, FEAT], F32R) for x in ("hi", "lo"))
        wv_hi, wv_lo = (m.sb(f"wv_{x}", [128, KT, FEAT], F32R) for x in ("hi", "lo"))
        raw = m.sb("raw", [128, 3, CHUNK, CTX_LEN])
        ctx_hi, ctx_lo = (m.sb(f"ctx_{x}", [128, KT, KW], F32R) for x in ("hi", "lo"))
        stage_v = m.sb_under("stage_v", [128, 3 * CHUNK * FEAT + CHUNK * CTX_LEN])
        v = m.sb("v", [128, MT, NH, 2, DH], F32R)
        k = m.sb("k", [128, 4, KW], F32R)
        probs = m.sb("probs", [QT, 2, 2, MT * 128])
        pT_hi, pT_lo = (m.sb(f"pT_{x}", [128, MT, S], F32R) for x in ("hi", "lo"))
        stage_q = m.sb_under("stage_q", [128, CHUNK, FEAT])
        q_hi = m.sb("q_hi", [128, NH, S], F32R)
        q_raw = m.sb_under("q_raw", [128, NH, S])
        q_lo = m.sb("q_lo", [128, NH, S], F32R)
        o_part = m.sb("o_part", [DH, S])
        oT = m.sb("oT", [128, NH // 2, S])
        stat = m.sb("stat", [QT, NH, 2, 4])
        null_k = m.sb("null_k", [128, 4])
        null_v = o_part[0:1, 0:DH]
        null_row = pT_lo[0:1].rearrange("p t s -> p (t s)")[:, 0:NH * 2 * DH].rearrange("p (h i d) -> p h i d", h=NH, i=2)
        ring = [m.bank(f"ring{n}") for n in range(RING)]
        s_bank = [m.bank(f"scores{j}", (128, 2, 512)) for j in range(2)]

        ident_done = m.sem("ident_done")
        raw_loaded = [m.sem(f"raw_loaded{n}") for n in range(NC)]
        first_loaded = [m.sem(f"first_loaded{n}") for n in range(NC)]
        raw_hi, raw_lo = m.sem("raw_hi"), m.sem("raw_lo")
        pool_hi, pool_lo = m.sem("pool_hi"), m.sem("pool_lo")
        key_first = m.sem("key_first")
        null_value_placed = m.sem("null_value_placed")
        null_loaded, null_placed, null_steps = m.sem("null_loaded"), m.sem("null_placed"), m.sem("null_steps")
        q_loaded, q_hi_done, q_lo_done = m.sem("q_loaded"), m.sem("q_hi_done"), m.sem("q_lo_done")
        ring_full, ring_first, ring_out = m.sem("ring_full"), m.sem("ring_first"), m.sem("ring_out")
        scores_ready = [m.sem(f"scores_ready{j}") for j in range(2)]
        max_done = m.sem("max_done")
        max_ready, exp_done = m.sem("max_ready"), m.sem("exp_done")
        inverse_ready, probs_ready = m.sem("inverse_ready"), m.sem("probs_ready")
        sum_steps = m.sem("sum_steps")
        oT_stored = m.sem("oT_stored")
        waits_alone = m.sem("waits_alone")

        f0 = half * FEAT
        BANK = [n % RING for n in range(JOBS)]
        BANK[JOBS - 3:JOBS] = [0, 3, 1]

        def number(b, *job):
            return (b - (job in EARLY)) * JOBS + PLACE[job] + BEFORE

        def first(b, *job):
            place = PLACE[job]
            return (b - (job in EARLY)) * FIRSTS + sum(j[0] != "keys" for j in order[:place]) + FIRSTS_BEFORE + 1

        def bank(*job):
            return ring[BANK[PLACE[job]]]

        def bank_free(b, *job):
            place = PLACE[job]
            last = max(j for j in range(place - JOBS, place) if BANK[j] == BANK[place])
            return (b - (job in EARLY)) * JOBS + last + BEFORE + 1 + RING

        def done(b, *job):
            return number(b, *job) + 1 + RING

        def leave_out(eng, sem, at, n):
            eng.wait_ge(sem, at)
            eng.sem_inc(sem, n)

        WK, WV = 0, 2

        def context_round(b):
            return 1 if isinstance(b, int) and b == 0 else b + 2

        def piece(rnd, n):
            buf = raw[:, (0, 1, 2, 1)[n]]
            size = CHUNK * FEAT
            if isinstance(rnd, int) and rnd == 0:
                buf = stage_q[:] if n == 3 else \
                    stage_v[:, n * size:(n + 1) * size].rearrange("p (t f) -> p t f", t=CHUNK)
            elif isinstance(rnd, int) and rnd == 1 and n == 3:
                buf = stage_v[:, 3 * size:3 * size + CHUNK * CTX_LEN].rearrange("p (t s) -> p t s", t=CHUNK)
            part = slice(n * CHUNK, (n + 1) * CHUNK)
            if isinstance(rnd, int) and rnd in (WK, WV):
                hi, lo = (wk_hi, wk_lo) if rnd == WK else (wv_hi, wv_lo)
                return buf[:, :, 0:FEAT], hi[:, part, :], lo[:, part, :]
            return buf, ctx_hi[:, part, 0:CTX_LEN], ctx_lo[:, part, 0:CTX_LEN]

        def loaded(rnd, n):
            return (first_loaded[n], 16) if isinstance(rnd, int) and rnd == 0 else (raw_loaded[n], rnd * 16)

        def wait_split(eng, rnd, n):
            if n == 0:
                eng.wait_ge(pool_lo, rnd + 1)
            else:
                eng.wait_ge(raw_lo, rnd * (NC - 1) + n)

        block = stack.enter_context(nc.Block())

        @block.sync
        def _(sp):
            for i in range(2):
                sp.dma_start(null_k[i * DH:(i + 1) * DH, 0:1], null_kv[0, :].rearrange("(d o) -> d o", o=1))\
                    .then_inc(null_loaded, 16)
            sp.dma_start(null_v, null_kv[1:2, :]).then_inc(null_loaded, 16)

            def wait_buffer(rnd, n):
                if isinstance(rnd, int) and rnd < 2:
                    return
                if n == 3:
                    wait_split(sp, rnd, 1)
                else:
                    last = n if n != 1 or (isinstance(rnd, int) and rnd == 2) else 3
                    wait_split(sp, rnd - 1, last)

            def load_weights(rnd, cols):
                for n in range(NC):
                    wait_buffer(rnd, n)
                    sp.dma_start(piece(rnd, n)[0], wkv[n * CHUNK * 128:(n + 1) * CHUNK * 128, cols:cols + FEAT]
                                 .rearrange("(t p) n -> p t n", p=128)).then_inc(loaded(rnd, n)[0], 16)

            def load_context(b):
                for n in range(NC):
                    wait_buffer(context_round(b), n)
                    sp.dma_start(piece(context_round(b), n)[0], ctxT[bass.ds(b, 1), :, n * CHUNK:(n + 1) * CHUNK, :]
                                 .rearrange("o p t s -> p (o t) s")).then_inc(raw_loaded[n], 16)

            def load_queries(b):
                src = qT_dram[bass.ds(b, 1), f0:f0 + FEAT, :].rearrange("o (h d) s -> d (o h) s", d=DH)
                for i in range(2):
                    sp.dma_start(q_raw[i * DH:(i + 1) * DH], src).then_inc(q_loaded, 16)

            def store(b):
                sp.wait_ge(ring_out, done(b, "product", NH - 1))
                sp.dma_start(oT_dram[bass.ds(b, 1), f0:f0 + FEAT, :].rearrange("o (t p) s -> p (o t) s", p=128),
                             oT[:]).then_inc(oT_stored, 16)

            load_weights(WK, f0)
            load_context(0)
            sp.wait_ge(null_placed, 1)
            sp.dma_start(as_f32(v[LAST:LAST + 1, MT - 1].rearrange("p h i d -> p (h i d)")),
                           as_f32(null_row.rearrange("p h i d -> p (h i d)"))).then_inc(null_value_placed, 16)
            load_weights(WV, INNER + f0)
            load_queries(0)
            load_context(1)
            with sp.Fori(1, B - 1) as b:
                sp.wait_ge(scores_ready[1], b * NH)
                load_queries(b)
                store(b - 1)
                load_context(b + 1)
            sp.wait_ge(scores_ready[1], (B - 1) * NH)
            load_queries(B - 1)
            store(B - 2)
            store(B - 1)
            sp.wait_ge(oT_stored, 16 * B)

        @block.gpsimd
        def _(pool):
            make_identity(pool, ident[:], ident_done)
            pool.memset(probs[:], 0.0).then_inc(ident_done, 1)

            def split_hi(rnd):
                hi = piece(rnd, 0)[1]
                pool.wait_ge(*loaded(rnd, 0))
                own_instruction(pool, waits_alone)
                pool_round(pool, hi, piece(rnd, 0)[0]).then_inc(pool_hi, 1)

            def split_lo(rnd):
                source, hi, lo = piece(rnd, 0)
                pool.wait_ge(pool_hi, rnd + 1)
                own_instruction(pool, waits_alone)
                pool.tensor_tensor(lo, source, as_f32(hi), ALU.subtract).then_inc(pool_lo, 1)

            def queries_hi(b):
                pool.wait_ge(q_loaded, b * 32 + 32)
                own_instruction(pool, waits_alone)
                pool_round(pool, q_hi[:], q_raw[:]).then_inc(q_hi_done, 1)

            def normalise(b, h):
                for j in range(2):
                    pool.wait_ge(inverse_ready, b * 2 * NH + 2 * h + j + 1)
                    own_instruction(pool, waits_alone)
                    pool.tensor_scalar(probs[:, h % 2, j, 0:KW], probs[:, h % 2, j, 0:KW], stat[:, h, j, 3:4], 1.0,
                                       ALU.mult, ALU.mult).then_inc(probs_ready, 1)

            def body(b, more):
                for h in range(NH):
                    if more and h == NH - 3:
                        pool.wait_ge(ring_full, number(b, "keys", 3, 1) + 1)
                        split_hi(context_round(b + 1))
                    normalise(b, h)
                    if more and h == NH - 3:
                        split_lo(context_round(b + 1))
                if more:
                    queries_hi(b + 1)

            for rnd in range(3):
                split_hi(rnd)
                split_lo(rnd)
            pool.wait_ge(raw_lo, 3)
            queries_hi(0)
            with pool.Fori(0, B - 1) as b:
                body(b, True)
            body(B - 1, False)

        @block.scalar
        def _(act):
            act.sem_inc(exp_done, 2)

            def split_hi(rnd, n):
                act.wait_ge(*loaded(rnd, n))
                act.copy(piece(rnd, n)[1], piece(rnd, n)[0]).then_inc(raw_hi, 1)

            def values(b, t):
                rows = 128 if t < MT - 1 else LAST
                act.wait_ge(ring_full, number(b, "values", t) + 1)
                if t == 0 and not (isinstance(b, int) and b == 0):
                    act.wait_ge(ring_full, number(b - 1, "product", NH - 1) + 1)
                act.copy(v[0:rows, t, :, 0, :], bank("values", t)[0:rows, :].rearrange("p (h d) -> p h d", h=NH))\
                    .then_inc(ring_first, 1)

            def keys(b, pair, n):
                act.wait_ge(ring_full, number(b, "keys", pair, n) + 1)
                width = HALF if n == 0 else CTX_LEN - HALF
                for i in range(2):
                    act.copy(k[0:DH, (2 * pair + i) % 4, n * HALF:n * HALF + width],
                             bank("keys", pair, n)[i * DH:(i + 1) * DH, 0:width]).then_inc(key_first, 1)

            def transposes(b, h):
                for n in range(MT // 2):
                    act.wait_ge(ring_full, number(b, "transposes", h, n) + 1)
                    act.copy(pT_hi[:, 2 * n:2 * n + 2, :].rearrange("p t s -> p (t s)"),
                             bank("transposes", h, n)[:, 0:2 * S]).then_inc(ring_first, 1)

            def product(b, h):
                act.wait_ge(ring_full, number(b, "product", h) + 1)
                act.wait_ge(ring_out, done(b, "product", h - 1) if h else done(b - 1, "product", NH - 1))
                act.copy(o_part[:], bank("product", h)[0:DH, 0:S]).then_inc(ring_first, 1)

            def exponents(b, h):
                for j in range(2):
                    act.wait_ge(max_ready, b * 2 * NH + 2 * h + j + 1)
                    act.activation(probs[:, h % 2, j, 0:KW].rearrange("p (i s) -> p i s", i=2),
                                   s_bank[j][0:QT, :, 0:HALF], ACT.Exp, bias=stat[:, h, j, 1:2], scale=SCALE,
                                   accum_out=stat[:, h, j, 2:3]).then_inc(exp_done, 1)

            def body(b, more):
                for t in range(1, MT):
                    values(b, t)
                for h in range(NH):
                    exponents(b, h)
                    if h < NH - 2:
                        keys(b, h // 2 + 1, h % 2)
                    if h >= 2:
                        product(b, h - 2)
                    if h == NH - 1 and more:
                        split_hi(context_round(b + 1), 3)
                        keys(b + 1, 0, 0)
                    if h >= 1:
                        transposes(b, h - 1)
                    if more and h in (NH - 3, NH - 2):
                        split_hi(context_round(b + 1), h - NH + 4)
                if more:
                    keys(b + 1, 0, 1)
                product(b, NH - 2)
                transposes(b, NH - 1)
                if more:
                    values(b + 1, 0)
                else:
                    leave_out(act, ring_first, first(b + 1, "values", 0) - 1, 1)
                product(b, NH - 1)

            for rnd in range(2):
                for n in range(1, NC):
                    split_hi(rnd, n)
            act.wait_ge(ident_done, 3)
            keys(0, 0, 0)
            split_hi(WV, 1)
            split_hi(WV, 2)
            keys(0, 0, 1)
            split_hi(WV, 3)
            act.sem_inc(ring_first, FIRSTS_BEFORE - 2)
            values(0, 0)
            leave_out(act, ring_first, FIRSTS_BEFORE - 1, 1)
            with act.Fori(0, B - 1) as b:
                body(b, True)
            body(B - 1, False)

        @block.vector
        def _(dve):
            dve.sem_inc(ring_out, RING)
            st = Steps(dve, null_steps)
            dve.wait_ge(null_loaded, 48)
            st.step(dve.tensor_copy(k[0:DH, 0, KW - 1:KW], null_k[0:DH, 0:1]))
            st.step(dve.tensor_copy(k[DH:128, 1, KW - 1:KW], null_k[DH:128, 0:1]))
            st.step(dve.tensor_tensor(null_k[DH:128, 1:2], null_k[DH:128, 0:1],
                                      as_f32(k[DH:128, 1, KW - 1:KW]), ALU.subtract))
            st.step(dve.tensor_copy(null_k[0:DH, 1:2], as_f32(k[0:DH, 0, KW - 1:KW])))
            for i in range(4):
                for c in range(2):
                    st.step(dve.tensor_copy(k[:, i, CTX_LEN + c:CTX_LEN + c + 1], null_k[:, 1:2]))
            st.step(dve.tensor_copy(null_row[:, :, 0, :],
                                    null_v.rearrange("p (o d) -> p o d", o=1).broadcast_to([1, NH, DH])))
            dve.tensor_tensor(null_row[:, :, 1, :],
                              null_v.rearrange("p (o d) -> p o d", o=1).broadcast_to([1, NH, DH]),
                              as_f32(null_row[:, :, 0, :]), ALU.subtract).then_inc(null_placed, 1)
            dve.memset(as_f32(ctx_hi[:, :, CTX_LEN:KW]), 0.0).then_inc(null_placed, 1)
            dve.memset(as_f32(ctx_lo[:, :, CTX_LEN:KW]), 0.0).then_inc(null_placed, 1)

            def split_lo(rnd, n):
                source, hi, lo = piece(rnd, n)
                dve.wait_ge(raw_hi, rnd * (NC - 1) + n)
                dve.tensor_tensor(lo, source, as_f32(hi), ALU.subtract).then_inc(raw_lo, 1)

            def queries_lo(b):
                dve.wait_ge(q_hi_done, b + 1)
                dve.tensor_tensor(q_lo[:], q_raw[:], as_f32(q_hi[:]), ALU.subtract).then_inc(q_lo_done, 1)

            def values(b, t):
                rows = 128 if t < MT - 1 else LAST
                dve.wait_ge(ring_first, first(b, "values", t))
                dve.tensor_tensor(v[0:rows, t, :, 1, :], bank("values", t)[0:rows, :].rearrange("p (h d) -> p h d", h=NH),
                                  as_f32(v[0:rows, t, :, 0, :]), ALU.subtract).then_inc(ring_out, 1)

            def keys(b, pair, n):
                width = HALF if n == 0 else CTX_LEN - HALF
                for i in range(2):
                    dve.wait_ge(key_first, b * 16 + 4 * pair + 2 * n + i + 1)
                    part = (2 * pair + i) % 4, slice(n * HALF, n * HALF + width)
                    ins = dve.tensor_tensor(k[(slice(DH, 128), *part)], bank("keys", pair, n)[i * DH:(i + 1) * DH, 0:width],
                                            as_f32(k[(slice(0, DH), *part)]), ALU.subtract)
                ins.then_inc(ring_out, 1)

            def transposes(b, h):
                for n in range(MT // 2):
                    dve.wait_ge(ring_first, first(b, "transposes", h, n))
                    part = (slice(None), slice(2 * n, 2 * n + 2), slice(None))
                    dve.tensor_tensor(pT_lo[part].rearrange("p t s -> p (t s)"), bank("transposes", h, n)[:, 0:2 * S],
                                      as_f32(pT_hi[part]).rearrange("p t s -> p (t s)"), ALU.subtract)\
                       .then_inc(ring_out, 1)

            def product(b, h):
                dve.wait_ge(ring_first, first(b, "product", h))
                dve.tensor_tensor(oT[(h % 2) * DH:(h % 2 + 1) * DH, h // 2, :], bank("product", h)[DH:128, 0:S], o_part[:],
                                  ALU.add).then_inc(ring_out, 1)

            def maxima(b, h):
                for j in range(2):
                    dve.wait_ge(scores_ready[j], b * NH + h + 1)
                    dve.tensor_reduce(stat[:, h, j, 0:1], s_bank[j][0:QT, :, 0:HALF], mybir.AxisListType.XY, ALU.max)\
                       .then_inc(max_done, 1)
                    dve.wait_ge(max_done, b * 2 * NH + 2 * h + j + 1)
                    dve.tensor_scalar(stat[:, h, j, 1:2], stat[:, h, j, 0:1], -SCALE, None, ALU.mult)\
                       .then_inc(max_ready, 1)

            def inverses(b, h):
                for j in range(2):
                    dve.wait_ge(exp_done, b * 2 * NH + 2 * h + j + 3)
                    dve.tensor_tensor(stat[:, h, j, 2:3], stat[:, h, j, 2:3], probs[:, h % 2, j, KW - 1:KW],
                                      ALU.subtract).then_inc(sum_steps, 1)
                    dve.wait_ge(sum_steps, b * 2 * NH + 2 * h + j + 1)
                    dve.reciprocal(stat[:, h, j, 3:4], stat[:, h, j, 2:3]).then_inc(inverse_ready, 1)

            def body(b, more, first_batch=False):
                for t in range(1, MT):
                    values(b, t)
                for h in range(NH):
                    maxima(b, h)
                    if more and h >= NH - 2:
                        split_lo(context_round(b + 1), h - NH + 3)
                    inverses(b, h)
                    if h < NH - 2:
                        keys(b, h // 2 + 1, h % 2)
                    if h == 2 and not first_batch:
                        dve.wait_ge(oT_stored, b * 16)
                    if h >= 2:
                        product(b, h - 2)
                    if h == NH - 1:
                        if more:
                            split_lo(context_round(b + 1), 3)
                            keys(b + 1, 0, 0)
                        else:
                            leave_out(dve, ring_out, number(b + 1, "keys", 0, 0) + RING, 1)
                    if h >= 1:
                        transposes(b, h - 1)
                if more:
                    keys(b + 1, 0, 1)
                else:
                    leave_out(dve, ring_out, number(b + 1, "keys", 0, 1) + RING, 1)
                product(b, NH - 2)
                transposes(b, NH - 1)
                if more:
                    values(b + 1, 0)
                else:
                    leave_out(dve, ring_out, number(b + 1, "values", 0) + RING, 1)
                product(b, NH - 1)
                if more:
                    queries_lo(b + 1)

            for rnd in range(2):
                for n in range(1, NC):
                    split_lo(rnd, n)
            keys(0, 0, 0)
            leave_out(dve, ring_out, RING + 1, 3)
            split_lo(WV, 1)
            split_lo(WV, 2)
            keys(0, 0, 1)
            split_lo(WV, 3)
            leave_out(dve, ring_out, RING + 5, 4)
            values(0, 0)
            leave_out(dve, ring_out, RING + 10, 1)
            queries_lo(0)
            body(0, True, first_batch=True)
            with dve.Fori(1, B - 1) as b:
                body(b, True)
            body(B - 1, False)

        @block.tensor
        def _(pe):
            def open_bank(b, *job):
                pe.wait_ge(ring_out, bank_free(b, *job))

            def values(b, t):
                rows = 128 if t < MT - 1 else LAST
                open_bank(b, "values", t)
                for c in range(KT):
                    if isinstance(b, int) and b == 0 and t == 0 and c % CHUNK == 0:
                        wait_split(pe, WV, c // CHUNK)
                    last = matmul3(pe, bank("values", t)[0:rows, :], ctx_hi[:, c, t * 128:t * 128 + rows],
                                   ctx_lo[:, c, t * 128:t * 128 + rows], wv_hi[:, c, :], wv_lo[:, c, :],
                                   c == 0, c == KT - 1)
                last.then_inc(ring_full, 1)

            def keys(b, pair, n):
                open_bank(b, "keys", pair, n)
                for c in range(KT):
                    if pair == 0 and n == 0 and c % CHUNK == 0:
                        if isinstance(b, int) and b == 0:
                            wait_split(pe, WK, c // CHUNK)
                        wait_split(pe, context_round(b), c // CHUNK)
                    last = matmul3(pe, bank("keys", pair, n)[:, 0:HALF], wk_hi[:, c, pair * 128:(pair + 1) * 128],
                                   wk_lo[:, c, pair * 128:(pair + 1) * 128],
                                   ctx_hi[:, c, n * HALF:(n + 1) * HALF], ctx_lo[:, c, n * HALF:(n + 1) * HALF],
                                   c == 0, c == KT - 1)
                last.then_inc(ring_full, 1)

            def scores(b, h):
                pe.wait_ge(ring_out, done(b, "keys", h // 2, 1))
                for j in range(2):
                    pe.wait_ge(exp_done, b * 2 * NH + 2 * h + j + 1)
                    for i in range(2):
                        for n, q in enumerate((q_hi, q_lo)):
                            last = pe.matmul(s_bank[j][0:QT, i, 0:HALF], q[:, h, j * QT:(j + 1) * QT],
                                             k[:, h % 4, i * HALF:(i + 1) * HALF], start=(n == 0), stop=(n == 1))
                    last.then_inc(scores_ready[j], 1)

            def transposes(b, h):
                pe.wait_ge(probs_ready, b * 2 * NH + 2 * h + 2)
                for n in range(MT // 2):
                    open_bank(b, "transposes", h, n)
                    for t in range(2):
                        for j in range(2):
                            c = (2 * n + t) * 128
                            last = pe.transpose(bank("transposes", h, n)[:, t * S + j * QT:t * S + (j + 1) * QT],
                                                probs[:, h % 2, j, c:c + 128], ident[0:QT, 0:QT])
                    last.then_inc(ring_full, 1)

            def product(b, h):
                open_bank(b, "product", h)
                pe.wait_ge(ring_out, done(b, "transposes", h, MT // 2 - 1))
                if h == 0:
                    pe.wait_ge(ring_out, done(b, "values", MT - 1))
                for t in range(MT):
                    rows = 128 if t < MT - 1 else LAST + 1
                    for n, p in enumerate((pT_hi, pT_lo)):
                        last = pe.matmul(bank("product", h)[:, 0:S], v[0:rows, t, h].rearrange("p i d -> p (i d)"),
                                         p[0:rows, t, :], start=(t == 0 and n == 0), stop=(t == MT - 1 and n == 1))
                last.then_inc(ring_full, 1)

            def body(b, more):
                for t in range(1, MT):
                    values(b, t)
                pe.wait_ge(q_lo_done, b + 1)
                for h in range(NH):
                    scores(b, h)
                    if h < NH - 2:
                        keys(b, h // 2 + 1, h % 2)
                    if h >= 2:
                        product(b, h - 2)
                    if h == NH - 1:
                        if more:
                            keys(b + 1, 0, 0)
                        else:
                            leave_out(pe, ring_full, number(b + 1, "keys", 0, 0), 1)
                    if h >= 1:
                        transposes(b, h - 1)
                if more:
                    keys(b + 1, 0, 1)
                else:
                    leave_out(pe, ring_full, number(b + 1, "keys", 0, 1), 1)
                product(b, NH - 2)
                transposes(b, NH - 1)
                if more:
                    values(b + 1, 0)
                else:
                    leave_out(pe, ring_full, number(b + 1, "values", 0), 1)
                product(b, NH - 1)

            pe.wait_ge(null_placed, 3)
            keys(0, 0, 0)
            leave_out(pe, ring_full, 1, 3)
            keys(0, 0, 1)
            leave_out(pe, ring_full, 5, 4)
            values(0, 0)
            leave_out(pe, ring_full, 10, 1)
            pe.wait_ge(ident_done, 3)
            pe.wait_ge(null_value_placed, 16)
            with pe.Fori(0, B - 1) as b:
                body(b, True)
            body(B - 1, False)


def output_router(nc, oT_dram, wout, ln_scale, ln_bias, x1_dram, wr, br, x2_dram, logits_dram):
    FT = INNER // 128
    with ExitStack() as stack:
        m = Scope(nc, stack, "out")
        two = lambda name, shape, dt=F32: [m.sb(f"{name}{n}", shape, dt) for n in range(2)]
        ident = m.sb("ident", [128, 128])
        NW = FT // 2
        w_raw = m.sb("w_raw", [128, NW, 2, D])
        w_hi, w_lo = (m.sb(f"w_{x}", [128, FT, D], F32R) for x in ("hi", "lo"))
        o_raw = two("o_raw", [128, FT, S])
        o_hi, o_lo = two("o_hi", [128, FT, S], F32R), two("o_lo", [128, FT, S], F32R)
        scale_b, bias_b = m.sb("scale_b", [QT, D]), m.sb("bias_b", [QT, D])
        wr_sb = m.sb("wr", [128, KD, E])
        br_b = m.sb("br_b", [QT, E])
        x1 = two("x1", [QT, 2, D])
        normed = m.sb("normed", [QT, 2, D])
        res = m.sb("res", [QT, 2, D])
        x2 = m.sb("x2", [QT, 2, D])
        x2T = m.sb("x2T", [128, KD, S])
        logits = m.sb("logits", [QT, 2, E])
        bn, mv, rs = m.sb("bn", [QT, 2, 6]), m.sb("mv", [QT, 2, 2]), m.sb("rs", [QT, 2, 1])
        minus_half = m.sb("minus_half", [QT, 2, 1])
        y_bank = [[m.bank(f"y{p}{j}") for j in range(2)] for p in range(2)]
        t_bank = [m.bank(f"t{j}") for j in range(2)]
        l_bank = m.bank("l")

        ident_done, consts_loaded = m.sem("ident_done"), m.sem("consts_loaded")
        w_loaded = [m.sem(f"w_loaded{n}") for n in range(NW)]
        w_hi_done, w_lo_done = m.sem("w_hi_done"), m.sem("w_lo_done")
        o_loaded, x1_loaded = ([m.sem(f"{x}_loaded{p}") for p in range(2)] for x in ("o", "x1"))
        o_hi_done, o_lo_done = m.sem("o_hi_done"), m.sem("o_lo_done")
        y_full, y_read = m.sem("y_full"), m.sem("y_read")
        x2_ready, x2_stored = m.sem("x2_ready"), m.sem("x2_stored")
        t_full, t_read = m.sem("t_full"), m.sem("t_read")
        l_full, l_read, l_stored = m.sem("l_full"), m.sem("l_read"), m.sem("l_stored")
        biased, summed = m.sem("biased"), m.sem("summed")
        mv_ready, root_done = m.sem("mv_ready"), m.sem("root_done")
        dve_steps = m.sem("dve_steps")
        waits_alone, dve_waits_alone = m.sem("waits_alone"), m.sem("dve_waits_alone")
        STEPS = 6
        block = stack.enter_context(nc.Block())

        def batches(eng, body):
            body(0, 0)
            body(0, 1)
            with eng.Fori(1, B // 2 - 1) as u:
                body(u, 0)
                body(u, 1)
            body(B // 2 - 1, 0)
            body(B // 2 - 1, 1)

        def real(b):
            return not isinstance(b, int) or 0 <= b < B

        def known_below(b, n):
            return isinstance(b, int) and b < n

        def loads(u, p, d=0):
            return (u + (p + d) // 2 + 1) * 16

        @block.sync
        def _(sp):
            def load_w(n):
                sp.dma_start(w_raw[:, n], wout[n * 256:(n + 1) * 256, :].rearrange("(t p) n -> p t n", p=128))\
                    .then_inc(w_loaded[n], 16)

            def load_o(b, p):
                sp.dma_start(o_raw[p][:], oT_dram[bass.ds(b, 1)].rearrange("o (t p) s -> p (o t) s", p=128))\
                    .then_inc(o_loaded[p], 16)

            def load_x1(b, p):
                sp.dma_start(x1[p][:], x1_dram[bass.ds(b, 1)].rearrange("o (j p) d -> p (o j) d", p=QT))\
                    .then_inc(x1_loaded[p], 16)

            def store(b):
                sp.wait_ge(x2_ready, b * 2 + 2)
                sp.dma_start(x2_dram[bass.ds(b, 1)].rearrange("o (j p) d -> p (o j) d", p=QT), x2[:])\
                    .then_inc(x2_stored, 16)

            def store_logits(b):
                sp.wait_ge(l_read, b + 1)
                sp.dma_start(logits_dram[:, bass.ds(b * 2, 2), :], logits[:]).then_inc(l_stored, 16)

            load_w(0)
            load_o(0, 0)
            for n in range(1, NW):
                load_w(n)
            sp.dma_start(scale_b[:], ln_scale.rearrange("(o n) -> o n", o=1).broadcast_to([QT, D])).then_inc(consts_loaded, 16)
            sp.dma_start(bias_b[:], ln_bias.rearrange("(o n) -> o n", o=1).broadcast_to([QT, D])).then_inc(consts_loaded, 16)
            sp.dma_start(wr_sb[:], wr.rearrange("(t p) e -> p t e", p=128)).then_inc(consts_loaded, 16)
            sp.dma_start(br_b[:], br.rearrange("(o n) -> o n", o=1).broadcast_to([QT, E])).then_inc(consts_loaded, 16)
            load_x1(0, 0)
            load_o(1, 1)

            def body(u, p):
                b, q = 2 * u + p, 1 - p
                if real(b + 2):
                    sp.wait_ge(o_lo_done, b + 1)
                    load_o(b + 2, p)
                if real(b + 1):
                    if not known_below(b, 1):
                        sp.wait_ge(summed, b * 2)
                    load_x1(b + 1, q)
                if real(b - 1):
                    store(b - 1)
                if real(b - 2):
                    store_logits(b - 2)

            batches(sp, body)
            store_logits(B - 2)
            store(B - 1)
            store_logits(B - 1)
            sp.wait_ge(x2_stored, 16 * B)
            sp.wait_ge(l_stored, 16 * B)

        @block.gpsimd
        def _(pool):
            make_identity(pool, ident[:], ident_done)
            pool.memset(minus_half[:], -0.5).then_inc(ident_done, 1)
            pool.wait_ge(ident_done, 3)
            pool.wait_ge(consts_loaded, 64)

            def body(u, p):
                b = 2 * u + p
                pool.wait_ge(x1_loaded[p], loads(u, p))
                pool.tensor_tensor(x1[p][:], x1[p][:],
                                   bias_b[:].rearrange("p (o d) -> p o d", o=1).broadcast_to([QT, 2, D]),
                                   ALU.add).then_inc(biased, 1)
                for n, eps in enumerate((OUT_EPS, LN_EPS)):
                    pool.wait_ge(mv_ready, b * 2 + n + 1)
                    pool_inverse_root(pool, rs[:], mv[:, :, 1:2], minus_half[:], eps, root_done, b * 4 + 2 * n, waits_alone)

            batches(pool, body)

        @block.scalar
        def _(act):
            def split_w(n):
                act.wait_ge(w_loaded[n], 16)
                act.copy(w_hi[:, 2 * n:2 * n + 2, :], w_raw[:, n]).then_inc(w_hi_done, 1)

            def split(u, p, d):
                b, q = 2 * u + p + d, (p + d) % 2
                act.wait_ge(o_loaded[q], loads(u, p, d))
                if not known_below(b, 2):
                    act.wait_ge(y_full, b * 2 - 2)
                act.copy(o_hi[q][:], o_raw[q][:]).then_inc(o_hi_done, 1)

            def transposed(b):
                for n in range(2):
                    act.wait_ge(t_full, b * 2 + n + 1)
                    act.copy(x2T[:, 2 * n:2 * n + 2, :].rearrange("p t s -> p (t s)"), t_bank[n][:, 0:2 * S])\
                        .then_inc(t_read, 1)

            def body(u, p):
                b = 2 * u + p
                if real(b + 1):
                    split(u, p, 1)
                if real(b - 1):
                    transposed(b - 1)

            split_w(0)
            split(0, 0, 0)
            for n in range(1, NW):
                split_w(n)
            batches(act, body)
            transposed(B - 1)

        @block.vector
        def _(dve):
            def split_w(n):
                dve.wait_ge(w_hi_done, n + 1)
                dve.tensor_tensor(w_lo[:, 2 * n:2 * n + 2, :], w_raw[:, n], as_f32(w_hi[:, 2 * n:2 * n + 2, :]),
                                  ALU.subtract).then_inc(w_lo_done, 1)

            def split(b, p):
                dve.wait_ge(o_hi_done, b + 1)
                dve.tensor_tensor(o_lo[p][:], o_raw[p][:], as_f32(o_hi[p][:]), ALU.subtract).then_inc(o_lo_done, 1)

            def moments(st, of, done, count):
                for j in range(2):
                    dve.wait_ge(done, count + j + 1)
                    st.step(dve.bn_stats(bn[:, j, :], of(j)))
                    own_instruction(dve, dve_waits_alone)
                    ins = dve.bn_aggr(mv[:, j, :], bn[:, j, :])
                    if j == 0:
                        st.step(ins)
                ins.then_inc(mv_ready, 1)

            def add_router_bias(b):
                dve.wait_ge(l_full, b + 1)
                if not known_below(b, 1):
                    dve.wait_ge(l_stored, b * 16)
                dve.tensor_tensor(logits[:], l_bank[0:QT, 0:2 * E].rearrange("p (j e) -> p j e", j=2),
                                  br_b[:].rearrange("p (o e) -> p o e", o=1).broadcast_to([QT, 2, E]), ALU.add)\
                   .then_inc(l_read, 1)

            def body(u, p):
                b = 2 * u + p
                if real(b + 1):
                    split(b + 1, 1 - p)
                st = Steps(dve, dve_steps, b * STEPS)
                moments(st, lambda j: y_bank[p][j][0:QT, :], y_full, b * 2)
                dve.wait_ge(mv_ready, b * 2 + 1)
                for j in range(2):
                    dve.scalar_tensor_tensor(out=normed[:, j, :], in0=y_bank[p][j][0:QT, :], scalar=mv[:, j, 0:1],
                                             in1=scale_b[:], op0=ALU.subtract, op1=ALU.mult).then_inc(y_read, 1)
                if real(b - 2):
                    add_router_bias(b - 2)
                dve.wait_ge(root_done, b * 4 + 2)
                dve.wait_ge(biased, b + 1)
                for j in range(2):
                    dve.wait_ge(y_read, b * 2 + j + 1)
                    dve.scalar_tensor_tensor(out=res[:, j, :], in0=normed[:, j, :], scalar=rs[:, j, 0:1],
                                             in1=x1[p][:, j, :], op0=ALU.mult, op1=ALU.add).then_inc(summed, 1)
                moments(st, lambda j: res[:, j, :], summed, b * 2)
                dve.wait_ge(root_done, b * 4 + 4)
                if not known_below(b, 1):
                    dve.wait_ge(x2_stored, b * 16)
                    dve.wait_ge(t_full, b * 2)
                for j in range(2):
                    dve.tensor_scalar(x2[:, j, :], res[:, j, :], mv[:, j, 0:1], rs[:, j, 0:1],
                                      ALU.subtract, ALU.mult).then_inc(x2_ready, 1)
                assert st.n == STEPS

            split_w(0)
            split(0, 0)
            for n in range(1, NW):
                split_w(n)
            dve.wait_ge(consts_loaded, 64)
            batches(dve, body)
            add_router_bias(B - 2)
            add_router_bias(B - 1)

        @block.tensor
        def _(pe):
            def projection(b, p, j):
                if j == 0:
                    pe.wait_ge(o_lo_done, b + 1)
                if not known_below(b, 2):
                    pe.wait_ge(y_read, b * 2 - 3 + j)
                for t in range(FT):
                    if isinstance(b, int) and b == 0 and j == 0 and t % 2 == 0:
                        pe.wait_ge(w_lo_done, t // 2 + 1)
                    last = matmul3(pe, y_bank[p][j][0:QT, :], o_hi[p][:, t, j * QT:(j + 1) * QT],
                                   o_lo[p][:, t, j * QT:(j + 1) * QT], w_hi[:, t, :], w_lo[:, t, :],
                                   t == 0, t == FT - 1)
                last.then_inc(y_full, 1)

            def transposes(b):
                pe.wait_ge(x2_ready, b * 2 + 2)
                if not known_below(b, 1):
                    pe.wait_ge(t_read, b * 2)
                for n in range(2):
                    for t in range(2):
                        for j in range(2):
                            c = (2 * n + t) * 128
                            last = pe.transpose(t_bank[n][:, t * S + j * QT:t * S + (j + 1) * QT],
                                                x2[:, j, c:c + 128], ident[0:QT, 0:QT])
                    last.then_inc(t_full, 1)

            def router(b):
                pe.wait_ge(t_read, b * 2 + 2)
                if not known_below(b, 1):
                    pe.wait_ge(l_read, b)
                for j in range(2):
                    for t in range(KD):
                        last = pe.matmul(l_bank[0:QT, j * E:(j + 1) * E], x2T[:, t, j * QT:(j + 1) * QT],
                                         wr_sb[:, t, :], start=(t == 0), stop=(t == KD - 1))
                last.then_inc(l_full, 1)

            def body(u, p):
                b = 2 * u + p
                projection(b, p, 0)
                if real(b - 2):
                    router(b - 2)
                projection(b, p, 1)
                if real(b - 1):
                    transposes(b - 1)

            pe.wait_ge(ident_done, 2)
            pe.wait_ge(consts_loaded, 64)
            batches(pe, body)
            router(B - 2)
            transposes(B - 1)
            router(B - 1)


def routing(nc, logits_dram, x2_dram, slot_x_dram, slot_of_dram, weight_dram, expert_dram):
    N = TILES * E
    with ExitStack() as stack:
        m = Scope(nc, stack, "rt")
        lg = m.sb("lg", [QT, TILES, E])
        pr = m.sb("pr", [QT, TILES, E])
        cand = m.sb("cand", [QT, TILES, E])
        picked = [m.sb(f"picked{c}", [QT, TILES, E]) for c in range(TOP_K)]
        chosen = m.sb("chosen", [QT, TILES, E], BF16)
        red = m.sb("red", [QT, TILES, 8])
        iota_e = m.sb("iota_e", [128, E])
        iota_t = m.sb("iota_t", [128, SLOT_TILES])
        lower = m.sb("lower", [QT, 128], BF16)
        ones = m.sb("ones", [QT, 128], BF16)
        count = m.sb("count", [128, E])
        ntile, ntile_i = m.sb("ntile", [128, E]), m.sb("ntile_i", [128, E], I32)
        cum = [m.sb(f"cum{n}", [128, E]) for n in range(2)]
        first_slot = m.sb("first_slot", [128, E])
        at = m.sb("at", [QT, TILES, E])
        tmp = m.sb("tmp", [QT, TILES, E])
        slot_f = m.sb("slot_f", [QT, TOP_K, TILES])
        slot_i = m.sb("slot_i", [QT, TOP_K, TILES], I32)
        weight = m.sb("weight", [QT, TOP_K, TILES])
        cmp = m.sb("cmp", [128, SLOT_TILES, E])
        expert = m.sb("expert", [128, SLOT_TILES])
        expert_i = m.sb("expert_i", [128, SLOT_TILES], I32)
        x2 = m.sb("x2", [QT, TILES, D])
        rank_bank = m.bank("rank")

        loaded, x2_loaded, consts_done = m.sem("loaded"), m.sem("x2_loaded"), m.sem("consts_done")
        shifted, exp_done = m.sem("shifted"), m.sem("exp_done")
        chosen_ready, rank_ready = m.sem("chosen_ready"), m.sem("rank_ready")
        slots_ready, weights_ready, experts_ready = m.sem("slots_ready"), m.sem("weights_ready"), m.sem("experts_ready")
        stored, scattered = m.sem("stored"), m.sem("scattered")
        steps = m.sem("steps")
        block = stack.enter_context(nc.Block())

        @block.sync
        def _(sp):
            sp.dma_start(lg[:], logits_dram).then_inc(loaded, 16)
            sp.dma_start(x2[:], x2_dram.rearrange("b (j p) d -> p (b j) d", p=QT)).then_inc(x2_loaded, 16)
            sp.wait_ge(slots_ready, 1)
            sp.dma_start(slot_of_dram, slot_i[:]).then_inc(stored, 16)
            sp.wait_ge(weights_ready, 1)
            sp.dma_start(weight_dram, weight[:]).then_inc(stored, 16)
            sp.wait_ge(experts_ready, 1)
            sp.dma_start(expert_dram, expert_i[:]).then_inc(stored, 16)
            sp.wait_ge(stored, 48)

        @block.gpsimd
        def _(pool):
            pool.iota(iota_e[:], pattern=[[1, E]], base=0, channel_multiplier=0,
                      allow_small_or_imprecise_dtypes=True).then_inc(consts_done, 1)
            pool.iota(iota_t[:], pattern=[[1, SLOT_TILES]], base=0, channel_multiplier=0,
                      allow_small_or_imprecise_dtypes=True).then_inc(consts_done, 1)
            pool.memset(ones[:], 1.0).then_inc(consts_done, 1)
            pool.memset(lower[:], 1.0).then_inc(consts_done, 1)
            pool.wait_ge(consts_done, 4)
            pool.affine_select(out=lower[:], in_=lower[:], compare_op=ALU.is_gt, fill=0.0, base=0,
                               pattern=[[1, 128]], channel_multiplier=-1).then_inc(consts_done, 1)
            pool.wait_ge(slots_ready, 1)
            pool.wait_ge(x2_loaded, 16)
            for c in range(TOP_K):
                for t in range(TILES):
                    pool.indirect_dma_start(slot_x_dram, bass.IndirectOffsetOnAxis(ap=slot_i[:, c, t:t + 1].bitcast(U32), axis=0),
                                            x2[:, t, :], None).then_inc(scattered, 16)
            pool.wait_ge(scattered, 16 * TOP_K * TILES)

        @block.scalar
        def _(act):
            act.wait_ge(shifted, 1)
            act.activation(pr[:], lg[:], ACT.Exp).then_inc(exp_done, 1)

        @block.tensor
        def _(pe):
            pe.wait_ge(consts_done, 5)
            pe.wait_ge(chosen_ready, 1)
            rank = rank_bank[:, 0:(TILES + 1) * E].rearrange("p (t e) -> p t e", e=E)
            pe.matmul(rank_bank[:, 0:N], lower[:], chosen[:].rearrange("p t e -> p (t e)"), start=True, stop=False,
                      skip_group_check=True)
            for t in range(TILES):
                later = TILES - t
                last = pe.matmul(rank[:, t + 1:TILES + 1, :], ones[:],
                                 chosen[:, t:t + 1, :].broadcast_to([QT, later, E]), start=False,
                                 stop=(t == TILES - 1), skip_group_check=True)
            last.then_inc(rank_ready, 1)

        @block.vector
        def _(dve):
            st = Steps(dve, steps)
            per_e = lambda ap: ap.rearrange("p (o e) -> p o e", o=1).broadcast_to([QT, TILES, E])
            per_t = lambda ap: ap.broadcast_to([QT, TILES, E])
            dve.wait_ge(loaded, 16)
            dve.wait_ge(consts_done, 5)
            st.step(dve.tensor_reduce(red[:, :, 0], lg[:], AX, ALU.max))
            dve.tensor_tensor(lg[:], lg[:], per_t(red[:, :, 0:1]), ALU.subtract).then_inc(shifted, 1)
            dve.wait_ge(exp_done, 1)
            st.step(dve.tensor_reduce(red[:, :, 1], pr[:], AX, ALU.add))
            st.step(dve.reciprocal(red[:, :, 2], red[:, :, 1]))
            st.step(dve.tensor_tensor(pr[:], pr[:], per_t(red[:, :, 2:3]), ALU.mult))
            for c in range(TOP_K):
                st.step(dve.tensor_reduce(red[:, :, 3 + c], pr[:], AX, ALU.max))
                st.step(dve.tensor_tensor(cand[:], pr[:], per_t(red[:, :, 3 + c:4 + c]), ALU.is_equal))
                st.step(dve.scalar_tensor_tensor(out=cand[:], in0=cand[:], scalar=-float(E), in1=per_e(iota_e[0:QT]),
                                                 op0=ALU.mult, op1=ALU.add))
                st.step(dve.tensor_reduce(red[:, :, 5], cand[:], AX, ALU.min))
                st.step(dve.tensor_tensor(picked[c][:], cand[:], per_t(red[:, :, 5:6]), ALU.is_equal))
                if c == 0:
                    st.step(dve.scalar_tensor_tensor(out=pr[:], in0=picked[0][:], scalar=-2.0, in1=pr[:],
                                                     op0=ALU.mult, op1=ALU.add))
            dve.tensor_tensor(chosen[:], picked[0][:], picked[1][:], ALU.add).then_inc(chosen_ready, 1)
            st.step(dve.tensor_tensor(red[:, :, 6], red[:, :, 3], red[:, :, 4], ALU.add))
            st.step(dve.tensor_scalar(red[:, :, 6], red[:, :, 6], 1e-9, None, ALU.max))
            st.step(dve.reciprocal(red[:, :, 7], red[:, :, 6]))
            for c in range(TOP_K):
                ins = dve.tensor_tensor(weight[:, c, :], red[:, :, 3 + c], red[:, :, 7], ALU.mult)
                if c == 0:
                    st.step(ins)
            ins.then_inc(weights_ready, 1)
            dve.wait_ge(rank_ready, 1)
            st.step(dve.tensor_copy(count[:], rank_bank[:, N:N + E]))
            st.step(dve.tensor_scalar(count[:], count[:], 1.0 / SLOT, (SLOT - 1) / SLOT - (SLOT - 1) / (2 * SLOT),
                                      ALU.mult, ALU.add))
            st.step(dve.tensor_copy(ntile_i[:], count[:]))
            st.step(dve.tensor_copy(ntile[:], ntile_i[:]))
            st.step(dve.tensor_copy(cum[0][:], ntile[:]))
            for n, d in enumerate((1, 2, 4, 8)):
                a, z = cum[n % 2], cum[(n + 1) % 2]
                st.step(dve.tensor_copy(z[:, 0:d], a[:, 0:d]))
                st.step(dve.tensor_tensor(z[:, d:E], a[:, d:E], a[:, 0:E - d], ALU.add))
            total = cum[0]
            st.step(dve.tensor_tensor(first_slot[:], total[:], ntile[:], ALU.subtract))
            st.step(dve.tensor_scalar(first_slot[:], first_slot[:], float(SLOT), None, ALU.mult))
            st.step(dve.tensor_tensor(at[:], rank_bank[0:QT, 0:N].rearrange("p (t e) -> p t e", e=E),
                                      per_e(first_slot[0:QT]), ALU.add))
            for c in range(TOP_K):
                st.step(dve.tensor_tensor(tmp[:], at[:], picked[c][:], ALU.mult))
                st.step(dve.tensor_reduce(slot_f[:, c, :], tmp[:], AX, ALU.add))
            dve.tensor_copy(slot_i[:], slot_f[:]).then_inc(slots_ready, 1)
            st.step(dve.tensor_tensor(cmp[:], iota_t[:].rearrange("p (t o) -> p t o", o=1).broadcast_to([128, SLOT_TILES, E]),
                                      total[:].rearrange("p (o e) -> p o e", o=1).broadcast_to([128, SLOT_TILES, E]),
                                      ALU.is_ge))
            st.step(dve.tensor_reduce(expert[:], cmp[:], AX, ALU.add))
            st.step(dve.tensor_scalar(expert[:], expert[:], float(E - 1), None, ALU.min))
            dve.tensor_copy(expert_i[:], expert[:]).then_inc(experts_ready, 1)


def experts(nc, slot_x_dram, expert_dram, w1, b1, ffn_gb, w2, b2, slot_y_dram):
    N = SLOT_TILES
    W2_POOL = 2
    with ExitStack() as stack:
        m = Scope(nc, stack, "ex")
        ident = m.sb("ident", [128, 128])
        two = lambda name, shape, dt=F32: [m.sb(f"{name}{n}", shape, dt) for n in range(2)]
        w1_raw, w1_hi, w1_lo = two("w1_raw", [128, KD, HID]), two("w1_hi", [128, KD, HID], F32R), two("w1_lo", [128, KD, HID], F32R)
        w2_raw, w2_hi, w2_lo = two("w2_raw", [128, KD, D]), two("w2_hi", [128, KD, D], F32R), two("w2_lo", [128, KD, D], F32R)
        gb = two("gb", [128, 2, KD])
        x = two("x", [128, D])
        xT_hi, xT_lo = two("xT_hi", [128, KD, SLOT], F32R), two("xT_lo", [128, KD, SLOT], F32R)
        normed = two("normed", [128, HID])
        g = two("g", [128, KD, SLOT])
        g_hi, g_lo = two("g_hi", [128, KD, SLOT], F32R), two("g_lo", [128, KD, SLOT], F32R)
        y = two("y", [128, D])
        bias_raw = m.sb("bias_raw", [64, 2, D])
        bias = m.sb("bias", [128, 2, D], F32R)
        row_expert = m.sb("row_expert", [128, SLOT])
        pick1, pick2 = two("pick1", [128, SLOT], F32R), two("pick2", [128, SLOT], F32R)
        expert_i = m.sb("expert_i", [128, N], I32)
        expert_f = m.sb("expert_f", [128, N])
        changed = m.sb("changed", [128, N], I32)
        minus_half = m.sb("minus_half", [128, 1])
        bn, mv, rs = m.sb("bn", [128, 6]), m.sb("mv", [128, 2]), two("rs", [128, 2])
        x_bank, g_bank = m.bank("xT"), m.bank("gT")
        h_bank = [m.bank(f"h{n}") for n in range(2)]
        y_bank = [m.bank(f"y_bank{n}") for n in range(2)]

        def sems(name):
            return [m.sem(f"{name}{n}") for n in range(2)]

        expert_loaded = m.sem("expert_loaded")
        ident_done, setup_loaded, setup = m.sem("ident_done"), m.sem("setup_loaded"), m.sem("setup")
        setup_pool, zeroed = m.sem("setup_pool"), m.sem("zeroed")
        w1_loaded, w2_loaded, gb_loaded, x_loaded = sems("w1_loaded"), sems("w2_loaded"), sems("gb_loaded"), sems("x_loaded")
        w1_hi_done, w1_done = m.sem("w1_hi_done"), m.sem("w1_done")
        w2_hi_done, w2_done, w2_pool_done = m.sem("w2_hi_done"), m.sem("w2_done"), m.sem("w2_pool_done")
        xT_full, xT_hi_done, xT_done = m.sem("xT_full"), m.sem("xT_hi_done"), m.sem("xT_done")
        h_full, norm_ready, normed_ready = m.sem("h_full"), m.sem("norm_ready"), m.sem("normed_ready")
        g_full, gelu_done, g_hi_done, g_done = m.sem("g_full"), m.sem("gelu_done"), m.sem("g_hi_done"), m.sem("g_done")
        pick1_done, pick2_done = m.sem("pick1_done"), m.sem("pick2_done")
        y_full, y_ready, y_stored = m.sem("y_full"), m.sem("y_ready"), sems("y_stored")
        dve_steps, dve_waits_alone, waits_alone = m.sem("dve_steps"), m.sem("dve_waits_alone"), m.sem("waits_alone")
        mv_ready, root_done = m.sem("mv_ready"), m.sem("root_done")
        block = stack.enter_context(nc.Block())

        def steps(eng, body, ahead=0, behind=0):
            low, high = 6, (N - ahead) // 2 * 2
            for i in range(-ahead, low):
                body(i // 2, i % 2)
            with eng.Fori(low // 2, high // 2) as u:
                body(u, 0)
                body(u, 1)
            for i in range(high, N + behind):
                body(i // 2, i % 2)

        def tile(u, p, d=0):
            return u + (p + d) // 2 + (N + 1) // 2 * ((p + d) % 2)

        def loads(u, p, d=0):
            return (u + (p + d) // 2 + 1) * 16

        def real(i):
            return not isinstance(i, int) or 0 <= i < N

        def known_below(i, n):
            return isinstance(i, int) and i < n

        SETUP = 7

        @block.sync
        def _(sp):
            sp.dma_start(expert_i[:], expert_dram).then_inc(expert_loaded, 16)

            def load_x(u, p, d):
                i, q = 2 * u + p + d, (p + d) % 2
                if not known_below(i, 2):
                    sp.wait_ge(xT_full, i - 1)
                sp.dma_start(x[q][:], slot_x_dram[bass.ds(tile(u, p, d) * SLOT, SLOT), :]).then_inc(x_loaded[q], 16)

            def load_weight(u, p, d, e, w, raw, split, loaded):
                i, q = 2 * u + p + d, (p + d) % 2
                new = dict()
                if not known_below(i, 2):
                    if isinstance(i, int) and i == 2:
                        sp.wait_ge(setup, SETUP)
                    new = dict(cond=sp.value_load(changed[0:1, bass.ds(tile(u, p, d), 1)], min_val=0, max_val=1))
                    for sem in split:
                        sp.wait_ge(sem, i - 1)
                sp.dma_start(raw[q][:], w[bass.ds(e, 1)].rearrange("o (t p) n -> p (o t) n", p=128), **new)\
                    .then_inc(loaded[q], 16)

            def expert_of(u, p, d=0):
                return sp.value_load(expert_i[0:1, bass.ds(tile(u, p, d), 1)], min_val=0, max_val=E - 1)

            def body(u, p):
                i, q = 2 * u + p, 1 - p
                if real(i + 1):
                    load_x(u, p, 1)
                if real(i):
                    if isinstance(i, int) and i == 0:
                        sp.wait_ge(expert_loaded, 16)
                    load_weight(u, p, 0, expert_of(u, p), w1, w1_raw, [w1_done], w1_loaded)
                if real(i - 1):
                    e = expert_of(u, p, -1)
                    if not known_below(i, 3):
                        sp.wait_ge(gelu_done, i - 2)
                    sp.dma_start(gb[q][:], ffn_gb[bass.ds(e, 1)].rearrange("o p i t -> p (o i) t")).then_inc(gb_loaded[q], 16)
                    load_weight(u, p, -1, e, w2, w2_raw, [w2_done, w2_pool_done], w2_loaded)

            steps(sp, body, 1, 1)
            for p in range(2):
                sp.wait_ge(y_stored[p], 16 * ((N + 1 - p) // 2))

        @block.gpsimd
        def _(pool):
            pool.memset(bias_raw[:], 0.0).then_inc(zeroed, 1)
            make_identity(pool, ident[:], ident_done)
            pool.iota(row_expert[:], pattern=[[0, SLOT]], base=0, channel_multiplier=1,
                      allow_small_or_imprecise_dtypes=True).then_inc(setup_pool, 1)

            pool.memset(minus_half[:], -0.5).then_inc(ident_done, 1)
            pool.wait_ge(ident_done, 3)

            def body(u, p):
                i, q = 2 * u + p, 1 - p
                j = i - 1
                if real(j):
                    pool.wait_ge(w2_loaded[q], loads(u, p, -1))
                    if not known_below(j, 2):
                        pool.wait_ge(y_full, j - 1)
                    own_instruction(pool, waits_alone)
                    pool_round(pool, w2_hi[q][:], w2_raw[q][:]).then_inc(w2_hi_done, 1)
                    pool.wait_ge(w2_hi_done, j + 1)
                    own_instruction(pool, waits_alone)
                    pool.tensor_tensor(w2_lo[q][:, 0:W2_POOL], w2_raw[q][:, 0:W2_POOL], as_f32(w2_hi[q][:, 0:W2_POOL]),
                                       ALU.subtract).then_inc(w2_pool_done, 1)
                if real(i):
                    pool.wait_ge(mv_ready, i + 1)
                    pool_inverse_root(pool, rs[p][:, 0:1], mv[:, 1:2], minus_half[:], LN_EPS, root_done, i * 2, waits_alone)
                    pool.wait_ge(root_done, i * 2 + 2)
                    own_instruction(pool, waits_alone)
                    pool.tensor_scalar(rs[p][:, 1:2], mv[:, 0:1], rs[p][:, 0:1], -1.0, ALU.mult, ALU.mult)\
                        .then_inc(norm_ready, 1)
                if real(j):
                    pool.wait_ge(gelu_done, j + 1)
                    own_instruction(pool, waits_alone)
                    pool_round(pool, g_hi[q][:], g[q][:]).then_inc(g_hi_done, 1)

            steps(pool, body, 0, 1)

        @block.scalar
        def _(act):
            act.wait_ge(zeroed, 1)
            for n, b in enumerate((b1, b2)):
                for r in range(2):
                    act.dma_start(bias_raw[32 * r:32 * r + E, n, :], b).then_inc(setup_loaded, 16)

            def body(u, p):
                i, q = 2 * u + p, 1 - p
                j = i - 1
                if real(j):
                    act.wait_ge(norm_ready, j + 1)
                    act.activation(normed[q][:], h_bank[q][:, :], ACT.Identity, bias=rs[q][:, 1:2], scale=rs[q][:, 0:1])\
                        .then_inc(normed_ready, 1)
                if real(i - 3):
                    act.wait_ge(y_full, i - 2)
                    if not known_below(i, 5):
                        act.wait_ge(y_stored[q], loads(u, p, -5))
                    act.copy(y[q][:], y_bank[q][:, :]).then_inc(y_ready, 1)
                    act.wait_ge(y_ready, i - 2)
                    act.dma_start(slot_y_dram[bass.ds(tile(u, p, -3) * SLOT, SLOT), :], y[q][:]).then_inc(y_stored[q], 16)
                if real(i + 1):
                    act.wait_ge(xT_full, i + 2)
                    act.copy(xT_hi[q][:].rearrange("p t s -> p (t s)"), x_bank[:, :]).then_inc(xT_hi_done, 1)
                    act.wait_ge(w1_loaded[q], loads(u, p, 1))
                    if not known_below(i, 1):
                        act.wait_ge(h_full, i)
                    act.copy(w1_hi[q][:], w1_raw[q][:]).then_inc(w1_hi_done, 1)
                if real(j):
                    act.wait_ge(g_full, j + 1)
                    act.wait_ge(gb_loaded[q], loads(u, p, -1))
                    for t in range(KD):
                        last = act.activation(g[q][:, t, :], g_bank[:, t * SLOT:(t + 1) * SLOT], ACT.Gelu,
                                              bias=gb[q][:, 1, t:t + 1], scale=gb[q][:, 0, t:t + 1])
                    last.then_inc(gelu_done, 1)

            steps(act, body, 1, 3)

        @block.vector
        def _(dve):
            st = Steps(dve, setup)
            dve.wait_ge(setup_pool, 1)
            st.step(dve.tensor_scalar(row_expert[32:64], row_expert[32:64], -32.0, None, ALU.add))
            st.step(dve.memset(row_expert[64:128], -1.0))
            dve.wait_ge(expert_loaded, 16)
            st.step(dve.tensor_copy(expert_f[:], expert_i[:]))
            st.step(dve.tensor_tensor(changed[:, 1:], expert_f[:, 1:], expert_f[:, 0:N - 1], ALU.not_equal))
            dve.wait_ge(setup_loaded, 64)
            st.step(dve.memset(as_f32(bias[64:128]), 0.0))
            st.step(dve.tensor_copy(bias[0:64], bias_raw[:]))
            st.step(dve.tensor_tensor(bias[32:64], bias_raw[32:64], as_f32(bias[32:64]), ALU.subtract))
            assert st.n == SETUP

            def pick(at, out, done):
                dve.tensor_scalar(out, row_expert[:], expert_f[:, bass.ds(at, 1)], None, ALU.is_equal).then_inc(done, 1)

            def body(u, p):
                i, q = 2 * u + p, 1 - p
                j = i - 1
                if real(i + 1):
                    if not known_below(i, 1):
                        dve.wait_ge(h_full, i)
                    pick(tile(u, p, 1), pick1[q][:], pick1_done)
                    dve.wait_ge(xT_hi_done, i + 2)
                    dve.tensor_tensor(xT_lo[q][:].rearrange("p t s -> p (t s)"), x_bank[:, :],
                                      as_f32(xT_hi[q][:]).rearrange("p t s -> p (t s)"), ALU.subtract).then_inc(xT_done, 1)
                if real(j):
                    dve.wait_ge(w2_hi_done, j + 1)
                    dve.tensor_tensor(w2_lo[q][:, W2_POOL:], w2_raw[q][:, W2_POOL:], as_f32(w2_hi[q][:, W2_POOL:]),
                                      ALU.subtract).then_inc(w2_done, 1)
                    pick(tile(u, p, -1), pick2[q][:], pick2_done)
                if real(i):
                    dve.wait_ge(h_full, i + 1)
                    dve.bn_stats(bn[:], h_bank[p][:, :]).then_inc(dve_steps, 1)
                    dve.wait_ge(dve_steps, i + 1)
                    if not known_below(i, 1):
                        dve.wait_ge(norm_ready, i)
                    own_instruction(dve, dve_waits_alone)
                    dve.bn_aggr(mv[:], bn[:]).then_inc(mv_ready, 1)
                if real(i + 1):
                    dve.wait_ge(w1_hi_done, i + 2)
                    dve.tensor_tensor(w1_lo[q][:], w1_raw[q][:], as_f32(w1_hi[q][:]), ALU.subtract).then_inc(w1_done, 1)
                if real(j):
                    dve.wait_ge(g_hi_done, j + 1)
                    dve.tensor_tensor(g_lo[q][:], g[q][:], as_f32(g_hi[q][:]), ALU.subtract).then_inc(g_done, 1)

            steps(dve, body, 1, 1)

        @block.tensor
        def _(pe):
            pe.wait_ge(ident_done, 2)

            def layer(bank, pick, n, a_hi, a_lo, w_hi, w_lo):
                pe.matmul(bank[:, :], pick[:], bias[:, n, :], start=True, stop=False)
                for t in range(KD):
                    last = matmul3(pe, bank[:, :], a_hi[:, t, :], a_lo[:, t, :], w_hi[:, t, :], w_lo[:, t, :],
                                   False, t == KD - 1)
                return last

            def body(u, p):
                i, q = 2 * u + p, 1 - p
                j = i - 1
                if real(i + 1):
                    pe.wait_ge(x_loaded[q], loads(u, p, 1))
                    if not known_below(i, 0):
                        pe.wait_ge(xT_done, i + 1)
                    for t in range(KD):
                        last = pe.transpose(x_bank[:, t * SLOT:(t + 1) * SLOT], x[q][:, t * 128:(t + 1) * 128], ident[:])
                    last.then_inc(xT_full, 1)
                if real(i):
                    pe.wait_ge(xT_done, i + 1)
                    pe.wait_ge(w1_done, i + 1)
                    if isinstance(i, int) and i == 0:
                        pe.wait_ge(setup, SETUP)
                    pe.wait_ge(pick1_done, i + 1)
                    if not known_below(i, 2):
                        pe.wait_ge(normed_ready, i - 1)
                    layer(h_bank[p], pick1[p], 0, xT_hi[p], xT_lo[p], w1_hi[p], w1_lo[p]).then_inc(h_full, 1)
                if real(j):
                    pe.wait_ge(normed_ready, j + 1)
                    if not known_below(j, 1):
                        pe.wait_ge(gelu_done, j)
                    for t in range(KD):
                        last = pe.transpose(g_bank[:, t * SLOT:(t + 1) * SLOT], normed[q][:, t * 128:(t + 1) * 128], ident[:])
                    last.then_inc(g_full, 1)
                if real(i - 2):
                    pe.wait_ge(g_done, i - 1)
                    pe.wait_ge(w2_done, i - 1)
                    pe.wait_ge(w2_pool_done, i - 1)
                    pe.wait_ge(pick2_done, i - 1)
                    if not known_below(i, 4):
                        pe.wait_ge(y_ready, i - 3)
                    layer(y_bank[p], pick2[p], 1, g_hi[p], g_lo[p], w2_hi[p], w2_lo[p]).then_inc(y_full, 1)

            steps(pe, body, 1, 2)


def combine(nc, slot_y_dram, slot_of_dram, weight_dram, x2_dram, out):
    HALF = TILES // 2
    with ExitStack() as stack:
        m = Scope(nc, stack, "cb")
        slot_i = m.sb("slot_i", [QT, TOP_K, TILES], I32)
        weight = m.sb("weight", [QT, TOP_K, TILES])
        x2 = m.sb("x2", [QT, TILES, D])
        y = m.sb("y", [QT, TOP_K, TILES, D])
        res = m.sb("res", [QT, TILES, D])
        bn, mv = m.sb("bn", [QT, TILES, 6]), m.sb("mv", [QT, TILES, 2])
        rs = m.sb("rs", [QT, 3, TILES])
        x2_loaded = [m.sem(f"x2_loaded{n}") for n in range(B // 2)]
        weight_loaded, slot_loaded = m.sem("weight_loaded"), m.sem("slot_loaded")
        gathered = [m.sem(f"gathered{n}") for n in range(TILES // 2)]
        steps, roots_done, ready, stored = m.sem("steps"), m.sem("roots_done"), m.sem("ready"), m.sem("stored")
        act_ready = m.sem("act_ready")
        block = stack.enter_context(nc.Block())

        @block.gpsimd
        def _(pool):
            pool.wait_ge(slot_loaded, 16)
            for t in range(TILES):
                for c in range(TOP_K):
                    pool.indirect_dma_start(y[:, c, t, :], None, slot_y_dram,
                                            bass.IndirectOffsetOnAxis(ap=slot_i[:, c, t:t + 1].bitcast(U32), axis=0))\
                        .then_inc(gathered[t // 2], 16)

        @block.sync
        def _(sp):
            sp.dma_start(slot_i[:], slot_of_dram).then_inc(slot_loaded, 16)
            sp.dma_start(weight[:], weight_dram).then_inc(weight_loaded, 16)
            for n in range(B // 2):
                sp.dma_start(x2[:, 4 * n:4 * n + 4, :], x2_dram[2 * n:2 * n + 2].rearrange("b (j p) d -> p (b j) d", p=QT))\
                    .then_inc(x2_loaded[n], 16)
            for b in range(B):
                sp.wait_ge(act_ready, b + 1)
                sp.wait_ge(ready, b + 1)
                sp.dma_start(out[b].rearrange("(j p) d -> p j d", p=QT), res[:, 2 * b:2 * b + 2, :]).then_inc(stored, 16)
            sp.wait_ge(stored, 16 * B)

        @block.scalar
        def _(act):
            for h in range(2):
                act.wait_ge(roots_done, h + 1)
                for t in range(h * HALF, (h + 1) * HALF, 2):
                    act.activation(res[:, t, :], res[:, t, :], ACT.Identity, bias=rs[:, 2, t:t + 1],
                                   scale=rs[:, 0, t:t + 1]).then_inc(act_ready, 1)

        @block.vector
        def _(dve):
            dve.wait_ge(weight_loaded, 16)
            st = Steps(dve, steps)
            for h in range(2):
                for t0 in range(h * HALF, (h + 1) * HALF, 2):
                    pair = (t0, t0 + 1)
                    if t0 % 4 == 0:
                        dve.wait_ge(x2_loaded[t0 // 4], 16)
                    first = st.n
                    for stage in range(4):
                        for t in pair:
                            if stage == 0:
                                dve.wait_ge(gathered[t // 2], 2 * 16 * TOP_K)
                            else:
                                dve.wait_ge(steps, first + 2 * stage - 1 + t - t0)
                            if stage < 2:
                                ins = dve.scalar_tensor_tensor(
                                    out=res[:, t, :], in0=y[:, stage, t, :], scalar=weight[:, stage, t:t + 1],
                                    in1=x2[:, t, :] if stage == 0 else res[:, t, :], op0=ALU.mult, op1=ALU.add)
                            elif stage == 2:
                                ins = dve.bn_stats(bn[:, t, :], res[:, t, :])
                            else:
                                ins = dve.bn_aggr(mv[:, t, :], bn[:, t, :])
                            ins.then_inc(steps, 1)
                    st.n = first + 8
                dve.wait_ge(steps, st.n)
                part = slice(h * HALF, (h + 1) * HALF)
                rsqrt_steps(st, rs[:, 0, part], mv[:, part, 1], rs[:, 1, part], LN_EPS)
                st.step(dve.tensor_tensor(rs[:, 2, part], mv[:, part, 0], rs[:, 0, part], ALU.mult))
                dve.tensor_scalar(rs[:, 2, part], rs[:, 2, part], -1.0, None, ALU.mult).then_inc(roots_done, 1)
                for t in range(h * HALF + 1, (h + 1) * HALF, 2):
                    dve.tensor_scalar(res[:, t, :], res[:, t, :], mv[:, t, 0:1], rs[:, 0, t:t + 1],
                                      ALU.subtract, ALU.mult).then_inc(ready, 1)


def decoder_layer(nc, a, out):
    def scratch(name, shape, dt=F32):
        return nc.dram_tensor(name, shape, dt).ap()

    x1 = scratch("x1_scratch", (B, S, D))
    qT = scratch("qT_scratch", (B, INNER, S))
    oT = scratch("oT_scratch", (B, INNER, S))
    x2 = scratch("x2_scratch", (B, S, D))
    logits = scratch("logits_scratch", (QT, TILES, E))
    slot_of = scratch("slot_of_scratch", (QT, TOP_K, TILES), I32)
    weight = scratch("weight_scratch", (QT, TOP_K, TILES))
    expert = scratch("expert_scratch", (128, SLOT_TILES), I32)
    slot_x = scratch("slot_x_scratch", (SLOTS, D))
    slot_y = scratch("slot_y_scratch", (SLOTS, D))
    Scope.made, Scope.free = {}, []
    with ExitStack() as Scope.kept:
        blocks(nc, a, out, x1, qT, oT, x2, logits, slot_of, weight, expert, slot_x, slot_y)


def blocks(nc, a, out, x1, qT, oT, x2, logits, slot_of, weight, expert, slot_x, slot_y):
    self_attention(nc, a["xT"], a["x"], a["L0_attn_W_Q"], a["L0_attn_W_K"], a["L0_attn_W_V"], a["L0_xattn_Wq"],
                   x1, qT, slot_x)
    for half in range(2):
        cross_attention(nc, half, a["ctxT"], a["L0_xattn_Wkv"], a["L0_xattn_null_kv"], qT, oT)
    output_router(nc, oT, a["L0_xattn_Wout"], a["L0_xattn_ln_scale"], a["L0_xattn_ln_bias"], x1,
                  a["L0_ffn_Wr"], a["L0_ffn_br"], x2, logits)
    routing(nc, logits, x2, slot_x, slot_of, weight, expert)
    experts(nc, slot_x, expert, a["L0_ffn_W1"], a["L0_ffn_b1"], a["ffn_gb"], a["L0_ffn_W2"], a["L0_ffn_b2"], slot_y)
    combine(nc, slot_y, slot_of, weight, x2, out)


def kernel(**inputs):
    import numpy as _np
    import concourse.bacc as _bacc
    from concourse import mybir as _mybir
    from concourse.bass_utils import run_bass_kernel_spmd as _run

    a = {k: _np.ascontiguousarray(v) for k, v in inputs.items()}

    def features_first(t):
        b, s, d = t.shape
        return _np.ascontiguousarray(t.reshape(b, s, d // 128, 128).transpose(0, 3, 2, 1))

    a["xT"] = features_first(a["x"])
    a["ctxT"] = features_first(a.pop("ctx_2048"))
    gb = _np.stack([a.pop("L0_ffn_g1"), a.pop("L0_ffn_be1")], axis=1)
    a["ffn_gb"] = _np.ascontiguousarray(gb.reshape(E, 2, HID // 128, 128).transpose(0, 3, 1, 2))

    nc = _bacc.Bacc("TRN2", target_bir_lowering=False, num_devices=1)
    arrays = {f"in_{k}_dram": v for k, v in a.items()}
    aps = {k: nc.dram_tensor(f"in_{k}_dram", v.shape, _mybir.dt.from_np(v.dtype), kind="ExternalInput").ap()
           for k, v in a.items()}
    out = nc.dram_tensor("out_0_dram", (B, S, D), F32, kind="ExternalOutput").ap()
    decoder_layer(nc, aps, out)
    r = _run(nc, [arrays], core_ids=[0])
    return r.results[0]["out_0_dram"]
```
